# Optimizing a Trainium2 kernel written in Bass

```python
import numpy as np
import jax
import jax.numpy as jnp

def _softmax(x, axis=-1):
    return jax.nn.softmax(x, axis=axis)

def _gelu(x):
    return jax.nn.gelu(x, approximate=True)

def _silu(x):
    return jax.nn.silu(x)

def _sigmoid(x):
    return jax.nn.sigmoid(x)

def _layernorm(x, axis=-1, eps=1e-05):
    m = jnp.mean(x, axis=axis, keepdims=True)
    v = jnp.var(x, axis=axis, keepdims=True)
    return (x - m) / jnp.sqrt(v + eps)

def _scatter_add(tgt, idx, src, axis=0):
    return tgt.at[idx].add(src)

def _segment_sum(src, seg, n):
    return jax.ops.segment_sum(src, seg, n)
kernel_name = 'mk_seq_preln_d4_jaxref_r8_466626'

def setup_inputs(seed: int=0):
    np.random.seed(seed)
    _w = jnp.asarray

    def _L0_attn_setup():
        import jax, jax.numpy as jnp
        import numpy as np
        import math
        EMB = 128
        HEADS = 16
        B, S = (2, 256)
        key = jax.random.key(seed)
        k_x, k_wq, k_bq, k_wu, k_bu = jax.random.split(key, 5)
        lim = 1.0 / math.sqrt(EMB)
        x = jax.random.normal(k_x, (B, S, EMB), dtype=jnp.float32)
        wq = jax.random.uniform(k_wq, (EMB, EMB), jnp.float32, -lim, lim)
        bq = jax.random.uniform(k_bq, (EMB,), jnp.float32, -lim, lim)
        wu = jax.random.uniform(k_wu, (EMB, EMB), jnp.float32, -lim, lim)
        bu = jax.random.uniform(k_bu, (EMB,), jnp.float32, -lim, lim)
        return {'x': x, 'wq': wq, 'bq': bq, 'wu': wu, 'bu': bu}
    _L0_attn_in = _L0_attn_setup()

    def _L0_ffn_setup():
        import jax, jax.numpy as jnp
        import numpy as np
        DIM = 128
        DEPTH = 6
        HEADS = 16
        DIM_HEAD = 64
        WINDOW = 32
        INNER = HEADS * DIM_HEAD
        DIM_INNER = int(DIM * 4 * 2 / 3)
        QK_SCALE = 8.0

        def shift_tokens(t):
            a, s = jnp.split(t, 2, -1)
            s = jnp.pad(s, ((0, 0), (1, 0), (0, 0)))[:, :-1]
            return jnp.concatenate([a, s], -1)

        def l2norm(t):
            return t / jnp.maximum(jnp.linalg.norm(t, axis=-1, keepdims=True), 1e-12)

        def rotate_half(x):
            x1, x2 = jnp.split(x, 2, -1)
            return jnp.concatenate([-x2, x1], -1)

        def rotary_tables(n):
            half = jnp.arange(0, DIM_HEAD, 2, dtype=jnp.float32)
            inv_freq = 1.0 / 10000.0 ** (half / DIM_HEAD)
            t = jnp.arange(n, dtype=jnp.float32)
            freqs = t[:, None] * inv_freq[None, :]
            freqs = jnp.concatenate([freqs, freqs], -1)
            base_scale = (half + 0.4 * DIM_HEAD) / (1.4 * DIM_HEAD)
            power = (t - n // 2) / (WINDOW // 2)
            scale = base_scale[None, :] ** power[:, None]
            scale = jnp.concatenate([scale, scale], -1)
            return (freqs, scale)

        def local_attention(q, k, v):
            b, h, n, d = q.shape
            w = WINDOW
            nw = n // w
            bq = q.reshape(b, h, nw, w, d)
            bk = k.reshape(b, h, nw, w, d)
            bv = v.reshape(b, h, nw, w, d)

            def look(t):
                p = jnp.pad(t, ((0, 0), (0, 0), (1, 0), (0, 0), (0, 0)))
                return jnp.concatenate([p[:, :, :nw], p[:, :, 1:]], axis=3)
            bk2, bv2 = (look(bk), look(bv))
            seq = jnp.arange(n).reshape(nw, w)
            seq_p = jnp.pad(seq, ((1, 0), (0, 0)), constant_values=-1)
            jt = jnp.concatenate([seq_p[:nw], seq_p[1:]], axis=1)
            it = seq[:, :, None]
            jb = jt[:, None, :]
            mask = (it < jb) | (it > jb + w) | (jb == -1)
            sim = jnp.einsum('bhwie,bhwje->bhwij', bq, bk2) * QK_SCALE
            sim = jnp.where(mask, -jnp.finfo(sim.dtype).max, sim)
            attn = jax.nn.softmax(sim, -1)
            out = jnp.einsum('bhwij,bhwje->bhwie', attn, bv2)
            return out.reshape(b, h, n, d)

        def attn_layer(x, Wqkv, qs, ksc, Wo):
            b, n, _ = x.shape
            qkv = x @ Wqkv
            q, k, v = jnp.split(qkv, 3, -1)
            sh = lambda t: t.reshape(b, n, HEADS, DIM_HEAD).transpose(0, 2, 1, 3)
            q, k, v = (sh(q), sh(k), sh(v))
            q = l2norm(q) * qs
            k = l2norm(k) * ksc
            freqs, scale = rotary_tables(n)
            cos, sin = (jnp.cos(freqs), jnp.sin(freqs))
            q = q * cos * scale + rotate_half(q) * sin * scale
            inv = 1.0 / scale
            k = k * cos * inv + rotate_half(k) * sin * inv
            out = local_attention(q, k, v)
            out = out.transpose(0, 2, 1, 3).reshape(b, n, INNER)
            return out @ Wo

        def ffn_layer(x, g, bln, W1, b1, W2, b2):
            mu = x.mean(-1, keepdims=True)
            var = ((x - mu) ** 2).mean(-1, keepdims=True)
            xn = (x - mu) / jnp.sqrt(var + 1e-05) * g + bln
            hg = xn @ W1 + b1
            a, gate = jnp.split(hg, 2, -1)
            return a * jax.nn.gelu(gate, approximate=False) @ W2 + b2
        key = jax.random.key(seed)
        ks = jax.random.split(key, 8)
        B, N = (2, 256)
        init = lambda k, shape: jax.random.normal(k, shape, jnp.float32) * 0.02
        return {'x': jax.random.normal(ks[0], (B, N, DIM), jnp.float32), 'Wqkv': init(ks[1], (DEPTH, DIM, 3 * INNER)), 'q_scale': jnp.ones((DEPTH, DIM_HEAD), jnp.float32), 'k_scale': jnp.ones((DEPTH, DIM_HEAD), jnp.float32), 'Wo': init(ks[2], (DEPTH, INNER, DIM)), 'ln_g': jnp.ones((DEPTH, DIM), jnp.float32), 'ln_b': jnp.zeros((DEPTH, DIM), jnp.float32), 'W1': init(ks[3], (DEPTH, DIM, 2 * DIM_INNER)), 'b1': jnp.zeros((DEPTH, 2 * DIM_INNER), jnp.float32), 'W2': init(ks[4], (DEPTH, DIM_INNER, DIM)), 'b2': jnp.zeros((DEPTH, DIM), jnp.float32)}
    _L0_ffn_in = _L0_ffn_setup()

    def _L1_attn_setup():
        import jax, jax.numpy as jnp
        import numpy as np
        N_HEAD = 16
        N_EMBD = 128
        CHUNK = 64
        ROPE_BASE = 10000.0

        def _rope_tables(head_dim, chunk_size, dtype):
            inv_freq = 1.0 / ROPE_BASE ** (jnp.arange(0, head_dim, 2, dtype=jnp.float32) / head_dim)
            t = jnp.arange(chunk_size, dtype=jnp.float32)
            freqs = jnp.outer(t, inv_freq)
            return (jnp.cos(freqs).astype(dtype), jnp.sin(freqs).astype(dtype))

        def _apply_rope(x, cos, sin):
            d = x.shape[-1] // 2
            x1, x2 = (x[..., :d], x[..., d:])
            c = cos[None, None, :, None, :]
            s = sin[None, None, :, None, :]
            return jnp.concatenate([x1 * c + x2 * s, -x1 * s + x2 * c], axis=-1)
        key = jax.random.key(seed)
        k1, k2, k3 = jax.random.split(key, 3)
        B, T, C = (4, 512, N_EMBD)
        x = jax.random.normal(k1, (B, T, C), dtype=jnp.float32)
        w_attn = jax.random.normal(k2, (3 * C, C), dtype=jnp.float32) / np.sqrt(C)
        w_proj = jax.random.normal(k3, (C, C), dtype=jnp.float32) / np.sqrt(C)
        return {'x': x, 'w_attn': w_attn, 'w_proj': w_proj}
    _L1_attn_in = _L1_attn_setup()

    def _L1_ffn_setup():
        import jax, jax.numpy as jnp
        import numpy as np
        DIM = 128
        HIDDEN = 384
        SCALE = 1.0 / 127.0

        def _dequant(w_int, dtype):
            return w_int.astype(dtype) * jnp.asarray(SCALE, dtype)
        key = jax.random.key(seed)
        k_x, k_g, k_u, k_d = jax.random.split(key, 4)
        x = jax.random.normal(k_x, (4, 256, DIM), dtype=jnp.float32)
        w_gate = jax.random.randint(k_g, (HIDDEN, DIM), -127, 128, dtype=jnp.int32)
        w_up = jax.random.randint(k_u, (HIDDEN, DIM), -127, 128, dtype=jnp.int32)
        w_down = jax.random.randint(k_d, (DIM, HIDDEN), -127, 128, dtype=jnp.int32)
        return {'x': x, 'w_gate': w_gate, 'w_up': w_up, 'w_down': w_down}
    _L1_ffn_in = _L1_ffn_setup()

    def _L2_attn_setup():
        import jax, jax.numpy as jnp
        import numpy as np
        B, L, D = (4, 256, 128)
        NREG, NMEM = (8, 16)
        DECAY = 0.995
        SHARP = 5.0
        key = jax.random.key(seed)
        ks = jax.random.split(key, 16)
        w = lambda k, shape: jax.random.normal(k, shape, jnp.float32) * 0.02
        return dict(u=jax.random.normal(ks[0], (B, L, D), jnp.float32), reg_gate_w=w(ks[1], (1, D)), reg_gate_b=jnp.full((1,), -2.0, jnp.float32), reg_addr_w=w(ks[2], (NREG, D)), reg_addr_b=jnp.zeros((NREG,), jnp.float32), reg_val_w=w(ks[3], (D, D)), reg_val_b=jnp.zeros((D,), jnp.float32), reg_q_w=w(ks[4], (D, D)), reg_q_b=jnp.zeros((D,), jnp.float32), mem_gate_w=w(ks[5], (1, D)), mem_gate_b=jnp.full((1,), -2.0, jnp.float32), mem_addr_w=w(ks[6], (NMEM, D)), mem_addr_b=jnp.zeros((NMEM,), jnp.float32), mem_val_w=w(ks[7], (D, D)), mem_val_b=jnp.zeros((D,), jnp.float32), mem_q_w=w(ks[8], (D, D)), mem_q_b=jnp.zeros((D,), jnp.float32), comb_w=w(ks[9], (D, 3 * D)), comb_b=jnp.zeros((D,), jnp.float32), ln_g=jnp.ones((D,), jnp.float32), ln_b=jnp.zeros((D,), jnp.float32))
    _L2_attn_in = _L2_attn_setup()

    def _L2_ffn_setup():
        import jax, jax.numpy as jnp
        import numpy as np
        DIM = 128
        DEPTH = 2
        HEADS = 8
        DIM_HEAD = 64
        WINDOW = 64
        INNER = HEADS * DIM_HEAD
        HID = int(DIM * 4 * 2 / 3)
        B, N = (2, 1024)
        QK_SCALE = 8.0

        def shift_token(t):
            t1, t2 = jnp.split(t, 2, axis=-1)
            t2 = jnp.pad(t2, ((0, 0), (1, 0), (0, 0)))[:, :-1]
            return jnp.concatenate([t1, t2], axis=-1)

        def l2norm(t):
            return t / jnp.clip(jnp.linalg.norm(t, axis=-1, keepdims=True), 1e-12)

        def rotate_half(x):
            x1, x2 = jnp.split(x, 2, axis=-1)
            return jnp.concatenate([-x2, x1], axis=-1)

        def rotary_xpos(q, k):
            n = q.shape[-2]
            half_idx = jnp.arange(0, DIM_HEAD, 2, dtype=jnp.float32)
            inv_freq = 1.0 / 10000.0 ** (half_idx / DIM_HEAD)
            t = jnp.arange(n, dtype=jnp.float32)
            freqs = t[:, None] * inv_freq[None, :]
            freqs = jnp.concatenate([freqs, freqs], axis=-1)
            base = (half_idx + 0.4 * DIM_HEAD) / (1.4 * DIM_HEAD)
            power = (t - n // 2) / float(WINDOW // 2)
            scale = base[None, :] ** power[:, None]
            scale = jnp.concatenate([scale, scale], axis=-1)
            cos, sin = (jnp.cos(freqs), jnp.sin(freqs))
            q = q * cos * scale + rotate_half(q) * sin * scale
            k = k * cos / scale + rotate_half(k) * sin / scale
            return (q, k)

        def local_attention(q, k, v):
            b, h, n, d = q.shape
            w = n // WINDOW
            bq = q.reshape(b, h, w, WINDOW, d) * QK_SCALE
            bk = k.reshape(b, h, w, WINDOW, d)
            bv = v.reshape(b, h, w, WINDOW, d)

            def look_around(t):
                p = jnp.pad(t, ((0, 0), (0, 0), (1, 0), (0, 0), (0, 0)))
                return jnp.concatenate([p[:, :, :w], p[:, :, 1:]], axis=3)
            bk, bv = (look_around(bk), look_around(bv))
            bt = jnp.arange(n).reshape(w, WINDOW)
            btp = jnp.pad(bt, ((1, 0), (0, 0)), constant_values=-1)
            btk = jnp.concatenate([btp[:w], btp[1:]], axis=1)
            sim = jnp.einsum('bhwid,bhwjd->bhwij', bq, bk)
            i = bt[:, :, None]
            j = btk[:, None, :]
            mask = (i < j) | (i > j + WINDOW) | (j == -1)
            sim = jnp.where(mask, -jnp.finfo(sim.dtype).max, sim)
            attn = jax.nn.softmax(sim, axis=-1)
            out = jnp.einsum('bhwij,bhwjd->bhwid', attn, bv)
            return out.reshape(b, h, n, d)

        def _layer(x, wqkv, qs, ksc, wo, lg, lb, w1, b1, w2, b2):
            b, n, _ = x.shape
            h = shift_token(x)
            qkv = h @ wqkv
            q, k, v = jnp.split(qkv, 3, axis=-1)
            to_heads = lambda t: t.reshape(b, n, HEADS, DIM_HEAD).transpose(0, 2, 1, 3)
            q, k, v = (to_heads(q), to_heads(k), to_heads(v))
            q = l2norm(q) * qs
            k = l2norm(k) * ksc
            q, k = rotary_xpos(q, k)
            o = local_attention(q, k, v)
            o = o.transpose(0, 2, 1, 3).reshape(b, n, INNER)
            x = x + o @ wo
            h = shift_token(x)
            mu = h.mean(-1, keepdims=True)
            var = h.var(-1, keepdims=True)
            h = (h - mu) / jnp.sqrt(var + 1e-05) * lg + lb
            h = h @ w1 + b1
            a, g = jnp.split(h, 2, axis=-1)
            h = a * jax.nn.gelu(g, approximate=False)
            x = x + h @ w2 + b2
            return x
        key = jax.random.key(seed)
        ks = jax.random.split(key, 6)
        return {'x': jax.random.normal(ks[0], (B, N, DIM), jnp.float32), 'wqkv': jax.random.normal(ks[1], (DEPTH, DIM, 3 * INNER), jnp.float32) * 0.02, 'q_scale': jnp.ones((DEPTH, DIM_HEAD), jnp.float32), 'k_scale': jnp.ones((DEPTH, DIM_HEAD), jnp.float32), 'wo': jax.random.normal(ks[2], (DEPTH, INNER, DIM), jnp.float32) * 0.02, 'ln_g': jnp.ones((DEPTH, DIM), jnp.float32), 'ln_b': jnp.zeros((DEPTH, DIM), jnp.float32), 'w1': jax.random.normal(ks[3], (DEPTH, DIM, 2 * HID), jnp.float32) * 0.02, 'b1': jnp.zeros((DEPTH, 2 * HID), jnp.float32), 'w2': jax.random.normal(ks[4], (DEPTH, HID, DIM), jnp.float32) * 0.02, 'b2': jnp.zeros((DEPTH, DIM), jnp.float32)}
    _L2_ffn_in = _L2_ffn_setup()

    def _L3_attn_setup():
        import math
        import jax, jax.numpy as jnp
        import numpy as np
        N_HEAD = 16
        key = jax.random.key(seed)
        k1, k2, k3, k4 = jax.random.split(key, 4)
        B, T, C, R = (4, 256, 128, 64)
        std = 0.02
        return {'hidden_states': jax.random.normal(k1, (B, T, C), dtype=jnp.float32), 'W_basis': jax.random.normal(k2, (R, C), dtype=jnp.float32) * std, 'W_v': jax.random.normal(k3, (C, C), dtype=jnp.float32) * std, 'b_v': jnp.zeros((C,), dtype=jnp.float32), 'W_o': jax.random.normal(k4, (C, C), dtype=jnp.float32) * std, 'b_o': jnp.zeros((C,), dtype=jnp.float32)}
    _L3_attn_in = _L3_attn_setup()

    def _L3_ffn_setup():
        import jax, jax.numpy as jnp
        import numpy as np
        H, E, DFF = (128, 8, 512)
        key = jax.random.key(seed)
        ks = jax.random.split(key, 7)
        s = lambda *shape: 1.0 / np.sqrt(shape[-2] if len(shape) > 1 else shape[-1])
        x = jax.random.normal(ks[0], (2, 256, H), dtype=jnp.float32)
        Wr = jax.random.normal(ks[1], (H, E), dtype=jnp.float32) * (1.0 / np.sqrt(H))
        br = jnp.zeros((E,), dtype=jnp.float32)
        W1 = jax.random.normal(ks[2], (E, H, DFF), dtype=jnp.float32) * (1.0 / np.sqrt(H))
        b1 = jnp.zeros((E, DFF), dtype=jnp.float32)
        W2 = jax.random.normal(ks[3], (E, DFF, H), dtype=jnp.float32) * (1.0 / np.sqrt(DFF))
        b2 = jnp.zeros((E, H), dtype=jnp.float32)
        return {'x': x, 'Wr': Wr, 'br': br, 'W1': W1, 'b1': b1, 'W2': W2, 'b2': b2}
    _L3_ffn_in = _L3_ffn_setup()
    _d = {'L0_attn_x': _L0_attn_in['x'], 'L0_attn_wq': _L0_attn_in['wq'], 'L0_attn_bq': _L0_attn_in['bq'], 'L0_attn_wu': _L0_attn_in['wu'], 'L0_attn_bu': _L0_attn_in['bu'], 'L0_ffn_Wqkv': _L0_ffn_in['Wqkv'], 'L0_ffn_q_scale': _L0_ffn_in['q_scale'], 'L0_ffn_k_scale': _L0_ffn_in['k_scale'], 'L0_ffn_Wo': _L0_ffn_in['Wo'], 'L0_ffn_ln_g': _L0_ffn_in['ln_g'], 'L0_ffn_ln_b': _L0_ffn_in['ln_b'], 'L0_ffn_W1': _L0_ffn_in['W1'], 'L0_ffn_b1': _L0_ffn_in['b1'], 'L0_ffn_W2': _L0_ffn_in['W2'], 'L0_ffn_b2': _L0_ffn_in['b2'], 'L1_attn_w_attn': _L1_attn_in['w_attn'], 'L1_attn_w_proj': _L1_attn_in['w_proj'], 'L1_ffn_w_gate': _L1_ffn_in['w_gate'], 'L1_ffn_w_up': _L1_ffn_in['w_up'], 'L1_ffn_w_down': _L1_ffn_in['w_down'], 'L2_attn_reg_gate_w': _L2_attn_in['reg_gate_w'], 'L2_attn_reg_gate_b': _L2_attn_in['reg_gate_b'], 'L2_attn_reg_addr_w': _L2_attn_in['reg_addr_w'], 'L2_attn_reg_addr_b': _L2_attn_in['reg_addr_b'], 'L2_attn_reg_val_w': _L2_attn_in['reg_val_w'], 'L2_attn_reg_val_b': _L2_attn_in['reg_val_b'], 'L2_attn_reg_q_w': _L2_attn_in['reg_q_w'], 'L2_attn_reg_q_b': _L2_attn_in['reg_q_b'], 'L2_attn_mem_gate_w': _L2_attn_in['mem_gate_w'], 'L2_attn_mem_gate_b': _L2_attn_in['mem_gate_b'], 'L2_attn_mem_addr_w': _L2_attn_in['mem_addr_w'], 'L2_attn_mem_addr_b': _L2_attn_in['mem_addr_b'], 'L2_attn_mem_val_w': _L2_attn_in['mem_val_w'], 'L2_attn_mem_val_b': _L2_attn_in['mem_val_b'], 'L2_attn_mem_q_w': _L2_attn_in['mem_q_w'], 'L2_attn_mem_q_b': _L2_attn_in['mem_q_b'], 'L2_attn_comb_w': _L2_attn_in['comb_w'], 'L2_attn_comb_b': _L2_attn_in['comb_b'], 'L2_attn_ln_g': _L2_attn_in['ln_g'], 'L2_attn_ln_b': _L2_attn_in['ln_b'], 'L2_ffn_wqkv': _L2_ffn_in['wqkv'], 'L2_ffn_q_scale': _L2_ffn_in['q_scale'], 'L2_ffn_k_scale': _L2_ffn_in['k_scale'], 'L2_ffn_wo': _L2_ffn_in['wo'], 'L2_ffn_ln_g': _L2_ffn_in['ln_g'], 'L2_ffn_ln_b': _L2_ffn_in['ln_b'], 'L2_ffn_w1': _L2_ffn_in['w1'], 'L2_ffn_b1': _L2_ffn_in['b1'], 'L2_ffn_w2': _L2_ffn_in['w2'], 'L2_ffn_b2': _L2_ffn_in['b2'], 'L3_attn_W_basis': _L3_attn_in['W_basis'], 'L3_attn_W_v': _L3_attn_in['W_v'], 'L3_attn_b_v': _L3_attn_in['b_v'], 'L3_attn_W_o': _L3_attn_in['W_o'], 'L3_attn_b_o': _L3_attn_in['b_o'], 'L3_ffn_Wr': _L3_ffn_in['Wr'], 'L3_ffn_br': _L3_ffn_in['br'], 'L3_ffn_W1': _L3_ffn_in['W1'], 'L3_ffn_b1': _L3_ffn_in['b1'], 'L3_ffn_W2': _L3_ffn_in['W2'], 'L3_ffn_b2': _L3_ffn_in['b2']}
    _x0 = _d['L0_attn_x']
    _d['L0_attn_x'] = jax.random.normal(jax.random.fold_in(jax.random.key(seed), 1), (16, 256, 128), dtype=_x0.dtype)
    del _x0
    return _d

def reference(L0_attn_x, L0_attn_wq, L0_attn_bq, L0_attn_wu, L0_attn_bu, L0_ffn_Wqkv, L0_ffn_q_scale, L0_ffn_k_scale, L0_ffn_Wo, L0_ffn_ln_g, L0_ffn_ln_b, L0_ffn_W1, L0_ffn_b1, L0_ffn_W2, L0_ffn_b2, L1_attn_w_attn, L1_attn_w_proj, L1_ffn_w_gate, L1_ffn_w_up, L1_ffn_w_down, L2_attn_reg_gate_w, L2_attn_reg_gate_b, L2_attn_reg_addr_w, L2_attn_reg_addr_b, L2_attn_reg_val_w, L2_attn_reg_val_b, L2_attn_reg_q_w, L2_attn_reg_q_b, L2_attn_mem_gate_w, L2_attn_mem_gate_b, L2_attn_mem_addr_w, L2_attn_mem_addr_b, L2_attn_mem_val_w, L2_attn_mem_val_b, L2_attn_mem_q_w, L2_attn_mem_q_b, L2_attn_comb_w, L2_attn_comb_b, L2_attn_ln_g, L2_attn_ln_b, L2_ffn_wqkv, L2_ffn_q_scale, L2_ffn_k_scale, L2_ffn_wo, L2_ffn_ln_g, L2_ffn_ln_b, L2_ffn_w1, L2_ffn_b1, L2_ffn_w2, L2_ffn_b2, L3_attn_W_basis, L3_attn_W_v, L3_attn_b_v, L3_attn_W_o, L3_attn_b_o, L3_ffn_Wr, L3_ffn_br, L3_ffn_W1, L3_ffn_b1, L3_ffn_W2, L3_ffn_b2):

    def _L0_attn_ref(x, wq, bq, wu, bu):
        import jax, jax.numpy as jnp
        import numpy as np
        import math
        EMB = 128
        HEADS = 16
        B, S = (2, 256)
        b, s, emb = x.shape
        hd = emb // HEADS
        q = jnp.einsum('bse,oe->bso', x, wq) + bq
        qh = q.reshape(HEADS, b, s, hd)
        kh = qh
        vh = qh
        scale = 1.0 / math.sqrt(emb)
        scores = jnp.einsum('hbqd,hbkd->hbqk', qh, kh) * scale
        attn = jax.nn.softmax(scores, axis=-1)
        out = jnp.einsum('hbqk,hbkd->hbqd', attn, vh)
        out = out.reshape(b, s, emb)
        return jnp.einsum('bse,oe->bso', out, wu) + bu

    def _L0_ffn_ref(x, Wqkv, q_scale, k_scale, Wo, ln_g, ln_b, W1, b1, W2, b2):
        import jax, jax.numpy as jnp
        import numpy as np
        DIM = 128
        DEPTH = 6
        HEADS = 16
        DIM_HEAD = 64
        WINDOW = 32
        INNER = HEADS * DIM_HEAD
        DIM_INNER = int(DIM * 4 * 2 / 3)
        QK_SCALE = 8.0

        def shift_tokens(t):
            a, s = jnp.split(t, 2, -1)
            s = jnp.pad(s, ((0, 0), (1, 0), (0, 0)))[:, :-1]
            return jnp.concatenate([a, s], -1)

        def l2norm(t):
            return t / jnp.maximum(jnp.linalg.norm(t, axis=-1, keepdims=True), 1e-12)

        def rotate_half(x):
            x1, x2 = jnp.split(x, 2, -1)
            return jnp.concatenate([-x2, x1], -1)

        def rotary_tables(n):
            half = jnp.arange(0, DIM_HEAD, 2, dtype=jnp.float32)
            inv_freq = 1.0 / 10000.0 ** (half / DIM_HEAD)
            t = jnp.arange(n, dtype=jnp.float32)
            freqs = t[:, None] * inv_freq[None, :]
            freqs = jnp.concatenate([freqs, freqs], -1)
            base_scale = (half + 0.4 * DIM_HEAD) / (1.4 * DIM_HEAD)
            power = (t - n // 2) / (WINDOW // 2)
            scale = base_scale[None, :] ** power[:, None]
            scale = jnp.concatenate([scale, scale], -1)
            return (freqs, scale)

        def local_attention(q, k, v):
            b, h, n, d = q.shape
            w = WINDOW
            nw = n // w
            bq = q.reshape(b, h, nw, w, d)
            bk = k.reshape(b, h, nw, w, d)
            bv = v.reshape(b, h, nw, w, d)

            def look(t):
                p = jnp.pad(t, ((0, 0), (0, 0), (1, 0), (0, 0), (0, 0)))
                return jnp.concatenate([p[:, :, :nw], p[:, :, 1:]], axis=3)
            bk2, bv2 = (look(bk), look(bv))
            seq = jnp.arange(n).reshape(nw, w)
            seq_p = jnp.pad(seq, ((1, 0), (0, 0)), constant_values=-1)
            jt = jnp.concatenate([seq_p[:nw], seq_p[1:]], axis=1)
            it = seq[:, :, None]
            jb = jt[:, None, :]
            mask = (it < jb) | (it > jb + w) | (jb == -1)
            sim = jnp.einsum('bhwie,bhwje->bhwij', bq, bk2) * QK_SCALE
            sim = jnp.where(mask, -jnp.finfo(sim.dtype).max, sim)
            attn = jax.nn.softmax(sim, -1)
            out = jnp.einsum('bhwij,bhwje->bhwie', attn, bv2)
            return out.reshape(b, h, n, d)

        def attn_layer(x, Wqkv, qs, ksc, Wo):
            b, n, _ = x.shape
            qkv = x @ Wqkv
            q, k, v = jnp.split(qkv, 3, -1)
            sh = lambda t: t.reshape(b, n, HEADS, DIM_HEAD).transpose(0, 2, 1, 3)
            q, k, v = (sh(q), sh(k), sh(v))
            q = l2norm(q) * qs
            k = l2norm(k) * ksc
            freqs, scale = rotary_tables(n)
            cos, sin = (jnp.cos(freqs), jnp.sin(freqs))
            q = q * cos * scale + rotate_half(q) * sin * scale
            inv = 1.0 / scale
            k = k * cos * inv + rotate_half(k) * sin * inv
            out = local_attention(q, k, v)
            out = out.transpose(0, 2, 1, 3).reshape(b, n, INNER)
            return out @ Wo

        def ffn_layer(x, g, bln, W1, b1, W2, b2):
            mu = x.mean(-1, keepdims=True)
            var = ((x - mu) ** 2).mean(-1, keepdims=True)
            xn = (x - mu) / jnp.sqrt(var + 1e-05) * g + bln
            hg = xn @ W1 + b1
            a, gate = jnp.split(hg, 2, -1)
            return a * jax.nn.gelu(gate, approximate=False) @ W2 + b2
        for i in range(DEPTH):
            x = attn_layer(shift_tokens(x), Wqkv[i], q_scale[i], k_scale[i], Wo[i]) + x
            x = ffn_layer(shift_tokens(x), ln_g[i], ln_b[i], W1[i], b1[i], W2[i], b2[i]) + x
        return x

    def _L1_attn_ref(x, w_attn, w_proj):
        import jax, jax.numpy as jnp
        import numpy as np
        N_HEAD = 16
        N_EMBD = 128
        CHUNK = 64
        ROPE_BASE = 10000.0

        def _rope_tables(head_dim, chunk_size, dtype):
            inv_freq = 1.0 / ROPE_BASE ** (jnp.arange(0, head_dim, 2, dtype=jnp.float32) / head_dim)
            t = jnp.arange(chunk_size, dtype=jnp.float32)
            freqs = jnp.outer(t, inv_freq)
            return (jnp.cos(freqs).astype(dtype), jnp.sin(freqs).astype(dtype))

        def _apply_rope(x, cos, sin):
            d = x.shape[-1] // 2
            x1, x2 = (x[..., :d], x[..., d:])
            c = cos[None, None, :, None, :]
            s = sin[None, None, :, None, :]
            return jnp.concatenate([x1 * c + x2 * s, -x1 * s + x2 * c], axis=-1)
        B, T, C = x.shape
        H, cs = (N_HEAD, CHUNK)
        d = C // H
        nc = T // cs
        qkv = jnp.einsum('btc,fc->btf', x, w_attn)
        q, k, v = jnp.split(qkv, 3, axis=2)
        q = q.reshape(B, nc, cs, H, d)
        k = k.reshape(B, nc, cs, H, d)
        v = v.reshape(B, nc, cs, H, d)
        cos, sin = _rope_tables(d, cs, x.dtype)
        q = _apply_rope(q, cos, sin)
        k = _apply_rope(k, cos, sin)
        scale = 1.0 / np.sqrt(d)
        scores = jnp.einsum('bnqhd,bnkhd->bnhqk', q, k) * scale
        p = jax.nn.softmax(scores, axis=-1)
        y = jnp.einsum('bnhqk,bnkhd->bnqhd', p, v)
        y = y.reshape(B, T, C)
        return jnp.einsum('btc,oc->bto', y, w_proj)

    def _L1_ffn_ref(x, w_gate, w_up, w_down):
        import jax, jax.numpy as jnp
        import numpy as np
        DIM = 128
        HIDDEN = 384
        SCALE = 1.0 / 127.0

        def _dequant(w_int, dtype):
            return w_int.astype(dtype) * jnp.asarray(SCALE, dtype)
        wg = _dequant(w_gate, x.dtype)
        wu = _dequant(w_up, x.dtype)
        wd = _dequant(w_down, x.dtype)
        gate = jnp.einsum('bsd,hd->bsh', x, wg)
        up = jnp.einsum('bsd,hd->bsh', x, wu)
        h = jax.nn.silu(gate) * up
        return jnp.einsum('bsh,dh->bsd', h, wd)

    def _L2_attn_ref(u, reg_gate_w, reg_gate_b, reg_addr_w, reg_addr_b, reg_val_w, reg_val_b, reg_q_w, reg_q_b, mem_gate_w, mem_gate_b, mem_addr_w, mem_addr_b, mem_val_w, mem_val_b, mem_q_w, mem_q_b, comb_w, comb_b, ln_g, ln_b):
        import jax, jax.numpy as jnp
        import numpy as np
        B, L, D = (4, 256, 128)
        NREG, NMEM = (8, 16)
        DECAY = 0.995
        SHARP = 5.0
        Bb, Ll, Dd = u.shape
        n_reg = reg_addr_w.shape[0]
        n_mem = mem_addr_w.shape[0]
        scale = Dd ** (-0.5)
        lin = lambda x, w, b: x @ w.T + b
        h = u
        rg = jax.nn.sigmoid(SHARP * lin(h, reg_gate_w, reg_gate_b))
        ra = jax.nn.softmax(lin(h, reg_addr_w, reg_addr_b), axis=-1)
        rv = lin(h, reg_val_w, reg_val_b)
        rq = lin(h, reg_q_w, reg_q_b)
        mg = jax.nn.sigmoid(SHARP * lin(h, mem_gate_w, mem_gate_b))
        ma = jax.nn.softmax(lin(h, mem_addr_w, mem_addr_b), axis=-1)
        mv = lin(h, mem_val_w, mem_val_b)
        mq = lin(h, mem_q_w, mem_q_b)
        W_h, W_r, W_m = (comb_w[:, :Dd], comb_w[:, Dd:2 * Dd], comb_w[:, 2 * Dd:])
        pre = h @ W_h.T + comb_b

        def layer_norm(x):
            m = x.mean(-1, keepdims=True)
            v = ((x - m) ** 2).mean(-1, keepdims=True)
            return ln_g * (x - m) * jax.lax.rsqrt(v + 1e-05) + ln_b

        def step(carry, xs):
            reg_s, mem_s = carry
            h_t, rg_t, ra_t, rv_t, rq_t, mg_t, ma_t, mv_t, mq_t, p_t = xs
            reg_s = reg_s + rg_t[:, :, None] * ra_t[:, :, None] * rv_t[:, None, :]
            r_scores = jnp.einsum('bnd,bd->bn', reg_s, rq_t) * scale
            r_read = jnp.einsum('bn,bnd->bd', jax.nn.softmax(r_scores, -1), reg_s)
            mem_s = mem_s * DECAY + mg_t[:, :, None] * ma_t[:, :, None] * mv_t[:, None, :]
            m_scores = jnp.einsum('bnd,bd->bn', mem_s, mq_t) * scale
            m_read = jnp.einsum('bn,bnd->bd', jax.nn.softmax(m_scores, -1), mem_s)
            c = p_t + r_read @ W_r.T + m_read @ W_m.T
            return ((reg_s, mem_s), layer_norm(c + h_t))
        to_time_major = lambda a: jnp.swapaxes(a, 0, 1)
        xs = tuple((to_time_major(a) for a in (h, rg, ra, rv, rq, mg, ma, mv, mq, pre)))
        init = (jnp.zeros((Bb, n_reg, Dd), u.dtype), jnp.zeros((Bb, n_mem, Dd), u.dtype))
        _, out = jax.lax.scan(step, init, xs)
        return jnp.swapaxes(out, 0, 1)

    def _L2_ffn_ref(x, wqkv, q_scale, k_scale, wo, ln_g, ln_b, w1, b1, w2, b2):
        import jax, jax.numpy as jnp
        import numpy as np
        DIM = 128
        DEPTH = 2
        HEADS = 8
        DIM_HEAD = 64
        WINDOW = 64
        INNER = HEADS * DIM_HEAD
        HID = int(DIM * 4 * 2 / 3)
        B, N = (2, 1024)
        QK_SCALE = 8.0

        def shift_token(t):
            t1, t2 = jnp.split(t, 2, axis=-1)
            t2 = jnp.pad(t2, ((0, 0), (1, 0), (0, 0)))[:, :-1]
            return jnp.concatenate([t1, t2], axis=-1)

        def l2norm(t):
            return t / jnp.clip(jnp.linalg.norm(t, axis=-1, keepdims=True), 1e-12)

        def rotate_half(x):
            x1, x2 = jnp.split(x, 2, axis=-1)
            return jnp.concatenate([-x2, x1], axis=-1)

        def rotary_xpos(q, k):
            n = q.shape[-2]
            half_idx = jnp.arange(0, DIM_HEAD, 2, dtype=jnp.float32)
            inv_freq = 1.0 / 10000.0 ** (half_idx / DIM_HEAD)
            t = jnp.arange(n, dtype=jnp.float32)
            freqs = t[:, None] * inv_freq[None, :]
            freqs = jnp.concatenate([freqs, freqs], axis=-1)
            base = (half_idx + 0.4 * DIM_HEAD) / (1.4 * DIM_HEAD)
            power = (t - n // 2) / float(WINDOW // 2)
            scale = base[None, :] ** power[:, None]
            scale = jnp.concatenate([scale, scale], axis=-1)
            cos, sin = (jnp.cos(freqs), jnp.sin(freqs))
            q = q * cos * scale + rotate_half(q) * sin * scale
            k = k * cos / scale + rotate_half(k) * sin / scale
            return (q, k)

        def local_attention(q, k, v):
            b, h, n, d = q.shape
            w = n // WINDOW
            bq = q.reshape(b, h, w, WINDOW, d) * QK_SCALE
            bk = k.reshape(b, h, w, WINDOW, d)
            bv = v.reshape(b, h, w, WINDOW, d)

            def look_around(t):
                p = jnp.pad(t, ((0, 0), (0, 0), (1, 0), (0, 0), (0, 0)))
                return jnp.concatenate([p[:, :, :w], p[:, :, 1:]], axis=3)
            bk, bv = (look_around(bk), look_around(bv))
            bt = jnp.arange(n).reshape(w, WINDOW)
            btp = jnp.pad(bt, ((1, 0), (0, 0)), constant_values=-1)
            btk = jnp.concatenate([btp[:w], btp[1:]], axis=1)
            sim = jnp.einsum('bhwid,bhwjd->bhwij', bq, bk)
            i = bt[:, :, None]
            j = btk[:, None, :]
            mask = (i < j) | (i > j + WINDOW) | (j == -1)
            sim = jnp.where(mask, -jnp.finfo(sim.dtype).max, sim)
            attn = jax.nn.softmax(sim, axis=-1)
            out = jnp.einsum('bhwij,bhwjd->bhwid', attn, bv)
            return out.reshape(b, h, n, d)

        def _layer(x, wqkv, qs, ksc, wo, lg, lb, w1, b1, w2, b2):
            b, n, _ = x.shape
            h = shift_token(x)
            qkv = h @ wqkv
            q, k, v = jnp.split(qkv, 3, axis=-1)
            to_heads = lambda t: t.reshape(b, n, HEADS, DIM_HEAD).transpose(0, 2, 1, 3)
            q, k, v = (to_heads(q), to_heads(k), to_heads(v))
            q = l2norm(q) * qs
            k = l2norm(k) * ksc
            q, k = rotary_xpos(q, k)
            o = local_attention(q, k, v)
            o = o.transpose(0, 2, 1, 3).reshape(b, n, INNER)
            x = x + o @ wo
            h = shift_token(x)
            mu = h.mean(-1, keepdims=True)
            var = h.var(-1, keepdims=True)
            h = (h - mu) / jnp.sqrt(var + 1e-05) * lg + lb
            h = h @ w1 + b1
            a, g = jnp.split(h, 2, axis=-1)
            h = a * jax.nn.gelu(g, approximate=False)
            x = x + h @ w2 + b2
            return x
        for l in range(DEPTH):
            x = _layer(x, wqkv[l], q_scale[l], k_scale[l], wo[l], ln_g[l], ln_b[l], w1[l], b1[l], w2[l], b2[l])
        return x

    def _L3_attn_ref(hidden_states, W_basis, W_v, b_v, W_o, b_o):
        import math
        import jax, jax.numpy as jnp
        import numpy as np
        N_HEAD = 16
        B, T, C = hidden_states.shape
        nh = N_HEAD
        hd = C // nh
        R = W_basis.shape[0]
        latent = hidden_states @ W_basis.T
        v = hidden_states @ W_v.T + b_v
        v = v.reshape(B, T, nh, hd).transpose(0, 2, 1, 3)
        scores = jnp.einsum('bqr,bkr->bqk', latent, latent) * (1.0 / math.sqrt(R))
        causal = jnp.tril(jnp.ones((T, T), dtype=bool))
        scores = jnp.where(causal[None, :, :], scores, -jnp.inf)
        att = jax.nn.softmax(scores, axis=-1)
        y = jnp.einsum('bqk,bhkd->bhqd', att, v)
        y = y.transpose(0, 2, 1, 3).reshape(B, T, C)
        out = y @ W_o.T + b_o
        return out

    def _L3_ffn_ref(x, Wr, br, W1, b1, W2, b2):
        import jax, jax.numpy as jnp
        import numpy as np
        H, E, DFF = (128, 8, 512)
        B, S, Hd = x.shape
        n_exp = W1.shape[0]
        xt = x.reshape(-1, Hd)
        logits = xt @ Wr + br
        probs = jax.nn.softmax(logits, axis=-1)
        gate = jnp.max(probs, axis=-1)
        idx = jnp.argmax(probs, axis=-1)
        h1 = jnp.maximum(jnp.einsum('th,ehf->etf', xt, W1) + b1[:, None, :], 0.0)
        ye = jnp.einsum('etf,efh->eth', h1, W2) + b2[:, None, :]
        onehot = jax.nn.one_hot(idx, n_exp, dtype=xt.dtype)
        y = jnp.einsum('te,eth->th', onehot, ye) * gate[:, None]
        return y.reshape(B, S, Hd)
    x = L0_attn_x
    x = x + _L0_attn_ref(_layernorm(x, axis=-1), L0_attn_wq, L0_attn_bq, L0_attn_wu, L0_attn_bu)
    x = x + _L0_ffn_ref(_layernorm(x, axis=-1), L0_ffn_Wqkv, L0_ffn_q_scale, L0_ffn_k_scale, L0_ffn_Wo, L0_ffn_ln_g, L0_ffn_ln_b, L0_ffn_W1, L0_ffn_b1, L0_ffn_W2, L0_ffn_b2)
    x = x + _L1_attn_ref(_layernorm(x, axis=-1), L1_attn_w_attn, L1_attn_w_proj)
    x = x + _L1_ffn_ref(_layernorm(x, axis=-1), L1_ffn_w_gate, L1_ffn_w_up, L1_ffn_w_down)
    x = x + _L2_attn_ref(_layernorm(x, axis=-1), L2_attn_reg_gate_w, L2_attn_reg_gate_b, L2_attn_reg_addr_w, L2_attn_reg_addr_b, L2_attn_reg_val_w, L2_attn_reg_val_b, L2_attn_reg_q_w, L2_attn_reg_q_b, L2_attn_mem_gate_w, L2_attn_mem_gate_b, L2_attn_mem_addr_w, L2_attn_mem_addr_b, L2_attn_mem_val_w, L2_attn_mem_val_b, L2_attn_mem_q_w, L2_attn_mem_q_b, L2_attn_comb_w, L2_attn_comb_b, L2_attn_ln_g, L2_attn_ln_b)
    x = x + _L2_ffn_ref(_layernorm(x, axis=-1), L2_ffn_wqkv, L2_ffn_q_scale, L2_ffn_k_scale, L2_ffn_wo, L2_ffn_ln_g, L2_ffn_ln_b, L2_ffn_w1, L2_ffn_b1, L2_ffn_w2, L2_ffn_b2)
    x = x + _L3_attn_ref(_layernorm(x, axis=-1), L3_attn_W_basis, L3_attn_W_v, L3_attn_b_v, L3_attn_W_o, L3_attn_b_o)
    x = x + _L3_ffn_ref(_layernorm(x, axis=-1), L3_ffn_Wr, L3_ffn_br, L3_ffn_W1, L3_ffn_b1, L3_ffn_W2, L3_ffn_b2)
    return x

_drawn_inputs = setup_inputs


def setup_inputs(seed=0):
    import zlib

    import numpy as np

    out = dict(_drawn_inputs(seed))
    spreads = {'L0_ffn_q_scale': (1.0, 0.6),
     'L0_ffn_k_scale': (1.0, 0.6),
     'L0_ffn_ln_g': (1.0, 0.6),
     'L0_ffn_ln_b': (0.0, 0.8),
     'L0_ffn_b1': (0.0, 0.653),
     'L0_ffn_b2': (0.0, 0.1),
     'L2_attn_reg_addr_b': (0.0, 0.8),
     'L2_attn_reg_val_b': (0.0, 2.0),
     'L2_attn_reg_q_b': (0.0, 0.8),
     'L2_attn_mem_addr_b': (0.0, 0.8),
     'L2_attn_mem_val_b': (0.0, 2.0),
     'L2_attn_mem_q_b': (0.0, 0.8),
     'L2_attn_comb_b': (0.0, 2.0),
     'L2_attn_ln_g': (1.0, 0.6),
     'L2_attn_ln_b': (0.0, 2.0),
     'L2_ffn_q_scale': (1.0, 0.6),
     'L2_ffn_k_scale': (1.0, 0.6),
     'L2_ffn_ln_g': (1.0, 0.6),
     'L2_ffn_ln_b': (0.0, 0.8),
     'L2_ffn_b1': (0.0, 0.8),
     'L2_ffn_b2': (0.0, 2.0),
     'L3_attn_b_v': (0.0, 2.0),
     'L3_attn_b_o': (0.0, 2.0),
     'L3_ffn_br': (0.0, 0.8),
     'L3_ffn_b1': (0.0, 2.0),
     'L3_ffn_b2': (0.0, 2.0)}
    factors = {'L0_attn_bq': 3.595,
     'L2_attn_reg_gate_w': 64.0,
     'L2_attn_reg_val_w': 64.0,
     'L2_attn_mem_gate_w': 64.0,
     'L2_attn_mem_val_w': 64.0,
     'L2_attn_comb_w': 61.289,
     'L2_ffn_wqkv': 8.0,
     'L2_ffn_wo': 8.0,
     'L2_ffn_w1': 8.0,
     'L2_ffn_w2': 8.0,
     'L3_attn_W_basis': 64.0,
     'L3_attn_W_v': 37.64,
     'L3_attn_W_o': 35.808,
     'L3_ffn_Wr': 8.0,
     'L3_ffn_W1': 8.0,
     'L3_ffn_W2': 8.0,
     'L2_attn_reg_addr_w': 8.0,
     'L2_attn_reg_q_w': 8.0,
     'L2_attn_mem_addr_w': 8.0,
     'L2_attn_mem_q_w': 8.0}
    for name, (base, spread) in spreads.items():
        noise = np.random.default_rng([zlib.crc32(name.encode()), seed]).standard_normal(out[name].shape)
        drawn = base * np.exp(spread * noise) if base else spread * noise
        out[name] = jnp.asarray(drawn.astype(out[name].dtype))
    for name, factor in factors.items():
        out[name] = (out[name] * factor).astype(out[name].dtype)
    return out
```

```python
from contextlib import ExitStack

import numpy as np

import concourse.bass as bass
from concourse import mybir

F32 = mybir.dt.float32
BF16 = mybir.dt.bfloat16
I32 = mybir.dt.int32
ALU = mybir.AluOpType
ACT = mybir.ActivationFunctionType
AX = mybir.AxisListType

P = 128
CH = 128
SEQ = 16
TOK = 256
NT = TOK // P
HD = 64
HID = 341
HCH = 3
HLAST = HID - 2 * P
MASKED = -1.0e37
EPS = 1e-5


class Count:

    def __init__(self, sem, per, credit=None):
        self.sem, self.per = sem, per
        self.credit = per if credit is None else credit

    def done(self, turn, m=0):
        return turn * self.per + (self.credit + m + 1)

    def prev(self, turn, m=0):
        return turn * self.per + (self.credit + m + 1 - self.per)


def hold(eng, sem, value, passed):
    eng.wait_ge(sem, value)
    eng.sem_inc(passed, 1)


def fresh(ap, n):
    return ap.rearrange("p (a b) -> p a b", b=n)


def norm_stream(nc, name, x, z, zT, ident, psum):
    GR = 4
    NG = SEQ * NT // GR
    with ExitStack() as ctx:
        def sem(n):
            return ctx.enter_context(nc.semaphore(f"{name}_{n}"))

        stats = ctx.enter_context(nc.sbuf_tensor(f"{name}_stats", [P, 2, GR, 6], F32))
        mv = ctx.enter_context(nc.sbuf_tensor(f"{name}_mv", [P, 2, GR, 2], F32))
        ve = ctx.enter_context(nc.sbuf_tensor(f"{name}_ve", [P, 2, GR], F32))
        rstd = ctx.enter_context(nc.sbuf_tensor(f"{name}_rstd", [P, 2, GR], F32))
        power = ctx.enter_context(nc.sbuf_tensor(f"{name}_pow", [P, GR], F32))
        zs = ctx.enter_context(nc.sbuf_tensor(f"{name}_zs", [P, 2, GR, CH], F32))
        stats_ready = Count(sem("stats"), 2)
        mv_ready = Count(sem("mv"), 2)
        ve_ready = Count(sem("ve"), 2)
        rstd_ready = Count(sem("rstd"), 2)
        z_ready = Count(sem("z"), 2)
        power_ready = sem("power")
        dve_passed, pool_passed = sem("dve_passed"), sem("pool_passed")
        turned = Count(sem("turned"), 2)
        zt_ready = Count(sem("zt"), 2)

        with nc.Block() as block:
            @block.vector
            def _(dve):
                for s in (stats_ready, mv_ready, z_ready):
                    dve.sem_inc(s.sem, s.credit)

                def statistics(g, h):
                    for k in range(GR):
                        last = dve.bn_stats(stats[:, h, k, :], x[:, bass.ds(g * 2 * GR + (h * GR + k), 1), :]
                                            .rearrange("p a c -> p (a c)"))
                    last.then_inc(stats_ready.sem, 1)
                    hold(dve, stats_ready.sem, stats_ready.done(g, h), dve_passed)
                    for k in range(GR):
                        last = dve.bn_aggr(mv[:, h, k, :], stats[:, h, k, :])
                    last.then_inc(mv_ready.sem, 1)

                def normalise(g, h):
                    dve.wait_ge(rstd_ready.sem, rstd_ready.done(g, h))
                    if zT is not None:
                        dve.wait_ge(turned.sem, turned.prev(g, h))
                    for k in range(GR):
                        tile = bass.ds(g * 2 * GR + (h * GR + k), 1)
                        for dst in ([] if z is None else [z[:, tile, :].rearrange("p a c -> p (a c)")]) + \
                                ([] if zT is None else [zs[:, h, k, :]]):
                            last = dve.tensor_scalar(dst, x[:, tile, :].rearrange("p a c -> p (a c)"),
                                                     mv[:, h, k, 0:1], rstd[:, h, k:k + 1],
                                                     ALU.subtract, ALU.mult)
                    last.then_inc(z_ready.sem, 1)

                with dve.Fori(0, NG // 2) as g:
                    for h in range(2):
                        statistics(g, h)
                    for h in range(2):
                        normalise(g, h)

            @block.gpsimd
            def _(pool):
                for s in (ve_ready, rstd_ready):
                    pool.sem_inc(s.sem, s.credit)
                pool.memset(power[:], -0.5).then_inc(power_ready, 1)
                pool.wait_ge(power_ready, 1)
                with pool.Fori(0, NG // 2) as g:
                    for h in range(2):
                        hold(pool, mv_ready.sem, mv_ready.done(g, h), pool_passed)
                        pool.tensor_scalar(ve[:, h, :], mv[:, h, :, 1], EPS, None, ALU.add).then_inc(ve_ready.sem, 1)
                        pool.wait_ge(ve_ready.sem, ve_ready.done(g, h))
                        pool.tensor_tensor(out=rstd[:, h, :], in0=ve[:, h, :], in1=power[:], op=ALU.pow)\
                            .then_inc(rstd_ready.sem, 1)

            if zT is not None:
                @block.tensor
                def _(pe):
                    pe.sem_inc(turned.sem, turned.credit)
                    with pe.Fori(0, NG // 2) as g:
                        for h in range(2):
                            pe.wait_ge(z_ready.sem, z_ready.done(g, h))
                            pe.wait_ge(zt_ready.sem, zt_ready.prev(g, h))
                            for k in range(GR):
                                last = pe.transpose(psum[h][:, k * P:(k + 1) * P], zs[:, h, k, :], ident[:])
                            last.then_inc(turned.sem, 1)

                @block.scalar
                def _(act):
                    act.sem_inc(zt_ready.sem, zt_ready.credit)
                    with act.Fori(0, NG // 2) as g:
                        for h in range(2):
                            act.wait_ge(turned.sem, turned.done(g, h))
                            act.activation(zT[:, bass.ds(g * 2 * GR * P + h * GR * P, GR * P)], psum[h][:], ACT.Copy)\
                               .then_inc(zt_ready.sem, 1)


def local_stack(nc, name, z, W, H, depth, wts, consts, psum, turns=SEQ):
    ident, identb = consts["ident"], consts["identb"]
    INNER = H * HD
    NP = H // 2
    G = P // W
    NW = TOK // W // 2
    K2 = 2 * W
    CW = 512
    QC = INNER // CW
    PC = CW // P
    per_round = ["qkv", "qkv"] if QC == 2 else ["qk", "v"]
    chunks, of_unit = [], []
    for u in range(4):
        of_unit.append(list(range(len(chunks), len(chunks) + len(per_round[u % 2]))))
        chunks += [(u // 2, w, u % 2 if QC == 2 else 0) for w in per_round[u % 2]]
    NC = len(chunks)
    qk = [c for c in range(NC) if chunks[c][1] != "v"]
    vs = [c for c in range(NC) if chunks[c][1] == "v"]
    NQ, NV = len(qk), len(vs)
    qk_of_unit = [[qk.index(c) for c in of_unit[u] if c in qk] for u in range(4)]
    needed = [max(n for v in qk_of_unit[:u + 1] for n in v) for u in range(4)]
    v_done = [max(c for c in vs if chunks[c][0] == t) for t in range(NT)]
    BP = K2 * NW // P
    WB = NW // BP
    VC = HD + 1
    B_QKV, B_S, B_PT, B_O, B_T = (0, 1), (2, 3), 4, (5, 6), 7

    with ExitStack() as ctx:
        def sb(n, shape, dt=F32):
            return ctx.enter_context(nc.sbuf_tensor(f"{name}_{n}", shape, dt))

        def sem(n):
            return ctx.enter_context(nc.semaphore(f"{name}_{n}"))

        wqkv = sb("wqkv", [P, 3 * INNER])
        wo = sb("wo", [P, NP, CH])
        w1 = sb("w1", [P, 2 * HID])
        w2 = sb("w2", [P, HCH, CH])
        b1 = sb("b1", [P, 2 * HCH])
        gb = sb("gb", [P, 2])
        scales = sb("scales", [P, 2, HD])
        rope = sb("rope", [P, NT, 4, HD])
        table = sb("table", [P, NT, 4, HD])
        maskb = sb("maskb", [P, 2, 512], BF16)
        power = sb("power", [P, 8])
        hs = sb("hs", [P, NT, CH])
        hT = sb("hT", [P, TOK])
        sq = sb("sq", [P, 2, CW])
        ssq = sb("ssq", [P, 2, 8])
        rn = sb("rn", [P, 2, 8])
        qc = sb("qc", [P, 4, CW])
        t1 = sb("t1", [P, 2, CW])
        t2 = sb("t2", [P, 2, CW])
        qr = sb("qr", [P, 4, CW])
        qT = sb("qT", [P, NP, TOK])
        kbd = sb("kbd", [P, NP, 2, NT * (W + P)])
        vtok = sb("vtok", [P, NT, INNER])
        VH = 2 if WB == 2 else 1
        vw = sb("vw", [P, 2 * BP, VH, H, VC])
        mx = sb("mx", [P, 2, NW * 2])
        sd = sb("sd", [P, 2, 512])
        pr = sb("pr", [P, 2, 512])
        pT = sb("pT", [P, 2, 512])
        rd = sb("rd", [P, 2, NW])
        on = sb("on", [P, 2, NW, 2, HD])
        oT = sb("oT", [P, NP, TOK])
        fhs = sb("fhs", [P, NT, CH])
        fst = sb("fst", [P, NT, 6])
        fmv = sb("fmv", [P, NT, 2])
        fve = sb("fve", [P, NT])
        frs = sb("frs", [P, NT])
        fhn = sb("fhn", [P, NT, CH])
        fhT = sb("fhT", [P, TOK])
        gl = sb("gl", [P, HCH, TOK])
        hu = sb("hu", [P, HCH, TOK])

        init = sem("init")
        mask_ready = sem("mask")
        dve_passed, pool_passed, sp_passed = sem("dve_passed"), sem("pool_passed"), sem("sp_passed")
        const_ld = sem("const_ld")
        attn_w = Count(sem("attn_w"), 16 * 3, 0)
        ffn_w = Count(sem("ffn_w"), 16 * 4, 0)
        table_ready = Count(sem("table"), 1, 1)
        hs_ld = Count(sem("hs_ld"), 16 * 3, 0)
        hT_ps = Count(sem("hT_ps"), 1)
        hT_ready = Count(sem("hT"), 1)
        qkv_ready = Count(sem("qkv"), NC)
        copied = Count(sem("copied"), NC)
        sq_ready = Count(sem("sq"), NQ)
        ssq_ready = Count(sem("ssq"), NQ)
        rmax_ready = Count(sem("rmax"), NQ)
        rn_ready = Count(sem("rn"), NQ)
        sum_ready = Count(sem("sum"), NQ)
        t1_ready = Count(sem("t1"), NQ)
        t2_ready = Count(sem("t2"), NQ)
        qr_ready = Count(sem("qr"), NQ)
        qrT_ps = Count(sem("qrT_ps"), NQ)
        qkT_ready = Count(sem("qkT"), NQ)
        s_ready = Count(sem("s"), 4)
        mx_ready = Count(sem("mx"), 4)
        sd_ready = Count(sem("sd"), 4)
        p_ready = Count(sem("p"), 4)
        pT_ps = Count(sem("pT_ps"), 4)
        pT_ready = Count(sem("pT"), 4)
        o_ready = Count(sem("o"), 8)
        rd_ready = Count(sem("rd"), 8)
        on_ready = Count(sem("on"), 8)
        oT_ps = Count(sem("oT_ps"), 4)
        oT_ready = Count(sem("oT"), 4)
        y_ready = Count(sem("y"), NT)
        za_done = Count(sem("za"), NT)
        zf_done = Count(sem("zf"), 1, turns)
        fhs_ld = Count(sem("fhs_ld"), 16 * 3, 0)
        fst_ready = Count(sem("fst"), 1)
        fmv_ready = Count(sem("fmv"), 1)
        fve_ready = Count(sem("fve"), 1)
        frs_ready = Count(sem("frs"), 1)
        fhn_ready = Count(sem("fhn"), 1)
        fhT_ps = Count(sem("fhT_ps"), 1)
        fhT_ready = Count(sem("fhT"), 1)
        g_ready = Count(sem("g"), HCH)
        gl_ready = Count(sem("gl"), HCH)
        hu_ready = Count(sem("hu"), HCH)
        fy_ready = Count(sem("fy"), 1)
        vdmas, tail = [[], []], None
        for w in range(TOK // W):
            k, blk, half = w // NW, w // WB, w % WB
            for part in range(2):
                tok = W * (w - 1 + part)
                if tok >= 0:
                    row = (half * K2 + part * W) if WB == 2 else part * W
                    piece = (row, blk, half, tok // P, tok % P)
                    if tok // P == k:
                        vdmas[k].append(piece)
                    else:
                        tail = piece
        vw_ld = [Count(sem(f"vw_ld{k}"), 16 * len(vdmas[k]), 1) for k in range(2)]
        tail_ld = Count(sem("tail_ld"), 16, 1)
        NINIT = 8

        def unit_pairs(u):
            return [(u % 2) * G + j for j in range(G)]

        def steps(i, u, new, old, ahead):
            now = (i, u) if new else None
            before1 = ((i, u - 1) if new else None) if u else ((i - 1, 3) if old else None)
            before2 = ((i, u - 2) if new else None) if u >= 2 else ((i - 1, u + 2) if old else None)
            turned = ((i, u + 1) if new else None) if u < 3 else ((i + 1, 0) if ahead else None)
            projected = ((i, u + 2) if new else None) if u < 2 else ((i + 1, u - 2) if ahead else None)
            return now, before1, before2, turned, projected

        def sweep(eng, l, slot):
            def turn(b, new, old, ahead):
                for u in range(4):
                    slot(l, b, u, new, old, ahead)

            turn(-1, False, False, True)
            turn(0, True, False, True)
            with eng.Fori(0, turns - 2) as b:
                turn(b + 1, True, True, True)
            turn(turns - 1, True, True, False)
            turn(turns, False, True, False)

        with nc.Block() as block:
            @block.sync
            def _(sp):
                sp.dma_start(rope[:], wts["rope"]).then_inc(const_ld, 16)
                sp.dma_start(sd[:], wts["mask"]).then_inc(const_ld, 16)

                def shifted(b, dst, ld):
                    sp.dma_start(dst[:, :, 0:64], z[:, bass.ds(b * NT, NT), 0:64]).then_inc(ld.sem, 16)
                    sp.dma_start(dst[1:P, :, 64:CH], z[0:P - 1, bass.ds(b * NT, NT), 64:CH]).then_inc(ld.sem, 16)
                    sp.dma_start(dst[0:1, 1, 64:CH], z[P - 1:P, bass.ds(b * NT, 1), 64:CH]
                                 .rearrange("p a c -> p (a c)")).then_inc(ld.sem, 16)

                def load_hs(l, b):
                    i = l * turns + b
                    hold(sp, zf_done.sem, i + 1, sp_passed)
                    hold(sp, hT_ps.sem, hT_ps.prev(i), sp_passed)
                    shifted(b, hs, hs_ld)

                def load_piece(piece, ld):
                    row, blk, half, t, src = piece
                    sp.dma_start(vw[row:row + W, blk, half, :, 0:HD],
                                 vtok[src:src + W, t, :].rearrange("p (h d) -> p h d", d=HD)).then_inc(ld.sem, 16)

                def load_tail(i):
                    hold(sp, copied.sem, copied.done(i, v_done[0]), sp_passed)
                    hold(sp, o_ready.sem, o_ready.prev(i, 7), sp_passed)
                    load_piece(tail, tail_ld)

                def load_vw(i, k):
                    hold(sp, copied.sem, copied.done(i, v_done[k]), sp_passed)
                    hold(sp, o_ready.sem, o_ready.prev(i, 4 * k + 3), sp_passed)
                    for piece in vdmas[k]:
                        load_piece(piece, vw_ld[k])

                def load_fhs(l, b):
                    i = l * turns + b
                    hold(sp, za_done.sem, za_done.done(i, 1), sp_passed)
                    hold(sp, fhn_ready.sem, fhn_ready.prev(i), sp_passed)
                    shifted(b, fhs, fhs_ld)

                for s in vw_ld + [tail_ld]:
                    sp.sem_inc(s.sem, s.credit)
                sp.wait_ge(init, NINIT)
                with sp.Fori(0, depth) as l:
                    at = bass.ds(l, 1)
                    hold(sp, zf_done.sem, l * turns + turns, sp_passed)
                    hold(sp, za_done.sem, za_done.prev(l * turns, 1), sp_passed)
                    sp.dma_start(wqkv[:], wts["Wqkv"][at].rearrange("l k n -> k (l n)")).then_inc(attn_w.sem, 16)
                    sp.dma_start(wo[:], wts["Wo"][at].rearrange("l (a k) n -> k (l a) n", k=P)).then_inc(attn_w.sem, 16)
                    sp.dma_start(scales[:], wts["qks"][at].rearrange("l a d -> (l a) d")
                                 .partition_broadcast(P)).then_inc(attn_w.sem, 16)
                    load_hs(l, 0)
                    sp.dma_start(w1[:], wts["W1"][at].rearrange("l k n -> k (l n)")).then_inc(ffn_w.sem, 16)
                    sp.dma_start(w2[:], wts["W2"][at].rearrange("l k a n -> k (l a) n")).then_inc(ffn_w.sem, 16)
                    sp.dma_start(b1[:], wts["b1"][at].rearrange("l k n -> k (l n)")).then_inc(ffn_w.sem, 16)
                    sp.dma_start(gb[:], wts["gb"][at].rearrange("l k n -> k (l n)")).then_inc(ffn_w.sem, 16)

                    def turn(b, ahead, ahead2):
                        i = l * turns + b
                        load_tail(i)
                        load_vw(i, 1)
                        if ahead2:
                            load_hs(l, b + 2)
                        if ahead:
                            load_vw(i + 1, 0)

                    load_hs(l, 1)
                    load_vw(l * turns, 0)
                    with sp.Fori(0, turns - 2) as b:
                        turn(b, True, True)
                    turn(turns - 2, True, False)
                    turn(turns - 1, False, False)
                    with sp.Fori(0, turns) as b:
                        load_fhs(l, b)

            @block.gpsimd
            def _(pool):
                pool.memset(power[:], -0.5).then_inc(init, 1)
                pool.memset(hs[:], 0.0).then_inc(init, 1)
                pool.memset(fhs[:], 0.0).then_inc(init, 1)
                pool.memset(kbd[:], 0.0).then_inc(init, 1)
                pool.memset(vw[:], 0.0).then_inc(init, 1)
                pool.wait_ge(init, 5)
                for half in range(VH):
                    rows = slice(half * 64, half * 64 + 64) if VH == 2 else slice(0, P)
                    pool.memset(vw[rows, :, half, :, HD:VC], 1.0).then_inc(init, 2 // VH)
                pool.wait_ge(init, 7)
                pool.memset(hu[:], 1.0).then_inc(init, 1)
                for s in (sq_ready, rmax_ready, rn_ready, t2_ready, fve_ready, frs_ready):
                    pool.sem_inc(s.sem, s.credit)

                def squares(i, n):
                    hold(pool, copied.sem, copied.done(i, qk[n]), pool_passed)
                    pool.wait_ge(ssq_ready.sem, ssq_ready.done(i, n - 2))
                    pool.tensor_tensor(out=sq[:, n % 2, :], in0=qc[:, n % 4, :], in1=qc[:, n % 4, :], op=ALU.mult)\
                        .then_inc(sq_ready.sem, 1)

                def norms(i, n):
                    hold(pool, ssq_ready.sem, ssq_ready.done(i, n), pool_passed)
                    pool.tensor_scalar(ssq[:, n % 2, :], ssq[:, n % 2, :], 1e-24, None, ALU.max)\
                        .then_inc(rmax_ready.sem, 1)
                    pool.wait_ge(rmax_ready.sem, rmax_ready.done(i, n))
                    pool.tensor_tensor(out=rn[:, n % 2, :], in0=ssq[:, n % 2, :], in1=power[:], op=ALU.pow)\
                        .then_inc(rn_ready.sem, 1)

                def turn_half(i, n):
                    t, what, _ = chunks[qk[n]]
                    pool.wait_ge(sum_ready.sem, sum_ready.done(i, n - 2))
                    row = 1 if what == "q" else 3
                    src, dst = fresh(qc[:, n % 4, :], HD), fresh(t2[:, n % 2, :], HD)
                    for a in range(2):
                        o, s = a * 32, 32 - a * 32
                        last = pool.tensor_tensor(
                            out=dst[:, :, o:o + 32], in0=src[:, :, s:s + 32],
                            in1=table[:, t, row, o:o + 32].unsqueeze(1).to_broadcast([P, 8, 32]), op=ALU.mult)
                    last.then_inc(t2_ready.sem, 1)

                def slot(l, b, u, new, old, ahead):
                    _, _, _, _, projected = steps(l * turns + b, u, new, old, ahead)
                    if projected and qk_of_unit[projected[1]]:
                        i, (q, k) = projected[0], qk_of_unit[projected[1]]
                        squares(i, q)
                        turn_half(i, q)
                        squares(i, k)
                        norms(i, q)
                        turn_half(i, k)
                        norms(i, k)

                def deviation(l, b):
                    i = l * turns + b
                    hold(pool, fmv_ready.sem, fmv_ready.done(i), pool_passed)
                    pool.tensor_scalar(fve[:], fmv[:, :, 1], EPS, None, ALU.add).then_inc(fve_ready.sem, 1)
                    pool.wait_ge(fve_ready.sem, fve_ready.done(i))
                    pool.tensor_tensor(out=frs[:], in0=fve[:], in1=power[:, 0:NT], op=ALU.pow)\
                        .then_inc(frs_ready.sem, 1)

                with pool.Fori(0, depth) as l:
                    pool.wait_ge(table_ready.sem, table_ready.done(l))
                    sweep(pool, l, slot)
                    with pool.Fori(0, turns) as b:
                        deviation(l, b)

            @block.vector
            def _(dve):
                for s in (ssq_ready, sum_ready, t1_ready, qr_ready, mx_ready, sd_ready, rd_ready, on_ready, za_done,
                          zf_done, fst_ready, fmv_ready, fhn_ready, hu_ready, table_ready):
                    dve.sem_inc(s.sem, s.credit)
                dve.wait_ge(const_ld, 32)
                dve.tensor_copy(maskb[:].rearrange("p a b -> p (a b)"), sd[:].rearrange("p a b -> p (a b)"))\
                   .then_inc(mask_ready, 1)
                dve.wait_ge(mask_ready, 1)
                dve.wait_ge(init, NINIT)

                def tables(l):
                    dve.wait_ge(attn_w.sem, attn_w.done(l, 47))
                    dve.wait_ge(t2_ready.sem, t2_ready.prev(l * turns, NQ - 1))
                    for w in range(2):
                        for t in range(NT):
                            last = dve.tensor_tensor(out=table[:, t, 2 * w, :], in0=rope[:, t, 2 * w, :],
                                                     in1=scales[:, w, :], op=ALU.mult)
                            for a in range(2):
                                o, s = a * 32, 32 - a * 32
                                last = dve.tensor_tensor(out=table[:, t, 2 * w + 1, o:o + 32],
                                                         in0=rope[:, t, 2 * w + 1, o:o + 32],
                                                         in1=scales[:, w, s:s + 32], op=ALU.mult)
                    last.then_inc(table_ready.sem, 1)
                    dve.wait_ge(table_ready.sem, table_ready.done(l))

                def squares(i, n):
                    dve.wait_ge(sq_ready.sem, sq_ready.done(i, n))
                    dve.wait_ge(rn_ready.sem, rn_ready.done(i, n - 2))
                    dve.tensor_reduce(ssq[:, n % 2, :], fresh(sq[:, n % 2, :], HD), AX.X, ALU.add)\
                       .then_inc(ssq_ready.sem, 1)

                def straight(i, n):
                    t, what, _ = chunks[qk[n]]
                    dve.wait_ge(copied.sem, copied.done(i, qk[n]))
                    dve.wait_ge(qr_ready.sem, qr_ready.done(i, n - 2))
                    row = 0 if what == "q" else 2
                    dve.tensor_tensor(out=fresh(t1[:, n % 2, :], HD), in0=fresh(qc[:, n % 4, :], HD),
                                      in1=table[:, t, row, :].unsqueeze(1).to_broadcast([P, 8, HD]), op=ALU.mult)\
                       .then_inc(t1_ready.sem, 1)

                def rotated(i, n):
                    dve.wait_ge(t2_ready.sem, t2_ready.done(i, n))
                    dve.wait_ge(t1_ready.sem, t1_ready.done(i, n))
                    dve.tensor_tensor(out=t1[:, n % 2, :], in0=t1[:, n % 2, :], in1=t2[:, n % 2, :], op=ALU.add)\
                       .then_inc(sum_ready.sem, 1)
                    dve.wait_ge(rn_ready.sem, rn_ready.done(i, n))
                    dve.wait_ge(qrT_ps.sem, qrT_ps.done(i, n - 4))
                    dve.wait_ge(sum_ready.sem, sum_ready.done(i, n))
                    dve.tensor_tensor(out=fresh(qr[:, n % 4, :], HD), in0=fresh(t1[:, n % 2, :], HD),
                                      in1=rn[:, n % 2, :].unsqueeze(2).to_broadcast([P, 8, HD]), op=ALU.mult)\
                       .then_inc(qr_ready.sem, 1)

                def softmax(i, u):
                    ps = psum[B_S[u % 2]][:].rearrange("p (a b) -> p a b", b=K2)
                    dve.wait_ge(s_ready.sem, s_ready.done(i, u))
                    dve.tensor_reduce(mx[:, u % 2, :], ps, AX.X, ALU.max).then_inc(mx_ready.sem, 1)
                    dve.wait_ge(mx_ready.sem, mx_ready.done(i, u))
                    dve.wait_ge(p_ready.sem, p_ready.done(i, u - 2) if u >= 2 else p_ready.prev(i, u + 2))
                    dve.tensor_tensor(out=sd[:, u % 2, :].rearrange("p (a b) -> p a b", b=K2), in0=ps,
                                      in1=mx[:, u % 2, :].unsqueeze(2).to_broadcast([P, 2 * NW, K2]),
                                      op=ALU.subtract).then_inc(sd_ready.sem, 1)

                def divided(i, u):
                    dve.wait_ge(oT_ps.sem, oT_ps.done(i, u - 2) if u >= 2 else oT_ps.prev(i, u + 2))
                    for e in range(2):
                        ps = psum[B_O[e]][:, 0:NW * VC].rearrange("p (w v) -> p w v", v=VC)
                        dve.wait_ge(o_ready.sem, o_ready.done(i, 2 * u + e))
                        dve.reciprocal(rd[:, e, :], ps[:, :, HD]).then_inc(rd_ready.sem, 1)
                        dve.wait_ge(rd_ready.sem, rd_ready.done(i, 2 * u + e))
                        dve.tensor_tensor(out=on[:, u % 2, :, e, :], in0=ps[:, :, 0:HD],
                                          in1=rd[:, e, :].unsqueeze(2).to_broadcast([P, NW, HD]), op=ALU.mult)\
                           .then_inc(on_ready.sem, 1)

                def to_stream(b, t, n, bank, ready, value, done):
                    dve.wait_ge(ready.sem, value)
                    zb = z[:, bass.ds(b * NT + t, n), :]
                    dve.tensor_tensor(out=zb, in0=psum[bank][:, 0:n * CH].rearrange("p (t c) -> p t c", c=CH),
                                      in1=zb, op=ALU.add).then_inc(done.sem, 1)

                def slot(l, b, u, new, old, ahead):
                    i = l * turns + b
                    now, before1, _, _, projected = steps(i, u, new, old, ahead)
                    late = ((i, u + 1) if new else None) if u < 3 else ((i + 1, 0) if ahead else None)
                    if now:
                        softmax(*now)
                    if late and qk_of_unit[late[1]]:
                        rotated(late[0], qk_of_unit[late[1]][1])
                    if old and u % 2 == 0:
                        to_stream(b - 1, u // 2, 1, B_PT, y_ready, y_ready.done(i - 1, u // 2), za_done)
                    here = qk_of_unit[projected[1]] if projected else []
                    for n in here:
                        straight(projected[0], n)
                        if n == here[0]:
                            squares(projected[0], n)
                    if before1:
                        divided(*before1)
                    if here:
                        squares(projected[0], here[1])
                        rotated(projected[0], here[0])

                def feed_norm(l, b):
                    i = l * turns + b
                    dve.wait_ge(fhs_ld.sem, fhs_ld.done(i, 47))
                    for t in range(NT):
                        last = dve.bn_stats(fst[:, t, :], fhs[:, t, :])
                    last.then_inc(fst_ready.sem, 1)
                    hold(dve, fst_ready.sem, fst_ready.done(i), dve_passed)
                    for t in range(NT):
                        last = dve.bn_aggr(fmv[:, t, :], fst[:, t, :])
                    last.then_inc(fmv_ready.sem, 1)
                    dve.wait_ge(frs_ready.sem, frs_ready.done(i))
                    dve.wait_ge(fhT_ps.sem, fhT_ps.prev(i))
                    for t in range(NT):
                        last = dve.tensor_scalar(fhn[:, t, :], fhs[:, t, :], fmv[:, t, 0:1], frs[:, t:t + 1],
                                                 ALU.subtract, ALU.mult)
                    last.then_inc(fhn_ready.sem, 1)

                def feed(l, b):
                    i = l * turns + b
                    dve.wait_ge(fy_ready.sem, fy_ready.prev(i))
                    for c in range(HCH):
                        n = P if c < 2 else HLAST
                        dve.wait_ge(gl_ready.sem, gl_ready.done(i, c))
                        dve.scalar_tensor_tensor(out=hu[0:n, c, :], in0=psum[c][0:n, 0:TOK],
                                                 scalar=b1[0:n, c:c + 1], in1=gl[0:n, c, :],
                                                 op0=ALU.add, op1=ALU.mult).then_inc(hu_ready.sem, 1)

                def feed_stream(l, b):
                    i = l * turns + b
                    to_stream(b, 0, NT, 3, fy_ready, fy_ready.done(i), zf_done)

                with dve.Fori(0, depth) as l:
                    tables(l)
                    sweep(dve, l, slot)
                    hold(dve, ffn_w.sem, ffn_w.done(l, 63), dve_passed)
                    feed_norm(l, 0)
                    with dve.Fori(0, turns - 1) as b:
                        feed(l, b)
                        feed_norm(l, b + 1)
                        feed_stream(l, b)
                    feed(l, turns - 1)
                    feed_stream(l, turns - 1)

            @block.scalar
            def _(act):
                for s in (hT_ready, copied, qkT_ready, p_ready, pT_ready, oT_ready, fhT_ready, gl_ready):
                    act.sem_inc(s.sem, s.credit)
                act.wait_ge(init, NINIT)

                def copy_hT(i):
                    act.wait_ge(hT_ps.sem, hT_ps.done(i))
                    act.wait_ge(qkv_ready.sem, qkv_ready.prev(i, NC - 1))
                    act.activation(hT[:], psum[B_T][:, 0:TOK], ACT.Copy).then_inc(hT_ready.sem, 1)

                def copy_chunk(i, c):
                    t, what, j = chunks[c]
                    act.wait_ge(qkv_ready.sem, qkv_ready.done(i, c))
                    if what == "v":
                        act.wait_ge(vw_ld[t].sem, vw_ld[t].prev(i, vw_ld[t].per - 1))
                        if t == 0:
                            act.wait_ge(tail_ld.sem, tail_ld.prev(i, 15))
                        dst = vtok[:, t, j * CW:(j + 1) * CW]
                    else:
                        n = qk.index(c)
                        act.wait_ge(t1_ready.sem, t1_ready.done(i, n - 4))
                        act.wait_ge(t2_ready.sem, t2_ready.done(i, n - 4))
                        dst = qc[:, n % 4, :]
                    act.activation(dst, psum[B_QKV[c % 2]][:], ACT.Copy).then_inc(copied.sem, 1)

                def copy_qk(i, n):
                    t, what, j = chunks[qk[n]]
                    act.wait_ge(qrT_ps.sem, qrT_ps.done(i, n))
                    act.wait_ge(s_ready.sem, s_ready.prev(i, 2 + j if QC == 2 else 3))
                    src = psum[B_T][:].rearrange("p (a b) -> p a b", b=P)
                    pairs = slice(j * PC, (j + 1) * PC)
                    if what == "q":
                        act.activation(qT[:, pairs, t * P:(t + 1) * P], src, ACT.Copy, scale=8.0)\
                           .then_inc(qkT_ready.sem, 1)
                        return
                    at = t * (W + P) + W
                    for e in range(2):
                        rows = slice(e * 64, e * 64 + 64)
                        last = act.activation(kbd[rows, pairs, e, at:at + P], src[rows], ACT.Copy)
                        if t == 0:
                            last = act.activation(kbd[rows, pairs, e, at + P:at + P + W], src[rows, :, P - W:P], ACT.Copy)
                    last.then_inc(qkT_ready.sem, 1)

                def exponentials(i, u):
                    act.wait_ge(sd_ready.sem, sd_ready.done(i, u))
                    act.wait_ge(pT_ps.sem, pT_ps.done(i, u - 2) if u >= 2 else pT_ps.prev(i, u + 2))
                    act.activation(pr[:, u % 2, :].rearrange("p (e w k) -> p w e k", e=2, w=NW),
                                   sd[:, u % 2, :].rearrange("p (w e k) -> p w e k", e=2, w=NW), ACT.Exp)\
                       .then_inc(p_ready.sem, 1)

                def copy_pT(i, u):
                    act.wait_ge(pT_ps.sem, pT_ps.done(i, u))
                    act.wait_ge(o_ready.sem, o_ready.done(i, 2 * u - 3) if u >= 2 else o_ready.prev(i, 2 * u + 5))
                    act.activation(pT[:, u % 2, :], psum[B_PT][:], ACT.Copy).then_inc(pT_ready.sem, 1)

                def copy_oT(i, u):
                    k, r = u // 2, u % 2
                    act.wait_ge(oT_ps.sem, oT_ps.done(i, u))
                    act.wait_ge(y_ready.sem, y_ready.prev(i, k))
                    act.activation(oT[:, r * G:(r + 1) * G, k * P:(k + 1) * P].rearrange("p j (w q) -> p w j q", q=W),
                                   psum[B_PT][:, 0:NW * P].rearrange("p (w j q) -> p w j q", w=NW, q=W),
                                   ACT.Copy).then_inc(oT_ready.sem, 1)

                def slot(l, b, u, new, old, ahead):
                    i = l * turns + b
                    now, before1, before2, turned, projected = steps(i, u, new, old, ahead)
                    if u == 2 and ahead:
                        copy_hT(i + 1)
                    t = list(qk_of_unit[turned[1]]) if turned else []
                    c = list(of_unit[projected[1]]) if projected else []
                    if t:
                        copy_qk(turned[0], t[0])
                    if c:
                        copy_chunk(projected[0], c[0])
                    if before1:
                        copy_pT(*before1)
                    if len(c) > 1:
                        copy_chunk(projected[0], c[1])
                    if now:
                        exponentials(*now)
                    if t:
                        copy_qk(turned[0], t[1])
                    if len(c) > 2:
                        copy_chunk(projected[0], c[2])
                    if before2:
                        copy_oT(*before2)

                def copy_fhT(l, b):
                    i = l * turns + b
                    act.wait_ge(fhT_ps.sem, fhT_ps.done(i))
                    act.wait_ge(g_ready.sem, g_ready.prev(i, HCH - 1))
                    act.activation(fhT[:], psum[B_T][:, 0:TOK], ACT.Identity, bias=gb[:, 1:2], scale=gb[:, 0:1])\
                       .then_inc(fhT_ready.sem, 1)

                def gates(l, b):
                    i = l * turns + b
                    for c in range(HCH):
                        n = P if c < 2 else HLAST
                        act.wait_ge(g_ready.sem, g_ready.done(i, c))
                        act.wait_ge(hu_ready.sem, hu_ready.prev(i, c))
                        act.activation(gl[0:n, c, :], psum[c][0:n, TOK:2 * TOK], ACT.Gelu,
                                       bias=b1[0:n, HCH + c:HCH + c + 1]).then_inc(gl_ready.sem, 1)

                with act.Fori(0, depth) as l:
                    sweep(act, l, slot)
                    act.wait_ge(ffn_w.sem, ffn_w.done(l, 63))
                    copy_fhT(l, 0)
                    with act.Fori(0, turns - 1) as b:
                        gates(l, b)
                        copy_fhT(l, b + 1)
                    gates(l, turns - 1)

            @block.tensor
            def _(pe):
                for s in (hT_ps, qkv_ready, qrT_ps, s_ready, pT_ps, o_ready, oT_ps, y_ready, fhT_ps, g_ready, fy_ready):
                    pe.sem_inc(s.sem, s.credit)
                pe.wait_ge(mask_ready, 1)
                pe.wait_ge(init, NINIT)

                def turn_h(i, free):
                    pe.wait_ge(hs_ld.sem, hs_ld.done(i, 47))
                    pe.wait_ge(*free)
                    for t in range(NT):
                        last = pe.transpose(psum[B_T][:, t * P:(t + 1) * P], hs[:, t, :], ident[:])
                    last.then_inc(hT_ps.sem, 1)

                def chunk(i, c):
                    t, what, j = chunks[c]
                    if c == 0:
                        pe.wait_ge(hT_ready.sem, hT_ready.done(i))
                    pe.wait_ge(copied.sem, copied.done(i, c - 2))
                    col = {"q": 0, "k": INNER, "v": 2 * INNER}[what] + j * CW
                    pe.matmul(psum[B_QKV[c % 2]][:], hT[:, t * P:(t + 1) * P], wqkv[:, col:col + CW],
                              start=True, stop=True).then_inc(qkv_ready.sem, 1)

                def turn_qk(i, n, held):
                    pe.wait_ge(qr_ready.sem, qr_ready.done(i, n))
                    pe.wait_ge(qkT_ready.sem, qkT_ready.done(i, n - 1))
                    if held is not None:
                        pe.wait_ge(hT_ready.sem, hT_ready.done(held))
                    for p in range(PC):
                        last = pe.transpose(psum[B_T][:, p * P:(p + 1) * P], qr[:, n % 4, p * P:(p + 1) * P], ident[:])
                    last.then_inc(qrT_ps.sem, 1)

                def scores(i, u):
                    k = u // 2
                    ps = psum[B_S[u % 2]]
                    pe.wait_ge(qkT_ready.sem, qkT_ready.done(i, needed[u]))
                    pe.wait_ge(sd_ready.sem, sd_ready.done(i, u - 2) if u >= 2 else sd_ready.prev(i, u + 2))
                    pe.matmul(ps[:], identb[:], maskb[:, k, :], start=True, stop=True)
                    psv = ps[:].rearrange("p (w e k) -> p w e k", w=NW, e=2)
                    for w in range(NW):
                        col, key = (k * NW + w) * W, k * (W + P) + w * W
                        for j, pair in enumerate(unit_pairs(u)):
                            last = pe.matmul(psv[j * W:(j + 1) * W, w], qT[:, pair, col:col + W],
                                             kbd[:, pair, :, key:key + K2], start=False,
                                             stop=True, skip_group_check=True)
                    last.then_inc(s_ready.sem, 1)

                def turn_p(i, u, y):
                    pe.wait_ge(p_ready.sem, p_ready.done(i, u))
                    pe.wait_ge(oT_ready.sem, oT_ready.done(i, u - 2))
                    if y is not None:
                        pe.wait_ge(za_done.sem, za_done.done(*y))
                    for n in range(4):
                        last = pe.transpose(psum[B_PT][:, n * P:(n + 1) * P], pr[:, u % 2, n * P:(n + 1) * P], ident[:])
                    last.then_inc(pT_ps.sem, 1)

                def values(i, u):
                    k = u // 2
                    pe.wait_ge(pT_ready.sem, pT_ready.done(i, u))
                    pe.wait_ge(vw_ld[k].sem, vw_ld[k].done(i, vw_ld[k].per - 1))
                    if k == 1:
                        pe.wait_ge(tail_ld.sem, tail_ld.done(i, 15))
                    for e in range(2):
                        m = 2 * u + e
                        pe.wait_ge(on_ready.sem, on_ready.done(i, m - 2) if m >= 2 else on_ready.prev(i, m + 6))
                        for blk in range(BP):
                            for j, pair in enumerate(unit_pairs(u)):
                                c0 = blk * WB * VC
                                lhs = pT[:, u % 2, (e * BP + blk) * P + j * W:(e * BP + blk) * P + (j + 1) * W]
                                last = pe.matmul(
                                    psum[B_O[e]][j * W:(j + 1) * W, c0:c0 + WB * VC]
                                    .rearrange("p (a v) -> p a v", v=VC), lhs,
                                    vw[:, k * BP + blk, :, 2 * pair + e, :],
                                    start=True, stop=True, skip_group_check=True)
                        last.then_inc(o_ready.sem, 1)

                def turn_o(i, u, free):
                    pe.wait_ge(on_ready.sem, on_ready.done(i, 2 * u + 1))
                    pe.wait_ge(*free)
                    for w in range(NW):
                        last = pe.transpose(psum[B_PT][:, w * P:(w + 1) * P],
                                            on[:, u % 2, w].rearrange("p e d -> p (e d)"), ident[:])
                    last.then_inc(oT_ps.sem, 1)

                def out_project(i, t):
                    pe.wait_ge(oT_ready.sem, oT_ready.done(i, 2 * t + 1))
                    for pair in range(NP):
                        last = pe.matmul(psum[B_PT][:, 0:CH], oT[:, pair, t * P:(t + 1) * P],
                                         wo[:, pair, :], start=(pair == 0), stop=(pair == NP - 1))
                    last.then_inc(y_ready.sem, 1)

                def slot(l, b, u, new, old, ahead):
                    i = l * turns + b
                    now, before1, before2, turned, projected = steps(i, u, new, old, ahead)
                    if now:
                        scores(*now)
                    y = (i - 1, u // 2) if old and u % 2 == 0 else None
                    if y:
                        out_project(*y)
                    t = list(qk_of_unit[turned[1]]) if turned else []
                    c = list(of_unit[projected[1]]) if projected else []
                    if t:
                        turn_qk(turned[0], t[0], i + 1 if u >= 2 and ahead else None)
                    if c:
                        chunk(projected[0], c[0])
                    if before1:
                        turn_p(*before1, y)
                    if len(c) > 1:
                        chunk(projected[0], c[1])
                    if t:
                        turn_qk(turned[0], t[1], None)
                    if before1:
                        values(*before1)
                    if len(c) > 2:
                        chunk(projected[0], c[2])
                    if before2:
                        turn_o(*before2, (pT_ready.sem, pT_ready.done(*before1)) if before1 else
                               (oT_ready.sem, oT_ready.done(before2[0], before2[1] - 1)))
                    if u == 1 and ahead:
                        turn_h(i + 1, (qkT_ready.sem, qkT_ready.done(i, qk_of_unit[2][1])))

                def turn_f(l, b):
                    i = l * turns + b
                    pe.wait_ge(fhn_ready.sem, fhn_ready.done(i))
                    pe.wait_ge(fhT_ready.sem, fhT_ready.prev(i))
                    for t in range(NT):
                        last = pe.transpose(psum[B_T][:, t * P:(t + 1) * P], fhn[:, t, :], ident[:])
                    last.then_inc(fhT_ps.sem, 1)

                def hidden(l, b):
                    i = l * turns + b
                    pe.wait_ge(fhT_ready.sem, fhT_ready.done(i))
                    for c in range(HCH):
                        n = P if c < 2 else HLAST
                        pe.wait_ge(hu_ready.sem, hu_ready.prev(i, c))
                        for a in range(2):
                            last = pe.matmul(psum[c][0:n, a * TOK:(a + 1) * TOK],
                                             w1[:, a * HID + c * P:a * HID + c * P + n], fhT[:],
                                             start=True, stop=True)
                        last.then_inc(g_ready.sem, 1)

                def down(l, b):
                    i = l * turns + b
                    pe.wait_ge(hu_ready.sem, hu_ready.done(i, HCH - 1))
                    pe.wait_ge(zf_done.sem, i + turns)
                    for t in range(NT):
                        for c in range(HCH):
                            n = P if c < 2 else HLAST + 1
                            last = pe.matmul(psum[3][:, t * CH:(t + 1) * CH], hu[0:n, c, t * P:(t + 1) * P],
                                             w2[0:n, c, :], start=(c == 0), stop=(c == HCH - 1))
                    last.then_inc(fy_ready.sem, 1)

                with pe.Fori(0, depth) as l:
                    pe.wait_ge(zf_done.sem, l * turns + turns)
                    pe.wait_ge(attn_w.sem, attn_w.done(l, 47))
                    sweep(pe, l, slot)
                    pe.wait_ge(za_done.sem, za_done.done(l * turns + turns - 1, NT - 1))
                    pe.wait_ge(ffn_w.sem, ffn_w.done(l, 63))
                    turn_f(l, 0)
                    with pe.Fori(0, turns - 1) as b:
                        hidden(l, b)
                        turn_f(l, b + 1)
                        down(l, b)
                    hidden(l, turns - 1)
                    down(l, turns - 1)


def grouped_attention(nc, name, x, zT, wts, scratch, ident, psum):
    NI = 16
    ROWS = 256
    GR = 16
    GD = 8
    SCALE = float(np.float32(1.0) / np.float32(np.sqrt(CH)))
    B_S, B_PT, B_O, B_OT, B_Q, B_V = (0, 1), (2, 3), 4, 5, 6, 7

    with ExitStack() as ctx:
        def sb(n, shape, dt=F32):
            return ctx.enter_context(nc.sbuf_tensor(f"{name}_{n}", shape, dt))

        def sem(n):
            return ctx.enter_context(nc.semaphore(f"{name}_{n}"))

        wq = sb("wq", [P, GR, P])
        bq = sb("bq", [P, GR])
        wu = sb("wu", [P, CH])
        bu = sb("bu", [1, CH])
        ones = sb("ones", [1, P])
        qT = sb("qT", [P, 2, NI * ROWS])
        v = sb("v", [P, 2, NI * 2, 32])
        mxr = sb("mxr", [P, 2, 2])
        nmx = sb("nmx", [P, 2, 2])
        pr = sb("pr", [P, 2, 2, ROWS])
        pT = sb("pT", [P, 2, 2, ROWS])
        ob = sb("ob", [P, 2, ROWS])
        rd = sb("rd", [P, 2, 4])
        on = sb("on", [P, 2, NI, 2, GD])
        ot = sb("ot", [P, NT, CH])
        oT = sb("oT", [P, TOK])

        w_ld, init = sem("w_ld"), sem("init")
        q_ps = Count(sem("q_ps"), GR // 2)
        q_ready = Count(sem("q"), GR // 2)
        v_ps = Count(sem("v_ps"), 1)
        v_ready = Count(sem("v"), 1)
        s_ready = Count(sem("s"), NI)
        mxr_ready = Count(sem("mxr"), NI)
        nmx_ready = Count(sem("nmx"), NI)
        p_ready = Count(sem("p"), NI)
        pT_ps = Count(sem("pT_ps"), NI)
        pT_ready = Count(sem("pT"), NI)
        o_ready = Count(sem("o"), NI)
        ob_ready = Count(sem("ob"), 4)
        ot_ps = Count(sem("ot_ps"), 4)
        rd_ready = Count(sem("rd"), 4)
        on_ready = Count(sem("on"), 4)
        stored = Count(sem("stored"), 16)
        loaded = Count(sem("loaded"), 16)
        oT_ps = Count(sem("oT_ps"), 1)
        oT_ready = Count(sem("oT"), 1)
        y_ready = Count(sem("y"), 1)
        x_done = Count(sem("x"), 1)
        pe_passed, sp_passed = sem("pe_passed"), sem("sp_passed")

        def rounds(eng, project, turn, close):
            project(0, 0)
            turn(0, 0, True, False)
            with eng.Fori(0, (SEQ - 2) // 2) as j:
                turn(j * 2 + 1, 1, True, True)
                turn(j * 2 + 2, 0, True, True)
            turn(SEQ - 1, 1, False, True)
            close(SEQ - 1)

        with nc.Block() as block:
            @block.sync
            def _(sp):
                sp.sem_inc(stored.sem, stored.credit)
                sp.sem_inc(loaded.sem, loaded.credit)
                for dst, n in ((wq, "wq"), (bq, "bq"), (wu, "wu"), (bu, "bu")):
                    sp.dma_start(dst[:], wts[n]).then_inc(w_ld, 16)

                def turn(b, par, *_):
                    sp.wait_ge(on_ready.sem, on_ready.done(b, 3))
                    sp.dma_start(scratch[bass.ds(b, 1)].rearrange("a (n p d) -> p (a n) d", p=P, d=GD),
                                 on[:, par].rearrange("p n h d -> p (n h) d")).then_inc(stored.sem, 16)
                    hold(sp, stored.sem, stored.done(b, 15), sp_passed)
                    hold(sp, oT_ps.sem, oT_ps.prev(b), sp_passed)
                    sp.dma_start(ot[:], scratch[bass.ds(b, 1)].rearrange("a (t p c) -> p (a t) c", p=P, c=CH))\
                      .then_inc(loaded.sem, 16)

                with sp.Fori(0, SEQ // 2) as j:
                    turn(j * 2, 0)
                    turn(j * 2 + 1, 1)

            @block.gpsimd
            def _(pool):
                pool.memset(v[:], 0.0).then_inc(init, 1)
                pool.memset(ones[:], 1.0).then_inc(init, 1)
                pool.wait_ge(init, 2)
                pool.memset(v[:, :, :, GD:GD + 1], 1.0).then_inc(init, 1)

            @block.tensor
            def _(pe):
                for s in (q_ps, v_ps, s_ready, pT_ps, o_ready, ot_ps, oT_ps, y_ready):
                    pe.sem_inc(s.sem, s.credit)
                pe.wait_ge(w_ld, 64)
                pe.wait_ge(init, 3)

                def groups(b, m):
                    pe.wait_ge(q_ready.sem, q_ready.done(b, m - 1) if m else q_ready.prev(b, GR // 2 - 1))
                    for a in range(2):
                        last = pe.matmul(psum[B_Q][:, a * TOK:(a + 1) * TOK], wq[:, 2 * m + a, :],
                                         zT[:, bass.ds(b * TOK, TOK)], start=True, stop=True)
                    last.then_inc(q_ps.sem, 1)

                def turn_v(b, par, free):
                    pe.wait_ge(q_ready.sem, q_ready.done(b, GR // 2 - 1))
                    hold(pe, *free, pe_passed)
                    for n in range(2 * NI):
                        last = pe.transpose(psum[B_V][:, n * GD:(n + 1) * GD], qT[0:GD, par, n * P:(n + 1) * P],
                                            ident[0:GD, 0:GD])
                    last.then_inc(v_ps.sem, 1)

                def scores(b, par, n):
                    if n == 0:
                        pe.wait_ge(q_ready.sem, q_ready.done(b, GR // 2 - 1))
                    pe.wait_ge(p_ready.sem, p_ready.done(b, n - 2) if n >= 2 else p_ready.prev(b, NI - 2 + n))
                    for h in range(2):
                        last = pe.matmul(psum[B_S[n % 2]][:, h * ROWS:(h + 1) * ROWS],
                                         qT[:, par, n * ROWS + h * P:n * ROWS + (h + 1) * P],
                                         qT[:, par, n * ROWS:(n + 1) * ROWS], start=True, stop=True)
                    last.then_inc(s_ready.sem, 1)

                def turn_p(b, n):
                    pe.wait_ge(p_ready.sem, p_ready.done(b, n))
                    pe.wait_ge(pT_ready.sem, pT_ready.done(b, n - 2) if n >= 2 else pT_ready.prev(b, NI - 2 + n))
                    for kh in range(2):
                        for qh in range(2):
                            last = pe.transpose(psum[B_PT[n % 2]][:, kh * ROWS + qh * P:kh * ROWS + (qh + 1) * P],
                                                pr[:, n % 2, qh, kh * P:(kh + 1) * P], ident[:])
                    last.then_inc(pT_ps.sem, 1)

                def values(b, par, n):
                    c = n % 4
                    pe.wait_ge(pT_ready.sem, pT_ready.done(b, n))
                    if n == 0:
                        pe.wait_ge(v_ready.sem, v_ready.done(b))
                    if c == 0:
                        pe.wait_ge(ob_ready.sem, ob_ready.done(b, n // 4 - 1) if n else ob_ready.prev(b, 3))
                    for kh in range(2):
                        last = pe.matmul(psum[B_O][32 * c:32 * c + 32, 0:ROWS],
                                         v[:, par, 2 * n + kh, :], pT[:, n % 2, kh, :],
                                         start=(kh == 0), stop=(kh == 1))
                    last.then_inc(o_ready.sem, 1)

                def turn_o(b, q):
                    pe.wait_ge(ob_ready.sem, ob_ready.done(b, q))
                    pe.wait_ge(on_ready.sem, on_ready.done(b, q - 1) if q else on_ready.prev(b, 3))
                    for h in range(2):
                        last = pe.transpose(psum[B_OT][:, h * P:(h + 1) * P], ob[:, q % 2, h * P:(h + 1) * P], ident[:])
                    last.then_inc(ot_ps.sem, 1)

                def close_turn(b, v_value):
                    pe.wait_ge(loaded.sem, loaded.done(b, 15))
                    pe.wait_ge(v_ready.sem, v_value)
                    for t in range(NT):
                        last = pe.transpose(psum[B_V][:, t * P:(t + 1) * P], ot[:, t, :], ident[:])
                    last.then_inc(oT_ps.sem, 1)

                def close_project(b):
                    pe.wait_ge(oT_ready.sem, oT_ready.done(b))
                    for t in range(NT):
                        pe.matmul(psum[B_V][:, TOK + t * CH:TOK + (t + 1) * CH], ones[:], bu[:], start=True, stop=False)
                        last = pe.matmul(psum[B_V][:, TOK + t * CH:TOK + (t + 1) * CH], oT[:, t * P:(t + 1) * P], wu[:],
                                         start=False, stop=True)
                    last.then_inc(y_ready.sem, 1)

                def project(b, par):
                    for m in range(GR // 2):
                        groups(b, m)
                    turn_v(b, par, (v_ready.sem, v_ready.prev(b)))

                def turn(b, par, ahead, behind):
                    scores(b, par, 0)
                    for n in range(NI):
                        if n + 1 < NI:
                            scores(b, par, n + 1)
                        if ahead and n % 2:
                            groups(b + 1, n // 2)
                        turn_p(b, n)
                        if n >= 1:
                            values(b, par, n - 1)
                        if n >= 5 and n % 4 == 1:
                            turn_o(b, (n - 5) // 4)
                        if behind and n == 8:
                            close_turn(b - 1, v_ready.done(b))
                        if behind and n == 10:
                            close_project(b - 1)
                    values(b, par, NI - 1)
                    if ahead:
                        turn_v(b + 1, 1 - par, (x_done.sem, x_done.prev(b)))
                    turn_o(b, 3)

                def close(b):
                    close_turn(b, v_ready.done(b))
                    close_project(b)

                rounds(pe, project, turn, close)

            @block.vector
            def _(dve):
                for s in (q_ready, v_ready, mxr_ready, nmx_ready, pT_ready, rd_ready, on_ready, x_done):
                    dve.sem_inc(s.sem, s.credit)
                dve.wait_ge(w_ld, 64)
                dve.wait_ge(init, 3)

                def groups(b, par, m):
                    dve.wait_ge(q_ps.sem, q_ps.done(b, m))
                    for g in (2 * m, 2 * m + 1):
                        last = dve.tensor_scalar(qT[:, par, :].rearrange("p (t g) -> p g t", g=GR)[:, g],
                                                 psum[B_Q][:, (g % 2) * TOK:(g % 2 + 1) * TOK], bq[:, g:g + 1], None,
                                                 ALU.add)
                    last.then_inc(q_ready.sem, 1)

                def copy_v(b, par):
                    dve.wait_ge(v_ps.sem, v_ps.done(b))
                    dve.tensor_copy(v[:, par, :, 0:GD], psum[B_V][:, 0:2 * NI * GD].rearrange("p (n d) -> p n d", d=GD))\
                       .then_inc(v_ready.sem, 1)

                def row_max(b, n):
                    dve.wait_ge(s_ready.sem, s_ready.done(b, n))
                    dve.tensor_reduce(mxr[:, n % 2, :], psum[B_S[n % 2]][:].rearrange("p (h k) -> p h k", h=2),
                                      AX.X, ALU.max).then_inc(mxr_ready.sem, 1)
                    dve.wait_ge(mxr_ready.sem, mxr_ready.done(b, n))
                    dve.wait_ge(p_ready.sem, p_ready.done(b, n - 2) if n >= 2 else p_ready.prev(b, NI - 2 + n))
                    dve.tensor_scalar(nmx[:, n % 2, :], mxr[:, n % 2, :], -SCALE, None, ALU.mult)\
                       .then_inc(nmx_ready.sem, 1)

                def copy_pT(b, n):
                    dve.wait_ge(pT_ps.sem, pT_ps.done(b, n))
                    dve.wait_ge(o_ready.sem, o_ready.done(b, n - 2) if n >= 2 else o_ready.prev(b, NI - 2 + n))
                    dve.tensor_copy(pT[:, n % 2].rearrange("p h k -> p (h k)"), psum[B_PT[n % 2]][:])\
                       .then_inc(pT_ready.sem, 1)

                def divide(b, par, q):
                    ps = psum[B_OT][:, 0:2 * P].rearrange("p (h c r) -> p h c r", h=2, c=4)
                    dve.wait_ge(ot_ps.sem, ot_ps.done(b, q))
                    dve.reciprocal(rd[:], ps[:, :, :, GD]).then_inc(rd_ready.sem, 1)
                    dve.wait_ge(rd_ready.sem, rd_ready.done(b, q))
                    dve.wait_ge(loaded.sem, loaded.prev(b, 15))
                    for h in range(2):
                        last = dve.tensor_tensor(out=on[:, par, 4 * q:4 * q + 4, h, :], in0=ps[:, h, :, 0:GD],
                                                 in1=rd[:, h, :].unsqueeze(2).to_broadcast([P, 4, GD]), op=ALU.mult)
                    last.then_inc(on_ready.sem, 1)

                def close(b):
                    dve.wait_ge(y_ready.sem, y_ready.done(b))
                    xb = x[:, bass.ds(b * NT, NT), :]
                    dve.tensor_tensor(out=xb, in0=psum[B_V][:, TOK:2 * TOK].rearrange("p (t c) -> p t c", c=CH), in1=xb,
                                      op=ALU.add).then_inc(x_done.sem, 1)

                def project(b, par):
                    for m in range(GR // 2):
                        groups(b, par, m)
                    copy_v(b, par)

                def turn(b, par, ahead, behind):
                    row_max(b, 0)
                    for n in range(NI):
                        if n + 1 < NI:
                            row_max(b, n + 1)
                        if ahead and n % 2:
                            groups(b + 1, 1 - par, n // 2)
                        copy_pT(b, n)
                        if n >= 5 and n % 4 == 1:
                            divide(b, par, (n - 5) // 4)
                        if behind and n == 11:
                            close(b - 1)
                    if ahead:
                        copy_v(b + 1, 1 - par)
                    divide(b, par, 3)

                rounds(dve, project, turn, close)

            @block.scalar
            def _(act):
                for s in (p_ready, ob_ready, oT_ready):
                    act.sem_inc(s.sem, s.credit)

                def exponentials(b, n):
                    act.wait_ge(nmx_ready.sem, nmx_ready.done(b, n))
                    act.wait_ge(pT_ps.sem, pT_ps.done(b, n - 2) if n >= 2 else pT_ps.prev(b, NI - 2 + n))
                    for h in range(2):
                        last = act.activation(pr[:, n % 2, h, :], psum[B_S[n % 2]][:, h * ROWS:(h + 1) * ROWS], ACT.Exp,
                                              bias=nmx[:, n % 2, h:h + 1], scale=SCALE)
                    last.then_inc(p_ready.sem, 1)

                def copy_o(b, q):
                    act.wait_ge(o_ready.sem, o_ready.done(b, 4 * q + 3))
                    act.wait_ge(ot_ps.sem, ot_ps.done(b, q - 2) if q >= 2 else ot_ps.prev(b, q + 2))
                    act.activation(ob[:, q % 2, :], psum[B_O][:, 0:ROWS], ACT.Copy)\
                       .then_inc(ob_ready.sem, 1)

                def close(b):
                    act.wait_ge(oT_ps.sem, oT_ps.done(b))
                    act.wait_ge(y_ready.sem, y_ready.prev(b))
                    act.activation(oT[:], psum[B_V][:, 0:TOK], ACT.Copy).then_inc(oT_ready.sem, 1)

                def turn(b, par, ahead, behind):
                    exponentials(b, 0)
                    for n in range(NI):
                        if n + 1 < NI:
                            exponentials(b, n + 1)
                        if n >= 4 and n % 4 == 0:
                            copy_o(b, n // 4 - 1)
                        if behind and n == 9:
                            close(b - 1)
                    copy_o(b, 3)

                rounds(act, lambda b, par: None, turn, close)


def gated_feed(nc, name, x, zT, wts, psum):
    CK, HC = 512, 3
    TURNS = SEQ * TOK // CK
    NTILE = CK // P
    B_G, B_U, B_Y = (0, 1, 2), (3, 4, 5), 6
    with ExitStack() as ctx:
        def sb(n, shape, dt=F32):
            return ctx.enter_context(nc.sbuf_tensor(f"{name}_{n}", shape, dt))

        def sem(n):
            return ctx.enter_context(nc.semaphore(f"{name}_{n}"))

        wi = sb("wi", [P, 3, HC * P], I32)
        wf = sb("wf", [P, 3, HC * P])
        sg = sb("sg", [P, HC, CK])
        h = sb("h", [P, HC, CK])
        w_ld, wf_ready = sem("w_ld"), sem("wf")
        g_ready = Count(sem("g"), HC)
        sg_ready = Count(sem("sg"), HC)
        h_ready = Count(sem("h"), HC)
        y_ready = Count(sem("y"), 1)
        x_done = Count(sem("x"), 1)

        def rounds(eng, up, down):
            for c in range(HC):
                up(0, c)
            with eng.Fori(0, TURNS - 1) as j:
                up(j + 1, 0)
                down(j)
                for c in range(1, HC):
                    up(j + 1, c)
            down(TURNS - 1)

        with nc.Block() as block:
            @block.sync
            def _(sp):
                for n in range(3):
                    sp.dma_start(wi[:, n, :], wts[("w_gate", "w_up", "w_down")[n]]).then_inc(w_ld, 16)

            @block.tensor
            def _(pe):
                for s in (g_ready, y_ready):
                    pe.sem_inc(s.sem, s.credit)
                pe.wait_ge(wf_ready, 1)

                def up(j, c):
                    pe.wait_ge(h_ready.sem, h_ready.prev(j, c))
                    for n, bank in ((0, B_G[c]), (1, B_U[c])):
                        last = pe.matmul(psum[bank][:], wf[:, n, c * P:(c + 1) * P], zT[:, bass.ds(j * CK, CK)],
                                         start=True, stop=True)
                    last.then_inc(g_ready.sem, 1)

                def down(j):
                    pe.wait_ge(h_ready.sem, h_ready.done(j, HC - 1))
                    pe.wait_ge(x_done.sem, x_done.prev(j))
                    for t in range(NTILE):
                        for c in range(HC):
                            last = pe.matmul(psum[B_Y][:, t * CH:(t + 1) * CH], h[:, c, t * P:(t + 1) * P],
                                             wf[:, 2, c * P:(c + 1) * P], start=(c == 0), stop=(c == HC - 1))
                    last.then_inc(y_ready.sem, 1)

                rounds(pe, up, down)

            @block.scalar
            def _(act):
                act.sem_inc(sg_ready.sem, sg_ready.credit)

                def up(j, c):
                    act.wait_ge(g_ready.sem, g_ready.done(j, c))
                    act.wait_ge(h_ready.sem, h_ready.prev(j, c))
                    act.activation(sg[:, c, :], psum[B_G[c]][:], ACT.Silu).then_inc(sg_ready.sem, 1)

                rounds(act, up, lambda j: None)

            @block.vector
            def _(dve):
                for s in (h_ready, x_done):
                    dve.sem_inc(s.sem, s.credit)
                dve.wait_ge(w_ld, 48)
                dve.tensor_scalar(wf[:].rearrange("p a b -> p (a b)"), wi[:].rearrange("p a b -> p (a b)"),
                                  float(np.float32(1.0 / 127.0)), None, ALU.mult).then_inc(wf_ready, 1)

                def up(j, c):
                    dve.wait_ge(sg_ready.sem, sg_ready.done(j, c))
                    dve.wait_ge(y_ready.sem, y_ready.prev(j))
                    dve.tensor_tensor(out=h[:, c, :], in0=psum[B_U[c]][:], in1=sg[:, c, :], op=ALU.mult)\
                       .then_inc(h_ready.sem, 1)

                def down(j):
                    dve.wait_ge(y_ready.sem, y_ready.done(j))
                    xb = x[:, bass.ds(j * NTILE, NTILE), :]
                    dve.tensor_tensor(out=xb, in0=psum[B_Y][:].rearrange("p (t c) -> p t c", c=CH), in1=xb, op=ALU.add)\
                       .then_inc(x_done.sem, 1)

                rounds(dve, up, down)


def chunk_attention(nc, name, x, zT, wts, ident, psum):
    H, D, CK = 16, 8, 64
    NCK = TOK // CK
    NG8 = NT * 2 * H
    VD = D + 1
    SCALE = float(np.float32(1.0 / np.sqrt(D)))
    B_QK, B_T, B_V, B_S, B_PT, B_O, B_Y = 0, 1, 2, (3, 4), 5, 6, 7
    with ExitStack() as ctx:
        def sb(n, shape, dt=F32):
            return ctx.enter_context(nc.sbuf_tensor(f"{name}_{n}", shape, dt))

        def sem(n):
            return ctx.enter_context(nc.semaphore(f"{name}_{n}"))

        wa = sb("wa", [P, 3 * CH])
        wp = sb("wp", [P, CH])
        rope = sb("rope", [P, 2, D])
        headmask = sb("headmask", [P, H])
        zs = sb("zs", [P, TOK])
        zd = sb("zd", [P, NCK, 2, CK])
        qk = sb("qk", [P, 2, NG8, D])
        qkr = sb("qkr", [P, NT, 2, CH])
        qT = sb("qT", [P, TOK])
        kbd = sb("kbd", [P, NCK, H, CK])
        vbd = sb("vbd", [P, NCK, H // 2, 2, VD])
        mx = sb("mx", [P, 2, 8])
        sd = sb("sd", [P, 2, 512])
        pr = sb("pr", [P, 2, 512])
        pT = sb("pT", [P, 2, 4, P])
        rd = sb("rd", [P, 8])
        on = sb("on", [P, NT, H, D])
        oT = sb("oT", [P, TOK])

        w_ld, init = sem("w_ld"), sem("init")
        zs_ready = Count(sem("zs"), 1)
        qk_ps = Count(sem("qk_ps"), 1)
        rot_ready = Count(sem("rot"), 1)
        qkr_ready = Count(sem("qkr"), 1)
        qkT_ps = Count(sem("qkT_ps"), 1)
        qT_ready = Count(sem("qT"), 1)
        kbd_ready = Count(sem("kbd"), 1)
        v_ps = Count(sem("v_ps"), 1)
        vbd_ready = Count(sem("vbd"), 1)
        s_ready = Count(sem("s"), 4)
        mx_ready = Count(sem("mx"), 4)
        sd_ready = Count(sem("sd"), 4)
        p_ready = Count(sem("p"), 4)
        pT_ps = Count(sem("pT_ps"), 4)
        pT_ready = Count(sem("pT"), 4)
        o_ready = Count(sem("o"), 4)
        rd_ready = Count(sem("rd"), 4)
        on_ready = Count(sem("on"), 4)
        oT_ps = Count(sem("oT_ps"), 1)
        oT_ready = Count(sem("oT"), 1)
        y_ready = Count(sem("y"), 1)
        x_done = Count(sem("x"), 1)
        dve_passed, act_passed, pe_passed = sem("dve_passed"), sem("act_passed"), sem("pe_passed")

        def rounds(eng, project, project_end, unit, close):
            project(0)
            project_end(0)
            with eng.Fori(0, SEQ - 1) as b:
                unit(b, 0)
                project(b + 1)
                for u in range(1, 4):
                    unit(b, u)
                project_end(b + 1)
                close(b)
            for u in range(4):
                unit(SEQ - 1, u)
            close(SEQ - 1)

        with nc.Block() as block:
            @block.sync
            def _(sp):
                for dst, n in ((wa, "w_attn"), (wp, "w_proj"), (rope, "rope"), (headmask, "headmask")):
                    sp.dma_start(dst[:], wts[n]).then_inc(w_ld, 16)

            @block.gpsimd
            def _(pool):
                pool.memset(vbd[:], 0.0).then_inc(init, 1)
                pool.wait_ge(init, 1)
                for e in range(2):
                    pool.memset(vbd[e * CK:(e + 1) * CK, :, :, e, D:VD], 1.0).then_inc(init, 1)

            @block.tensor
            def _(pe):
                for s in (qk_ps, qkT_ps, v_ps, s_ready, pT_ps, o_ready, oT_ps, y_ready):
                    pe.sem_inc(s.sem, s.credit)
                pe.wait_ge(w_ld, 64)

                def project(b):
                    pe.wait_ge(zs_ready.sem, zs_ready.done(b))
                    pe.wait_ge(rot_ready.sem, rot_ready.prev(b))
                    for t in range(NT):
                        last = pe.matmul(psum[B_QK][:, t * TOK:(t + 1) * TOK], zs[:, t * P:(t + 1) * P], wa[:, 0:2 * CH],
                                         start=True, stop=True)
                    last.then_inc(qk_ps.sem, 1)
                    pe.wait_ge(vbd_ready.sem, vbd_ready.prev(b))
                    for c in range(NCK):
                        last = pe.matmul(psum[B_V][:, c * CH:(c + 1) * CH], zd[:, c].rearrange("p a k -> p (a k)"),
                                         wa[:, 2 * CH:3 * CH], start=True, stop=True)
                    last.then_inc(v_ps.sem, 1)

                def project_end(b):
                    pe.wait_ge(qkr_ready.sem, qkr_ready.done(b))
                    pe.wait_ge(qT_ready.sem, qT_ready.prev(b))
                    pe.wait_ge(kbd_ready.sem, kbd_ready.prev(b))
                    for w in range(2):
                        for t in range(NT):
                            last = pe.transpose(psum[B_T][:, (w * NT + t) * P:(w * NT + t + 1) * P], qkr[:, t, w, :],
                                                ident[:])
                    last.then_inc(qkT_ps.sem, 1)

                def unit(b, u):
                    t, hh = u // 2, u % 2
                    if u == 0:
                        hold(pe, qT_ready.sem, qT_ready.done(b), pe_passed)
                        hold(pe, kbd_ready.sem, kbd_ready.done(b), pe_passed)
                    hold(pe, sd_ready.sem, sd_ready.done(b, u - 2) if u >= 2 else sd_ready.prev(b, u + 2), pe_passed)
                    for c in range(2):
                        ck = 2 * t + c
                        last = pe.matmul(psum[B_S[u % 2]][c * CK:(c + 1) * CK, :], qT[:, ck * CK:(ck + 1) * CK],
                                         kbd[:, ck, hh * 8:hh * 8 + 8, :], start=True, stop=True)
                    last.then_inc(s_ready.sem, 1)
                    pe.wait_ge(p_ready.sem, p_ready.done(b, u))
                    pe.wait_ge(pT_ready.sem, pT_ready.done(b, u - 1) if u else pT_ready.prev(b, 3))
                    for pair in range(4):
                        last = pe.transpose(psum[B_PT][:, pair * P:(pair + 1) * P], pr[:, u % 2, pair * P:(pair + 1) * P],
                                            ident[:])
                    last.then_inc(pT_ps.sem, 1)
                    if u == 0:
                        hold(pe, vbd_ready.sem, vbd_ready.done(b), pe_passed)
                    hold(pe, pT_ready.sem, pT_ready.done(b, u), pe_passed)
                    hold(pe, on_ready.sem, on_ready.done(b, u - 1) if u else on_ready.prev(b, 3), pe_passed)
                    for c in range(2):
                        for pair in range(4):
                            last = pe.matmul(psum[B_O][c * CK:(c + 1) * CK, pair * 2 * VD:(pair + 1) * 2 * VD],
                                             pT[:, u % 2, pair, c * CK:(c + 1) * CK],
                                             vbd[:, 2 * t + c, hh * 4 + pair].rearrange("p e d -> p (e d)"),
                                             start=True, stop=True, skip_group_check=True)
                    last.then_inc(o_ready.sem, 1)

                def close(b):
                    pe.wait_ge(on_ready.sem, on_ready.done(b, 3))
                    pe.wait_ge(x_done.sem, x_done.prev(b))
                    for t in range(NT):
                        last = pe.transpose(psum[B_Y][:, t * P:(t + 1) * P], on[:, t].rearrange("p h d -> p (h d)"),
                                            ident[:])
                    last.then_inc(oT_ps.sem, 1)
                    pe.wait_ge(oT_ready.sem, oT_ready.done(b))
                    for t in range(NT):
                        last = pe.matmul(psum[B_Y][:, t * CH:(t + 1) * CH], oT[:, t * P:(t + 1) * P], wp[:],
                                         start=True, stop=True)
                    last.then_inc(y_ready.sem, 1)

                rounds(pe, project, project_end, unit, close)

            @block.scalar
            def _(act):
                for s in (zs_ready, qT_ready, vbd_ready, p_ready, pT_ready, oT_ready):
                    act.sem_inc(s.sem, s.credit)
                act.wait_ge(init, 3)

                def project(b):
                    act.wait_ge(v_ps.sem, v_ps.prev(b))
                    src = zT[:, bass.ds(b * TOK, TOK)]
                    act.activation(zs[:], src, ACT.Copy)
                    for a in range(2):
                        last = act.activation(zd[:, :, a, :], src.rearrange("p (c k) -> p c k", k=CK), ACT.Copy)
                    last.then_inc(zs_ready.sem, 1)

                def project_end(b):
                    act.wait_ge(qkT_ps.sem, qkT_ps.done(b))
                    act.wait_ge(s_ready.sem, s_ready.prev(b, 3))
                    act.activation(qT[:], psum[B_T][:, 0:TOK], ACT.Copy).then_inc(qT_ready.sem, 1)
                    act.wait_ge(v_ps.sem, v_ps.done(b))
                    act.wait_ge(o_ready.sem, o_ready.prev(b, 3))
                    for e in range(2):
                        rows = slice(e * CK, (e + 1) * CK)
                        last = act.activation(
                            vbd[rows, :, :, e, 0:D],
                            psum[B_V][rows].rearrange("p (c h e d) -> p c h e d", c=NCK, e=2, d=D)[:, :, :, e, :], ACT.Copy)
                    last.then_inc(vbd_ready.sem, 1)

                def unit(b, u):
                    act.wait_ge(sd_ready.sem, sd_ready.done(b, u))
                    act.wait_ge(pT_ps.sem, pT_ps.done(b, u - 2) if u >= 2 else pT_ps.prev(b, u + 2))
                    act.activation(pr[:, u % 2, :], sd[:, u % 2, :], ACT.Exp, scale=SCALE).then_inc(p_ready.sem, 1)
                    act.wait_ge(pT_ps.sem, pT_ps.done(b, u))
                    act.wait_ge(o_ready.sem, o_ready.done(b, u - 2) if u >= 2 else o_ready.prev(b, u + 2))
                    act.activation(pT[:, u % 2].rearrange("p a b -> p (a b)"), psum[B_PT][:], ACT.Copy)\
                       .then_inc(pT_ready.sem, 1)

                def close(b):
                    act.wait_ge(oT_ps.sem, oT_ps.done(b))
                    act.wait_ge(y_ready.sem, y_ready.prev(b))
                    act.activation(oT[:], psum[B_Y][:, 0:TOK], ACT.Copy).then_inc(oT_ready.sem, 1)

                def unit_first(b, u):
                    unit(b, u)

                rounds(act, project, project_end, unit_first, close)

            @block.vector
            def _(dve):
                for s in (rot_ready, qkr_ready, kbd_ready, mx_ready, sd_ready, rd_ready, on_ready, x_done):
                    dve.sem_inc(s.sem, s.credit)
                dve.wait_ge(w_ld, 64)

                def project(b):
                    src = psum[B_QK][:].rearrange("p (n d) -> p n d", d=D)
                    dve.wait_ge(qk_ps.sem, qk_ps.done(b))
                    dve.wait_ge(qkr_ready.sem, qkr_ready.prev(b))
                    dve.tensor_tensor(out=qk[:, 0], in0=src, in1=rope[:, 0, :].unsqueeze(1).to_broadcast([P, NG8, D]),
                                      op=ALU.mult)
                    for a in range(2):
                        o, s = a * 4, 4 - a * 4
                        last = dve.tensor_tensor(
                            out=qk[:, 1, :, o:o + 4], in0=src[:, :, s:s + 4],
                            in1=rope[:, 1, o:o + 4].unsqueeze(1).to_broadcast([P, NG8, 4]), op=ALU.mult)
                    last.then_inc(rot_ready.sem, 1)
                    dve.wait_ge(rot_ready.sem, rot_ready.done(b))
                    dve.wait_ge(qkT_ps.sem, qkT_ps.prev(b))
                    dve.tensor_tensor(out=qkr[:].rearrange("p t w c -> p (t w c)"),
                                      in0=qk[:, 0].rearrange("p n d -> p (n d)"),
                                      in1=qk[:, 1].rearrange("p n d -> p (n d)"), op=ALU.add).then_inc(qkr_ready.sem, 1)

                def project_end(b):
                    dve.wait_ge(qT_ready.sem, qT_ready.done(b))
                    dve.wait_ge(s_ready.sem, s_ready.prev(b, 3))
                    for c in range(NCK):
                        last = dve.tensor_tensor(
                            out=kbd[:, c],
                            in0=psum[B_T][:, TOK + c * CK:TOK + (c + 1) * CK].unsqueeze(1).to_broadcast([P, H, CK]),
                            in1=headmask[:].unsqueeze(2).to_broadcast([P, H, CK]), op=ALU.mult)
                    last.then_inc(kbd_ready.sem, 1)

                def unit(b, u):
                    t, hh = u // 2, u % 2
                    ps = psum[B_S[u % 2]][:].rearrange("p (a b) -> p a b", b=CK)
                    dve.wait_ge(s_ready.sem, s_ready.done(b, u))
                    dve.tensor_reduce(mx[:, u % 2, :], ps, AX.X, ALU.max).then_inc(mx_ready.sem, 1)
                    dve.wait_ge(mx_ready.sem, mx_ready.done(b, u))
                    dve.wait_ge(p_ready.sem, p_ready.done(b, u - 2) if u >= 2 else p_ready.prev(b, u + 2))
                    dve.tensor_tensor(out=sd[:, u % 2, :].rearrange("p (a b) -> p a b", b=CK), in0=ps,
                                      in1=mx[:, u % 2, :].unsqueeze(2).to_broadcast([P, 8, CK]), op=ALU.subtract)\
                       .then_inc(sd_ready.sem, 1)
                    pso = psum[B_O][:, 0:8 * VD].rearrange("p (h v) -> p h v", v=VD)
                    dve.wait_ge(o_ready.sem, o_ready.done(b, u))
                    dve.reciprocal(rd[:], pso[:, :, D]).then_inc(rd_ready.sem, 1)
                    dve.wait_ge(rd_ready.sem, rd_ready.done(b, u))
                    dve.wait_ge(oT_ps.sem, oT_ps.prev(b))
                    dve.tensor_tensor(out=on[:, t, hh * 8:hh * 8 + 8, :], in0=pso[:, :, 0:D],
                                      in1=rd[:].unsqueeze(2).to_broadcast([P, 8, D]), op=ALU.mult)\
                       .then_inc(on_ready.sem, 1)

                def close(b):
                    dve.wait_ge(y_ready.sem, y_ready.done(b))
                    xb = x[:, bass.ds(b * NT, NT), :]
                    dve.tensor_tensor(out=xb, in0=psum[B_Y][:, 0:TOK].rearrange("p (t c) -> p t c", c=CH), in1=xb,
                                      op=ALU.add).then_inc(x_done.sem, 1)

                rounds(dve, project, project_end, unit, close)


def latent_attention(nc, name, x, zT, wts, ident, identb, psum):
    R, VD = 64, CH + 1
    SCALE = 0.125
    BLOCKS = ((0, 0), (1, 0), (1, 1))
    B_L, B_V, B_S, B_PT, B_O, B_OT, B_Y = 0, 1, 2, 3, 4, 5, 6
    with ExitStack() as ctx:
        def sb(n, shape, dt=F32):
            return ctx.enter_context(nc.sbuf_tensor(f"{name}_{n}", shape, dt))

        def sem(n):
            return ctx.enter_context(nc.semaphore(f"{name}_{n}"))

        wb = sb("wb", [P, R])
        wv = sb("wv", [P, CH])
        wo = sb("wo", [P, CH])
        bv = sb("bv", [1, CH])
        bo = sb("bo", [1, CH])
        ones = sb("ones", [1, P])
        mask = sb("mask", [P, P])
        maskb = sb("maskb", [P, P], BF16)
        zs = sb("zs", [P, TOK])
        lat = sb("lat", [R, TOK])
        v = sb("v", [P, 2, NT, VD])
        mxr = sb("mxr", [P, NT])
        nmx = sb("nmx", [P, NT])
        pr = sb("pr", [P, 3, P])
        pT = sb("pT", [P, 3, P])
        rd = sb("rd", [P, NT])
        on = sb("on", [P, NT, CH])
        oT = sb("oT", [P, TOK])

        w_ld, init = sem("w_ld"), sem("init")
        names = ("zs", "l_ps", "lat", "v_ps", "v", "s", "mxr", "nmx", "p", "pT_ps", "pT", "o", "rd", "on", "oT_ps",
                 "oT", "y", "x")
        (zs_ready, l_ps, lat_ready, v_ps, v_ready, s_ready, mxr_ready, nmx_ready, p_ready, pT_ps, pT_ready, o_ready,
         rd_ready, on_ready, oT_ps, oT_ready, y_ready, x_done) = (Count(sem(n), 1) for n in names)
        pe_passed = sem("pe_passed")

        def rounds(eng, project, scores, middle, close):
            project(0, 0)
            scores(0)
            with eng.Fori(0, (SEQ - 2) // 2) as j:
                for a in range(2):
                    project(j * 2 + (a + 1), 1 - a)
                    middle(j * 2 + a, a)
                    scores(j * 2 + (a + 1))
                    close(j * 2 + a)
            project(SEQ - 1, 1)
            middle(SEQ - 2, 0)
            scores(SEQ - 1)
            close(SEQ - 2)
            middle(SEQ - 1, 1)
            close(SEQ - 1)

        with nc.Block() as block:
            @block.sync
            def _(sp):
                for dst, n in ((wb, "W_basis"), (wv, "W_v"), (wo, "W_o"), (bv, "b_v"), (bo, "b_o"), (mask, "causal")):
                    sp.dma_start(dst[:], wts[n]).then_inc(w_ld, 16)

            @block.gpsimd
            def _(pool):
                pool.memset(v[:], 1.0).then_inc(init, 1)
                pool.memset(ones[:], 1.0).then_inc(init, 1)

            @block.tensor
            def _(pe):
                for s in (l_ps, v_ps, s_ready, pT_ps, o_ready, oT_ps, y_ready):
                    pe.sem_inc(s.sem, s.credit)
                pe.wait_ge(w_ld, 96)
                pe.wait_ge(init, 3)

                def project(b, par):
                    hold(pe, lat_ready.sem, lat_ready.prev(b), pe_passed)
                    pe.wait_ge(zs_ready.sem, zs_ready.done(b))
                    pe.matmul(psum[B_L][0:R, 0:TOK], wb[:], zs[:], start=True, stop=True).then_inc(l_ps.sem, 1)
                    hold(pe, v_ready.sem, v_ready.prev(b), pe_passed)
                    for t in range(NT):
                        pe.matmul(psum[B_V][:, t * CH:(t + 1) * CH], ones[:], bv[:], start=True, stop=False)
                        last = pe.matmul(psum[B_V][:, t * CH:(t + 1) * CH], zs[:, t * P:(t + 1) * P], wv[:],
                                         start=False, stop=True)
                    last.then_inc(v_ps.sem, 1)

                def scores(b):
                    pe.wait_ge(lat_ready.sem, lat_ready.done(b))
                    pe.wait_ge(p_ready.sem, p_ready.prev(b))
                    for n, (qt, kt) in enumerate(BLOCKS):
                        out = psum[B_S][:, n * P:(n + 1) * P]
                        if qt == kt:
                            pe.matmul(out, identb[:], maskb[:], start=True, stop=False)
                        last = pe.matmul(out, lat[:, qt * P:(qt + 1) * P], lat[:, kt * P:(kt + 1) * P],
                                         start=(qt != kt), stop=True)
                    last.then_inc(s_ready.sem, 1)

                def middle(b, par):
                    pe.wait_ge(p_ready.sem, p_ready.done(b))
                    pe.wait_ge(pT_ready.sem, pT_ready.prev(b))
                    for n in range(3):
                        last = pe.transpose(psum[B_PT][:, n * P:(n + 1) * P], pr[:, n, :], ident[:])
                    last.then_inc(pT_ps.sem, 1)
                    hold(pe, v_ready.sem, v_ready.done(b), pe_passed)
                    pe.wait_ge(pT_ready.sem, pT_ready.done(b))
                    pe.wait_ge(on_ready.sem, on_ready.prev(b))
                    for n, (qt, kt) in enumerate(BLOCKS):
                        last = pe.matmul(psum[B_O][:, qt * VD:(qt + 1) * VD], pT[:, n, :], v[:, par, kt, :],
                                         start=(kt == 0), stop=(kt == qt))
                    last.then_inc(o_ready.sem, 1)

                def close(b):
                    pe.wait_ge(on_ready.sem, on_ready.done(b))
                    pe.wait_ge(oT_ready.sem, oT_ready.prev(b))
                    for t in range(NT):
                        last = pe.transpose(psum[B_OT][:, t * P:(t + 1) * P], on[:, t, :], ident[:])
                    last.then_inc(oT_ps.sem, 1)
                    pe.wait_ge(oT_ready.sem, oT_ready.done(b))
                    pe.wait_ge(x_done.sem, x_done.prev(b))
                    for t in range(NT):
                        pe.matmul(psum[B_Y][:, t * CH:(t + 1) * CH], ones[:], bo[:], start=True, stop=False)
                        last = pe.matmul(psum[B_Y][:, t * CH:(t + 1) * CH], oT[:, t * P:(t + 1) * P], wo[:],
                                         start=False, stop=True)
                    last.then_inc(y_ready.sem, 1)

                rounds(pe, project, scores, middle, close)

            @block.scalar
            def _(act):
                for s in (zs_ready, lat_ready, p_ready, pT_ready, oT_ready):
                    act.sem_inc(s.sem, s.credit)
                act.wait_ge(init, 3)

                def project(b, par):
                    act.wait_ge(v_ps.sem, v_ps.prev(b))
                    act.activation(zs[:], zT[:, bass.ds(b * TOK, TOK)], ACT.Copy).then_inc(zs_ready.sem, 1)
                    act.wait_ge(l_ps.sem, l_ps.done(b))
                    act.wait_ge(s_ready.sem, s_ready.prev(b))
                    act.activation(lat[:], psum[B_L][0:R, 0:TOK], ACT.Copy).then_inc(lat_ready.sem, 1)

                def scores(b):
                    act.wait_ge(nmx_ready.sem, nmx_ready.done(b))
                    act.wait_ge(pT_ps.sem, pT_ps.prev(b))
                    act.activation(pr[:, 0, :], psum[B_S][:, 0:P], ACT.Exp, bias=nmx[:, 0:1], scale=SCALE)
                    act.activation(pr[:, 1:3, :].rearrange("p a b -> p (a b)"), psum[B_S][:, P:3 * P], ACT.Exp,
                                   bias=nmx[:, 1:2], scale=SCALE).then_inc(p_ready.sem, 1)

                def middle(b, par):
                    act.wait_ge(pT_ps.sem, pT_ps.done(b))
                    act.wait_ge(o_ready.sem, o_ready.prev(b))
                    act.activation(pT[:].rearrange("p a b -> p (a b)"), psum[B_PT][:, 0:3 * P], ACT.Copy)\
                       .then_inc(pT_ready.sem, 1)

                def close(b):
                    act.wait_ge(oT_ps.sem, oT_ps.done(b))
                    act.wait_ge(y_ready.sem, y_ready.prev(b))
                    act.activation(oT[:], psum[B_OT][:, 0:TOK], ACT.Copy).then_inc(oT_ready.sem, 1)

                rounds(act, project, scores, middle, close)

            @block.vector
            def _(dve):
                for s in (v_ready, mxr_ready, nmx_ready, rd_ready, on_ready, x_done):
                    dve.sem_inc(s.sem, s.credit)
                dve.wait_ge(w_ld, 96)
                dve.tensor_copy(maskb[:], mask[:]).then_inc(init, 1)
                dve.wait_ge(init, 3)

                def project(b, par):
                    dve.wait_ge(v_ps.sem, v_ps.done(b))
                    dve.tensor_copy(v[:, par, :, 0:CH], psum[B_V][:, 0:TOK].rearrange("p (t c) -> p t c", c=CH))\
                       .then_inc(v_ready.sem, 1)

                def scores(b):
                    dve.wait_ge(s_ready.sem, s_ready.done(b))
                    dve.tensor_reduce(mxr[:, 0:1], psum[B_S][:, 0:P], AX.X, ALU.max)
                    dve.tensor_reduce(mxr[:, 1:2], psum[B_S][:, P:3 * P], AX.X, ALU.max).then_inc(mxr_ready.sem, 1)
                    dve.wait_ge(mxr_ready.sem, mxr_ready.done(b))
                    dve.wait_ge(p_ready.sem, p_ready.prev(b))
                    dve.tensor_scalar(nmx[:], mxr[:], -SCALE, None, ALU.mult).then_inc(nmx_ready.sem, 1)

                def middle(b, par):
                    ps = psum[B_O][:, 0:2 * VD].rearrange("p (t v) -> p t v", v=VD)
                    dve.wait_ge(o_ready.sem, o_ready.done(b))
                    dve.reciprocal(rd[:], ps[:, :, CH]).then_inc(rd_ready.sem, 1)
                    dve.wait_ge(rd_ready.sem, rd_ready.done(b))
                    dve.wait_ge(oT_ps.sem, oT_ps.prev(b))
                    dve.tensor_tensor(out=on[:], in0=ps[:, :, 0:CH], in1=rd[:].unsqueeze(2).to_broadcast([P, NT, CH]),
                                      op=ALU.mult).then_inc(on_ready.sem, 1)

                def close(b):
                    dve.wait_ge(y_ready.sem, y_ready.done(b))
                    xb = x[:, bass.ds(b * NT, NT), :]
                    dve.tensor_tensor(out=xb, in0=psum[B_Y][:, 0:TOK].rearrange("p (t c) -> p t c", c=CH), in1=xb,
                                      op=ALU.add).then_inc(x_done.sem, 1)

                rounds(dve, project, scores, middle, close)


def memory_attention(nc, name, x, z, zT, wts, ident, psum):
    A48, TW = 48, 48 + 2 * CH
    SL = (slice(0, 8), slice(32, 48))
    NS = (8, 16)
    BW = TOK + P
    SCALE = float(np.float32(CH) ** np.float32(-0.5))
    B_TOK, B_CH, B_M, B_SR, B_T = (0, 1), (2, 3), (4, 5), 6, 7
    with ExitStack() as ctx:
        def sb(n, shape, dt=F32):
            return ctx.enter_context(nc.sbuf_tensor(f"{name}_{n}", shape, dt))

        def sem(n):
            return ctx.enter_context(nc.semaphore(f"{name}_{n}"))

        wt = sb("wt", [P, TW])
        wc = sb("wc", [P, 4, CH])
        wm = sb("wm", [P, 3, CH])
        tokb = sb("tokb", [P, TW])
        chb = sb("chb", [P, 4])
        combb = sb("combb", [1, CH])
        gbr = sb("gbr", [P, 2, CH])
        decay = sb("decay", [P, 2, BW])
        ones = sb("ones", [1, P])
        power = sb("power", [P, NT])
        zs = sb("zs", [P, 2, TOK])
        tok = sb("tok", [P, 2, NT, TW])
        mxa = sb("mxa", [P, NT, 2])
        sa = sb("sa", [P, NT, A48])
        ea = sb("ea", [P, NT, A48])
        gp = sb("gp", [P, NT, 4])
        eg = sb("eg", [P, NT, 4])
        rg = sb("rg", [P, NT, 2])
        eg1 = sb("eg1", [P, NT, 2])
        den = sb("den", [P, NT, 2])
        dg = sb("dg", [P, NT, 2])
        ra = sb("ra", [P, NT, 2])
        adr = sb("adr", [P, 2, NT, A48])
        aT = sb("aT", [A48, 2, TOK])
        ch = sb("ch", [P, 4, TOK])
        mt = sb("mt", [P, 2, BW])
        mxs = sb("mxs", [P, NT, 2])
        ss = sb("ss", [P, NT, A48])
        es = sb("es", [P, NT, A48])
        dens = sb("dens", [P, NT, 2])
        rs = sb("rs", [P, NT, 2])
        w = sb("w", [P, NT, A48])
        wT = sb("wT", [A48, TOK])
        gt = sb("gt", [P, 2, BW])
        rT = sb("rT", [P, 2, TOK])
        cc = sb("cc", [P, NT, CH])
        st = sb("st", [P, NT, 6])
        mv = sb("mv", [P, NT, 2])
        ve = sb("ve", [P, NT])
        rstd = sb("rstd", [P, NT])
        cn = sb("cn", [P, NT, CH])

        w_ld, init = sem("w_ld"), sem("init")
        names = ("zs", "tok_ps", "tok", "mxa", "sa", "ea", "den", "dg", "rg", "ra", "adr", "aT_ps", "aT", "ch_ps", "ch",
                 "m", "mt", "s", "mxs", "ss", "es", "dens", "rs", "w", "wT_ps", "wT", "g", "gt", "r", "rT", "c", "cc",
                 "st", "mv", "ve", "rstd", "cn", "cg", "cb", "x")
        (zs_ready, tok_ps, tok_ready, mxa_ready, sa_ready, ea_ready, den_ready, dg_ready, rg_ready, ra_ready, adr_ready, aT_ps,
         aT_ready, ch_ps, ch_ready, m_ready, mt_ready, s_ready, mxs_ready, ss_ready, es_ready, dens_ready, rs_ready,
         w_ready, wT_ps, wT_ready, g_ready, gt_ready, r_ready, rT_ready, c_ready, cc_ready, st_ready, mv_ready,
         ve_ready, rstd_ready, cn_ready, cg_ready, cb_ready, x_done) = (Count(sem(n), 1) for n in names)
        c_ready.credit = 2
        pe_passed, dve_passed, pool_passed = sem("pe_passed"), sem("dve_passed"), sem("pool_passed")

        def rounds(eng, project, turn_adr, match, score, read, close):
            project(0, 0)
            turn_adr(0, 0, None)

            def turn(b, par, ahead):
                match(b, par)
                if ahead:
                    project(b + 1, 1 - par)
                score(b, par)
                if ahead:
                    turn_adr(b + 1, 1 - par, b)
                read(b, par)
                close(b, par, ahead)

            with eng.Fori(0, (SEQ - 2) // 2) as j:
                turn(j * 2, 0, True)
                turn(j * 2 + 1, 1, True)
            turn(SEQ - 2, 0, True)
            turn(SEQ - 1, 1, False)

        with nc.Block() as block:
            @block.sync
            def _(sp):
                for dst, n in ((wt, "wt"), (wc, "wc"), (wm, "wm"), (chb, "chb"), (combb, "combb"), (decay, "decay")):
                    sp.dma_start(dst[:], wts[n]).then_inc(w_ld, 16)
                sp.dma_start(tokb[:], wts["tokb"].partition_broadcast(P)).then_inc(w_ld, 16)
                sp.dma_start(gbr[:], wts["gbr"].partition_broadcast(P)).then_inc(w_ld, 16)

            @block.gpsimd
            def _(pool):
                for s in (ve_ready, rstd_ready):
                    pool.sem_inc(s.sem, s.credit)
                pool.memset(ones[:], 1.0).then_inc(init, 1)
                pool.memset(power[:], -0.5).then_inc(init, 1)
                for a in (sa, ss, w, adr):
                    pool.memset(a[:], 0.0).then_inc(init, 1)
                pool.wait_ge(init, 6)
                with pool.Fori(0, SEQ) as b:
                    hold(pool, mv_ready.sem, mv_ready.done(b), pool_passed)
                    pool.tensor_scalar(ve[:], mv[:, :, 1], EPS, None, ALU.add).then_inc(ve_ready.sem, 1)
                    pool.wait_ge(ve_ready.sem, ve_ready.done(b))
                    pool.tensor_tensor(out=rstd[:], in0=ve[:], in1=power[:], op=ALU.pow).then_inc(rstd_ready.sem, 1)

            @block.tensor
            def _(pe):
                for s in (tok_ps, aT_ps, ch_ps, m_ready, s_ready, wT_ps, g_ready, r_ready, c_ready):
                    pe.sem_inc(s.sem, s.credit)
                pe.wait_ge(w_ld, 128)
                pe.wait_ge(init, 6)

                def project(b, par):
                    pe.wait_ge(zs_ready.sem, zs_ready.done(b))
                    hold(pe, tok_ready.sem, tok_ready.prev(b), pe_passed)
                    for t in range(NT):
                        last = pe.matmul(psum[B_TOK[t]][:, 0:TW], zs[:, par, t * P:(t + 1) * P], wt[:],
                                         start=True, stop=True)
                    last.then_inc(tok_ps.sem, 1)
                    pe.wait_ge(ch_ready.sem, ch_ready.prev(b))
                    for k in range(4):
                        last = pe.matmul(psum[B_CH[k // 2]][:, (k % 2) * TOK:(k % 2 + 1) * TOK], wc[:, k, :],
                                         zs[:, par, :], start=True, stop=True)
                    last.then_inc(ch_ps.sem, 1)

                def turn_adr(b, par, before):
                    hold(pe, adr_ready.sem, adr_ready.done(b), pe_passed)
                    if before is not None:
                        hold(pe, wT_ready.sem, wT_ready.done(before), pe_passed)
                    for t in range(NT):
                        last = pe.transpose(psum[B_T][0:A48, t * P:(t + 1) * P], adr[:, par, t, :], ident[:])
                    last.then_inc(aT_ps.sem, 1)

                def blocks(out, lhs, rhs):
                    pe.matmul(out[:, 0:TOK], lhs[:, 0:P], rhs[:, 0:TOK], start=True, stop=True)
                    return pe.matmul(out[:, TOK:BW], lhs[:, P:TOK], rhs[:, P:TOK], start=True, stop=True)

                def match(b, par):
                    pe.wait_ge(ch_ready.sem, ch_ready.done(b))
                    hold(pe, gt_ready.sem, gt_ready.prev(b), pe_passed)
                    for r in range(2):
                        last = blocks(psum[B_M[r]], ch[:, 2 * r, :], ch[:, 2 * r + 1, :])
                    last.then_inc(m_ready.sem, 1)

                def score(b, par):
                    hold(pe, rT_ready.sem, rT_ready.prev(b), pe_passed)
                    pe.wait_ge(mt_ready.sem, mt_ready.done(b))
                    for r in range(2):
                        for t in range(NT):
                            out = psum[B_SR][:, t * A48 + SL[r].start:t * A48 + SL[r].stop]
                            last = pe.matmul(out, mt[:, r, t * P:(t + 1) * P], adr[:, par, 0, SL[r]],
                                             start=True, stop=(t == 0))
                        last = pe.matmul(out, mt[:, r, TOK:BW], adr[:, par, 1, SL[r]], start=False, stop=True)
                    last.then_inc(s_ready.sem, 1)
                    hold(pe, cc_ready.sem, cc_ready.prev(b), pe_passed)
                    hold(pe, w_ready.sem, w_ready.done(b), pe_passed)
                    for t in range(NT):
                        last = pe.transpose(psum[B_T][0:A48, t * P:(t + 1) * P], w[:, t, :], ident[:])
                    last.then_inc(wT_ps.sem, 1)

                def read(b, par):
                    hold(pe, wT_ready.sem, wT_ready.done(b), pe_passed)
                    hold(pe, aT_ready.sem, aT_ready.done(b), pe_passed)
                    for r in range(2):
                        last = blocks(psum[B_M[r]], aT[SL[r], par, :], wT[SL[r], :])
                    last.then_inc(g_ready.sem, 1)
                    pe.wait_ge(gt_ready.sem, gt_ready.done(b))
                    for r in range(2):
                        val = slice(A48 + r * CH, A48 + (r + 1) * CH)
                        pe.matmul(psum[B_SR][:, r * TOK:(r + 1) * TOK], tok[:, par, 0, val], gt[:, r, 0:TOK],
                                  start=True, stop=True)
                        last = pe.matmul(psum[B_SR][:, r * TOK + P:(r + 1) * TOK], tok[:, par, 1, val],
                                         gt[:, r, TOK:BW], start=False, stop=True, skip_group_check=True)
                    last.then_inc(r_ready.sem, 1)

                def close(b, par, ahead):
                    if ahead:
                        hold(pe, aT_ready.sem, aT_ready.done(b + 1), pe_passed)
                    pe.wait_ge(rT_ready.sem, rT_ready.done(b))
                    for t in range(NT):
                        out = psum[B_T][:, t * CH:(t + 1) * CH]
                        tt = slice(t * P, (t + 1) * P)
                        pe.matmul(out, ones[:], combb[:], start=True, stop=False)
                        pe.matmul(out, zs[:, par, tt], wm[:, 0, :], start=False, stop=False)
                        pe.matmul(out, rT[:, 0, tt], wm[:, 1, :], start=False, stop=False)
                        last = pe.matmul(out, rT[:, 1, tt], wm[:, 2, :], start=False, stop=True)
                    last.then_inc(c_ready.sem, 1)

                rounds(pe, project, turn_adr, match, score, read, close)

            @block.scalar
            def _(act):
                for s in (zs_ready, ch_ready, ea_ready, aT_ready, es_ready, wT_ready, rT_ready):
                    act.sem_inc(s.sem, s.credit)
                act.wait_ge(w_ld, 128)

                def project(b, par):
                    act.wait_ge(c_ready.sem, c_ready.prev(b, -1))
                    act.activation(zs[:, par, :], zT[:, bass.ds(b * TOK, TOK)], ACT.Copy).then_inc(zs_ready.sem, 1)
                    act.wait_ge(sa_ready.sem, sa_ready.done(b))
                    act.activation(ea[:], sa[:], ACT.Exp)
                    act.activation(eg[:], gp[:], ACT.Exp, scale=5.0).then_inc(ea_ready.sem, 1)
                    act.wait_ge(ch_ps.sem, ch_ps.done(b))
                    act.wait_ge(m_ready.sem, m_ready.prev(b))
                    for k in range(4):
                        last = act.activation(ch[:, k, :], psum[B_CH[k // 2]][:, (k % 2) * TOK:(k % 2 + 1) * TOK],
                                              ACT.Identity, bias=chb[:, k:k + 1])
                    last.then_inc(ch_ready.sem, 1)

                def turn_adr(b, par, before):
                    act.wait_ge(aT_ps.sem, aT_ps.done(b))
                    act.activation(aT[:, par, :], psum[B_T][0:A48, 0:TOK], ACT.Copy).then_inc(aT_ready.sem, 1)

                def score(b, par):
                    act.wait_ge(ss_ready.sem, ss_ready.done(b))
                    act.activation(es[:], ss[:], ACT.Exp, scale=SCALE).then_inc(es_ready.sem, 1)
                    act.wait_ge(wT_ps.sem, wT_ps.done(b))
                    act.wait_ge(g_ready.sem, g_ready.prev(b))
                    act.activation(wT[:], psum[B_T][0:A48, 0:TOK], ACT.Copy).then_inc(wT_ready.sem, 1)

                def read(b, par):
                    act.wait_ge(r_ready.sem, r_ready.done(b))
                    act.wait_ge(c_ready.sem, c_ready.prev(b))
                    act.activation(rT[:].rearrange("p r t -> p (r t)"), psum[B_SR][:], ACT.Copy)\
                       .then_inc(rT_ready.sem, 1)

                rounds(act, project, turn_adr, lambda b, par: None, score, read, lambda b, par, ahead: None)

            @block.vector
            def _(dve):
                for s in (tok_ready, mxa_ready, sa_ready, den_ready, dg_ready, rg_ready, ra_ready, adr_ready, mt_ready, mxs_ready,
                          ss_ready, dens_ready, rs_ready, w_ready, gt_ready, cc_ready, st_ready, mv_ready, cn_ready,
                          cg_ready, cb_ready, x_done):
                    dve.sem_inc(s.sem, s.credit)
                dve.wait_ge(w_ld, 128)
                dve.wait_ge(init, 6)

                def each(op):
                    for r in range(2):
                        last = op(r)
                    return last

                def bc(ap, r):
                    return ap[:, :, r:r + 1].to_broadcast([P, NT, NS[r]])

                def project(b, par):
                    tk = tok[:, par]
                    dve.wait_ge(tok_ps.sem, tok_ps.done(b))
                    for t in range(NT):
                        last = dve.tensor_tensor(out=tok[:, par, t, :], in0=psum[B_TOK[t]][:, 0:TW], in1=tokb[:],
                                                 op=ALU.add)
                    last.then_inc(tok_ready.sem, 1)
                    dve.wait_ge(tok_ready.sem, tok_ready.done(b))
                    each(lambda r: dve.tensor_reduce(mxa[:, :, r], tk[:, :, SL[r]], AX.X, ALU.max))\
                        .then_inc(mxa_ready.sem, 1)
                    dve.wait_ge(mxa_ready.sem, mxa_ready.done(b))
                    dve.tensor_scalar(gp[:, :, 0:2], tk[:, :, 8:10], 0.0, None, ALU.min)
                    dve.tensor_scalar(gp[:, :, 2:4], tk[:, :, 8:10], 0.0, -1.0, ALU.max, ALU.mult)
                    each(lambda r: dve.tensor_tensor(out=sa[:, :, SL[r]], in0=tk[:, :, SL[r]], in1=bc(mxa, r),
                                                     op=ALU.subtract)).then_inc(sa_ready.sem, 1)
                    dve.wait_ge(ea_ready.sem, ea_ready.done(b))
                    dve.tensor_tensor(out=eg1[:], in0=eg[:, :, 0:2], in1=eg[:, :, 2:4], op=ALU.add)
                    each(lambda r: dve.tensor_reduce(den[:, :, r], ea[:, :, SL[r]], AX.X, ALU.add))\
                        .then_inc(den_ready.sem, 1)
                    dve.wait_ge(den_ready.sem, den_ready.done(b))
                    dve.tensor_tensor(out=dg[:], in0=den[:], in1=eg1[:], op=ALU.mult).then_inc(dg_ready.sem, 1)
                    dve.wait_ge(dg_ready.sem, dg_ready.done(b))
                    dve.reciprocal(rg[:], dg[:]).then_inc(rg_ready.sem, 1)
                    dve.wait_ge(rg_ready.sem, rg_ready.done(b))
                    dve.tensor_tensor(out=ra[:], in0=rg[:], in1=eg[:, :, 0:2], op=ALU.mult).then_inc(ra_ready.sem, 1)
                    dve.wait_ge(ra_ready.sem, ra_ready.done(b))
                    each(lambda r: dve.tensor_tensor(out=adr[:, par, :, SL[r]], in0=ea[:, :, SL[r]], in1=bc(ra, r),
                                                     op=ALU.mult)).then_inc(adr_ready.sem, 1)

                def match(b, par):
                    dve.wait_ge(m_ready.sem, m_ready.done(b))
                    dve.wait_ge(s_ready.sem, s_ready.prev(b))
                    each(lambda r: dve.tensor_tensor(out=mt[:, r, :], in0=psum[B_M[r]][:, 0:BW], in1=decay[:, r, :],
                                                     op=ALU.mult)).then_inc(mt_ready.sem, 1)

                def score(b, par):
                    ps = psum[B_SR][:, 0:NT * A48].rearrange("p (t a) -> p t a", t=NT)
                    dve.wait_ge(s_ready.sem, s_ready.done(b))
                    each(lambda r: dve.tensor_reduce(mxs[:, :, r], ps[:, :, SL[r]], AX.X, ALU.max))\
                        .then_inc(mxs_ready.sem, 1)
                    dve.wait_ge(mxs_ready.sem, mxs_ready.done(b))
                    each(lambda r: dve.tensor_tensor(out=ss[:, :, SL[r]], in0=ps[:, :, SL[r]], in1=bc(mxs, r),
                                                     op=ALU.subtract)).then_inc(ss_ready.sem, 1)
                    dve.wait_ge(es_ready.sem, es_ready.done(b))
                    each(lambda r: dve.tensor_reduce(dens[:, :, r], es[:, :, SL[r]], AX.X, ALU.add))\
                        .then_inc(dens_ready.sem, 1)
                    dve.wait_ge(dens_ready.sem, dens_ready.done(b))
                    dve.reciprocal(rs[:], dens[:]).then_inc(rs_ready.sem, 1)
                    dve.wait_ge(rs_ready.sem, rs_ready.done(b))
                    dve.wait_ge(wT_ps.sem, wT_ps.prev(b))
                    each(lambda r: dve.tensor_tensor(out=w[:, :, SL[r]], in0=es[:, :, SL[r]], in1=bc(rs, r),
                                                     op=ALU.mult)).then_inc(w_ready.sem, 1)

                def read(b, par):
                    dve.wait_ge(g_ready.sem, g_ready.done(b))
                    dve.wait_ge(r_ready.sem, r_ready.prev(b))
                    each(lambda r: dve.tensor_tensor(out=gt[:, r, :], in0=psum[B_M[r]][:, 0:BW], in1=decay[:, r, :],
                                                     op=ALU.mult)).then_inc(gt_ready.sem, 1)

                def close(b, par, ahead):
                    tiles = bass.ds(b * NT, NT)
                    dve.wait_ge(c_ready.sem, c_ready.done(b))
                    dve.tensor_tensor(out=cc[:], in0=psum[B_T][:, 0:TOK].rearrange("p (t c) -> p t c", c=CH),
                                      in1=z[:, tiles, :], op=ALU.add).then_inc(cc_ready.sem, 1)
                    hold(dve, cc_ready.sem, cc_ready.done(b), dve_passed)
                    for t in range(NT):
                        last = dve.bn_stats(st[:, t, :], cc[:, t, :])
                    last.then_inc(st_ready.sem, 1)
                    hold(dve, st_ready.sem, st_ready.done(b), dve_passed)
                    for t in range(NT):
                        last = dve.bn_aggr(mv[:, t, :], st[:, t, :])
                    last.then_inc(mv_ready.sem, 1)
                    dve.wait_ge(rstd_ready.sem, rstd_ready.done(b))
                    for t in range(NT):
                        last = dve.tensor_scalar(cn[:, t, :], cc[:, t, :], mv[:, t, 0:1], rstd[:, t:t + 1],
                                                 ALU.subtract, ALU.mult)
                    last.then_inc(cn_ready.sem, 1)
                    dve.wait_ge(cn_ready.sem, cn_ready.done(b))
                    dve.tensor_tensor(out=cc[:], in0=cn[:], in1=gbr[:, 0:1, :].to_broadcast([P, NT, CH]), op=ALU.mult)\
                       .then_inc(cg_ready.sem, 1)
                    dve.wait_ge(cg_ready.sem, cg_ready.done(b))
                    dve.tensor_tensor(out=cn[:], in0=cc[:], in1=gbr[:, 1:2, :].to_broadcast([P, NT, CH]), op=ALU.add)\
                       .then_inc(cb_ready.sem, 1)
                    dve.wait_ge(cb_ready.sem, cb_ready.done(b))
                    dve.tensor_tensor(out=x[:, tiles, :], in0=cn[:], in1=x[:, tiles, :], op=ALU.add)\
                       .then_inc(x_done.sem, 1)

                rounds(dve, project, lambda b, par, before: None, match, score, read, close)


def routed_feed(nc, name, x, zT, wts, ident, psum):
    E, FC, CK = 8, 4, 512
    NTILE = SEQ * NT
    TURNS = SEQ * TOK // CK
    CT = CK // P
    with ExitStack() as ctx:
        def sb(n, shape, dt=F32):
            return ctx.enter_context(nc.sbuf_tensor(f"{name}_{n}", shape, dt))

        def sem(n):
            return ctx.enter_context(nc.semaphore(f"{name}_{n}"))

        w1 = sb("w1", [P, E, FC * P])
        w2 = sb("w2", [P, E, FC, CH])
        b1 = sb("b1", [P, E * FC])
        b2 = sb("b2", [P, 16 * CH])
        wr = sb("wr", [P, E])
        br = sb("br", [P, E])
        rank = sb("rank", [P, E])
        zs = sb("zs", [P, 2, TOK])
        lg = sb("lg", [P, NTILE, E])
        work = sb("work", [P, NTILE, E])
        gate = sb("gate", [P, NTILE, E])
        best = sb("best", [P, NTILE])
        den = sb("den", [P, NTILE])
        prob = sb("prob", [P, NTILE])
        gT = sb("gT", [P, 2, P])
        h = sb("h", [P, 2, FC, CK])
        w_ld, w2_ld, step, lg_all = sem("w_ld"), sem("w2_ld"), sem("step"), sem("lg_all")
        exps, gT_ps, gT_ready, bias_ps, bias_done = (sem(n) for n in ("exps", "gT_ps", "gT", "bias_ps", "bias_done"))
        zs_ready = Count(sem("zs"), 2)
        l_ps = Count(sem("l_ps"), 2)
        lg_ready = Count(sem("lg"), 2)
        h_ps = Count(sem("h_ps"), E * FC)
        ha_ready = Count(sem("ha"), E * FC // 2)
        hv_ready = Count(sem("hv"), E * FC // 2)
        y_ready = Count(sem("y"), E)
        x_done = Count(sem("x"), E)

        with nc.Block() as block:
            @block.sync
            def _(sp):
                for dst, n in ((wr, "Wr"), (b1, "b1"), (b2, "b2"), (rank, "rank")):
                    sp.dma_start(dst[:], wts[n]).then_inc(w_ld, 16)
                sp.dma_start(br[:], wts["br"].partition_broadcast(P)).then_inc(w_ld, 16)
                sp.dma_start(w1[:], wts["W1"].rearrange("e k f -> k e f")).then_inc(w2_ld, 16)
                sp.dma_start(w2[:], wts["W2"].rearrange("e (f k) n -> k e f n", k=P)).then_inc(w2_ld, 16)

            @block.tensor
            def _(pe):
                for s in (l_ps, h_ps, y_ready):
                    pe.sem_inc(s.sem, s.credit)
                pe.wait_ge(w_ld, 80)
                with pe.Fori(0, SEQ // 2) as j:
                    for a in range(2):
                        pe.wait_ge(lg_ready.sem, lg_ready.prev(j, a))
                        pe.wait_ge(zs_ready.sem, zs_ready.done(j, a))
                        for t in range(NT):
                            last = pe.matmul(psum[a][:, t * E:(t + 1) * E], zs[:, a, t * P:(t + 1) * P], wr[:],
                                             start=True, stop=True)
                        last.then_inc(l_ps.sem, 1)
                pe.wait_ge(step, 9)
                for a in range(2):
                    last = pe.transpose(psum[a][:, 0:P], gate[:, a * 16:(a + 1) * 16, :].rearrange("p t e -> p (t e)"),
                                        ident[:])
                last.then_inc(gT_ps, 1)
                pe.wait_ge(gT_ready, 1)
                for n in range(8):
                    pe.matmul(psum[n][:], gT[:, n // 4, :], b2[:, (n % 4) * 512:(n % 4 + 1) * 512], start=True, stop=True)\
                      .then_inc(bias_ps, 1)
                pe.wait_ge(bias_done, 8)
                pe.wait_ge(w2_ld, 32)

                def hidden(j, e, f):
                    m = e * (FC // 2) + f // 2
                    done = (ha_ready, hv_ready)[f % 2]
                    pe.wait_ge(done.sem, done.done(j, m - FC // 2) if e else done.prev(j, m + (E - 1) * FC // 2))
                    pe.matmul(psum[f][:], w1[:, e, f * P:(f + 1) * P], zT[:, bass.ds(j * CK, CK)], start=True, stop=True)\
                      .then_inc(h_ps.sem, 1)

                def down(j, e):
                    pe.wait_ge(ha_ready.sem, ha_ready.done(j, (e + 1) * FC // 2 - 1))
                    pe.wait_ge(hv_ready.sem, hv_ready.done(j, (e + 1) * FC // 2 - 1))
                    pe.wait_ge(x_done.sem, x_done.done(j, e - 2) if e >= 2 else x_done.prev(j, E - 2 + e))
                    for t in range(CT):
                        for f in range(FC):
                            last = pe.matmul(psum[4 + e % 2][:, t * CH:(t + 1) * CH], h[:, e % 2, f, t * P:(t + 1) * P],
                                             w2[:, e, f, :], start=(f == 0), stop=(f == FC - 1))
                    last.then_inc(y_ready.sem, 1)

                with pe.Fori(0, TURNS) as j:
                    for e in range(E):
                        for f in range(FC):
                            hidden(j, e, f)
                        if e:
                            down(j, e - 1)
                    down(j, E - 1)

            @block.scalar
            def _(act):
                for s in (zs_ready, ha_ready):
                    act.sem_inc(s.sem, s.credit)
                with act.Fori(0, SEQ // 2) as j:
                    for a in range(2):
                        act.wait_ge(l_ps.sem, l_ps.prev(j, a))
                        act.activation(zs[:, a, :], zT[:, bass.ds(j * 2 * TOK + a * TOK, TOK)], ACT.Copy)\
                           .then_inc(zs_ready.sem, 1)
                act.wait_ge(step, 2)
                act.activation(work[:].rearrange("p t e -> p (t e)"), work[:].rearrange("p t e -> p (t e)"), ACT.Exp)\
                   .then_inc(exps, 1)
                act.wait_ge(gT_ps, 1)
                for a in range(2):
                    last = act.activation(gT[:, a, :], psum[a][:, 0:P], ACT.Copy)
                last.then_inc(gT_ready, 1)
                act.wait_ge(w_ld, 80)
                with act.Fori(0, TURNS) as j:
                    for e in range(E):
                        for f in range(0, FC, 2):
                            act.wait_ge(h_ps.sem, h_ps.done(j, e * FC + f))
                            act.wait_ge(y_ready.sem, y_ready.done(j, e - 2) if e >= 2 else y_ready.prev(j, E - 2 + e))
                            act.activation(h[:, e % 2, f, :], psum[f][:], ACT.Relu, bias=b1[:, e * FC + f:e * FC + f + 1])\
                               .then_inc(ha_ready.sem, 1)

            @block.vector
            def _(dve):
                for s in (lg_ready, hv_ready, x_done):
                    dve.sem_inc(s.sem, s.credit)
                dve.wait_ge(w_ld, 80)
                with dve.Fori(0, SEQ // 2) as j:
                    for a in range(2):
                        dve.wait_ge(l_ps.sem, l_ps.done(j, a))
                        dve.tensor_tensor(out=lg[:, bass.ds(j * 2 * NT + a * NT, NT), :],
                                          in0=psum[a][:, 0:NT * E].rearrange("p (t e) -> p t e", e=E),
                                          in1=br[:].unsqueeze(1).to_broadcast([P, NT, E]), op=ALU.add)\
                           .then_inc(lg_ready.sem, 1)

                def over(ap):
                    return ap[:].unsqueeze(2).to_broadcast([P, NTILE, E])

                ranks = rank[:].unsqueeze(1).to_broadcast([P, NTILE, E])
                dve.wait_ge(lg_ready.sem, SEQ + lg_ready.credit)
                dve.tensor_reduce(best[:], lg[:], AX.X, ALU.max).then_inc(step, 1)
                dve.wait_ge(step, 1)
                dve.tensor_tensor(out=work[:], in0=lg[:], in1=over(best), op=ALU.subtract).then_inc(step, 1)
                dve.wait_ge(exps, 1)
                dve.tensor_reduce(den[:], work[:], AX.X, ALU.add).then_inc(step, 1)
                dve.wait_ge(step, 3)
                dve.reciprocal(prob[:], den[:])
                dve.tensor_tensor(out=work[:], in0=lg[:], in1=over(best), op=ALU.is_equal).then_inc(step, 1)
                dve.wait_ge(step, 4)
                dve.tensor_tensor(out=lg[:], in0=work[:], in1=ranks, op=ALU.mult).then_inc(step, 1)
                dve.wait_ge(step, 5)
                dve.tensor_reduce(best[:], lg[:], AX.X, ALU.max).then_inc(step, 1)
                dve.wait_ge(step, 6)
                dve.tensor_tensor(out=work[:], in0=lg[:], in1=over(best), op=ALU.is_equal).then_inc(step, 2)
                dve.wait_ge(step, 8)
                dve.tensor_tensor(out=gate[:], in0=work[:], in1=over(prob), op=ALU.mult).then_inc(step, 1)
                for n in range(8):
                    dve.wait_ge(bias_ps, n + 1)
                    dve.tensor_tensor(out=x[:, 4 * n:4 * n + 4, :], in0=psum[n][:].rearrange("p (t c) -> p t c", c=CH),
                                      in1=x[:, 4 * n:4 * n + 4, :], op=ALU.add).then_inc(bias_done, 1)
                dve.wait_ge(bias_done, 8)

                def relus(j, e):
                    for f in range(1, FC, 2):
                        dve.wait_ge(h_ps.sem, h_ps.done(j, e * FC + f))
                        dve.wait_ge(y_ready.sem, y_ready.done(j, e - 2) if e >= 2 else y_ready.prev(j, E - 2 + e))
                        dve.tensor_scalar(h[:, e % 2, f, :], psum[f][:], b1[:, e * FC + f:e * FC + f + 1], 0.0,
                                          ALU.add, ALU.max).then_inc(hv_ready.sem, 1)

                def add(j, e):
                    dve.wait_ge(y_ready.sem, y_ready.done(j, e))
                    dve.wait_ge(x_done.sem, x_done.done(j, e - 1) if e else x_done.prev(j, E - 1))
                    for t in range(CT):
                        tile = bass.ds(j * CT + t, 1)
                        xt = x[:, tile, :].rearrange("p a c -> p (a c)")
                        last = dve.scalar_tensor_tensor(out=xt, in0=psum[4 + e % 2][:, t * CH:(t + 1) * CH],
                                                        scalar=gate[:, tile, e:e + 1].rearrange("p a c -> p (a c)"),
                                                        in1=xt, op0=ALU.mult, op1=ALU.add)
                    last.then_inc(x_done.sem, 1)

                with dve.Fori(0, TURNS) as j:
                    for e in range(E):
                        relus(j, e)
                        if e:
                            add(j, e - 1)
                    add(j, E - 1)


def local_constants(W):
    f = np.float32
    half = np.arange(0, HD, 2, dtype=f)
    inv_freq = (f(1.0) / np.power(f(10000.0), half / f(HD))).astype(f)
    t = np.arange(TOK, dtype=f)
    freqs = t[:, None] * inv_freq[None, :]
    freqs = np.concatenate([freqs, freqs], -1)
    base = ((half + f(0.4 * HD)) / f(1.4 * HD)).astype(f)
    power = ((t - f(TOK // 2)) / f(W // 2)).astype(f)
    scale = np.power(base[None, :], power[:, None]).astype(f)
    scale = np.concatenate([scale, scale], -1)
    sign = np.where(np.arange(HD) < HD // 2, -1.0, 1.0).astype(f)[None, :]
    cos, sin = np.cos(freqs).astype(f), np.sin(freqs).astype(f) * sign
    inv = (f(1.0) / scale).astype(f)
    tabs = np.stack([cos * scale, sin * scale, cos * inv, sin * inv], 1).astype(f)
    rope = np.ascontiguousarray(tabs.reshape(NT, P, 4, HD).transpose(1, 0, 2, 3))
    q = np.arange(P)[:, None] % W
    k = np.arange(2 * W)[None, :]
    seen = (k >= q) & (k <= q + W)
    NW = TOK // W // 2
    mask = np.zeros((P, 2, NW, 2, 2 * W), f)
    for h in range(2):
        for w in range(NW):
            ok = seen & (k >= W) if (h == 0 and w == 0) else seen
            mask[:, h, w] = np.where(ok, 0.0, MASKED)[:, None, :]
    return rope, mask.reshape(P, 2, 512)


def local_weights(inp, pre, names):
    wqkv, qs, ks, wo, g, b, w1, b1, w2, b2 = (np.asarray(inp[pre + n]) for n in names)
    depth = wqkv.shape[0]
    b1t = np.zeros((depth, P, 2 * HCH), b1.dtype)
    w2t = np.zeros((depth, P, HCH, CH), w2.dtype)
    for c in range(HCH):
        n = min(P, HID - c * P)
        for a in range(2):
            b1t[:, :n, a * HCH + c] = b1[:, a * HID + c * P:a * HID + c * P + n]
        w2t[:, :n, c] = w2[:, c * P:c * P + n]
    w2t[:, HLAST, HCH - 1] = b2
    return {"Wqkv": wqkv, "Wo": wo, "qks": np.stack([qs, ks], 1), "W1": w1, "W2": w2t, "b1": b1t,
            "gb": np.stack([g, b], 2)}


def grouped_weights(inp):
    wq, bq, wu, bu = (np.asarray(inp["L0_attn_" + n]) for n in ("wq", "bq", "wu", "bu"))
    wt = np.zeros((CH, 16, P), wq.dtype)
    wt[:, :, :8] = wq.T.reshape(CH, 16, 8)
    bt = np.zeros((P, 16), bq.dtype)
    bt[:8] = bq.reshape(16, 8).T
    return {"wq": wt, "bq": bt, "wu": np.ascontiguousarray(wu.T), "bu": bu[None, :]}


def swiglu_weights(inp):
    wg, wu, wd = (np.asarray(inp["L1_ffn_" + n]) for n in ("w_gate", "w_up", "w_down"))
    return {"w_gate": np.ascontiguousarray(wg.T), "w_up": np.ascontiguousarray(wu.T),
            "w_down": np.ascontiguousarray(wd.T.reshape(3, P, CH).transpose(1, 0, 2).reshape(P, 3 * CH))}


def chunk_weights(inp):
    f = np.float32
    inv_freq = (f(1.0) / np.power(f(10000.0), np.arange(0, 8, 2, dtype=f) / f(8))).astype(f)
    freqs = np.outer(np.arange(64, dtype=f), inv_freq).astype(f)
    cos, sin = np.tile(np.cos(freqs).astype(f), (2, 1)), np.tile(np.sin(freqs).astype(f), (2, 1))
    rope = np.stack([np.concatenate([cos, cos], 1), np.concatenate([sin, -sin], 1)], 1)
    head = (np.arange(P)[:, None] // 8 == np.arange(16)[None, :]).astype(f)
    return {"w_attn": np.ascontiguousarray(np.asarray(inp["L1_attn_w_attn"]).T),
            "w_proj": np.ascontiguousarray(np.asarray(inp["L1_attn_w_proj"]).T), "rope": rope, "headmask": head}


def latent_weights(inp):
    w = {n: np.asarray(inp["L3_attn_" + n]) for n in ("W_basis", "W_v", "W_o", "b_v", "b_o")}
    causal = np.where(np.arange(P)[None, :] <= np.arange(P)[:, None], 0.0, MASKED).astype(np.float32)
    return {"W_basis": np.ascontiguousarray(w["W_basis"].T), "W_v": np.ascontiguousarray(w["W_v"].T),
            "W_o": np.ascontiguousarray(w["W_o"].T), "b_v": w["b_v"][None, :], "b_o": w["b_o"][None, :],
            "causal": causal}


def memory_weights(inp):
    g = {n[8:]: np.asarray(v) for n, v in inp.items() if n.startswith("L2_attn_")}
    dt = g["reg_val_w"].dtype
    wt, tb = np.zeros((CH, 48 + 2 * CH), dt), np.zeros((48 + 2 * CH,), dt)
    for at, n in ((0, "reg_addr"), (8, "reg_gate"), (9, "mem_gate"), (32, "mem_addr"), (48, "reg_val"),
                  (48 + CH, "mem_val")):
        w, b = g[n + "_w"], g[n + "_b"]
        wt[:, at:at + w.shape[0]] = w.T
        tb[at:at + w.shape[0]] = b
    four = ("reg_val", "reg_q", "mem_val", "mem_q")
    s, t = np.arange(P)[:, None], np.arange(TOK)[None, :]
    blocks = []
    for d in (1.0, 0.995):
        first = np.where(s <= t, np.power(d, np.maximum(t - s, 0)), 0.0)
        second = np.where(s + P <= t[:, P:], np.power(d, np.maximum(t[:, P:] - s - P, 0)), 0.0)
        blocks.append(np.concatenate([first, second], 1))
    return {"wt": wt, "tokb": tb, "wc": np.stack([g[n + "_w"].T for n in four], 1),
            "chb": np.stack([g[n + "_b"] for n in four], 1),
            "wm": g["comb_w"].T.reshape(3, CH, CH).transpose(1, 0, 2), "combb": g["comb_b"][None, :],
            "gbr": np.stack([g["ln_g"], g["ln_b"]]), "decay": np.stack(blocks, 1).astype(np.float32)}


def routed_weights(inp):
    w = {n: np.asarray(inp["L3_ffn_" + n]) for n in ("Wr", "br", "W1", "b1", "W2", "b2")}
    b2 = np.zeros((16, 8, 16, CH), w["b2"].dtype)
    for t in range(16):
        b2[t, :, t] = w["b2"]
    rank = np.broadcast_to(np.arange(8, 0, -1, dtype=np.float32), (P, 8))
    return {"Wr": w["Wr"], "br": w["br"], "W1": w["W1"], "W2": w["W2"], "rank": rank,
            "b1": w["b1"].reshape(8, 4, P).transpose(2, 0, 1).reshape(P, 32), "b2": b2.reshape(P, 16 * CH)}


L0_FFN = ("Wqkv", "q_scale", "k_scale", "Wo", "ln_g", "ln_b", "W1", "b1", "W2", "b2")
L2_FFN = ("wqkv", "q_scale", "k_scale", "wo", "ln_g", "ln_b", "w1", "b1", "w2", "b2")


def add_stream(nc, name, x, z):
    with nc.semaphore(f"{name}_added") as added, nc.Block() as block:
        @block.vector
        def _(dve):
            for part in range(2):
                tiles = slice(part * SEQ, (part + 1) * SEQ)
                dve.tensor_tensor(out=x[:, tiles, :], in0=x[:, tiles, :], in1=z[:, tiles, :], op=ALU.add)\
                   .then_inc(added, 1)
            dve.wait_ge(added, 2)


def clear_semaphores(nc):
    given_back = sorted(int(s) for s in nc.released_uncleared_semaphores)
    first = [s for s in given_back if s - 1 not in given_back]
    last = [s for s in given_back if s + 1 not in given_back]
    with nc.Block() as block:
        @block.gpsimd
        def _(pool):
            for a, b in zip(first, last):
                pool.sem_clear(range(a, b + 1))


def build_program(nc, dram, out):
    scratch = nc.dram_tensor("group_scratch_dram", (SEQ, TOK * CH), F32, kind="Internal").ap()

    def wts(module):
        return {n[len(module) + 1:]: ap for n, ap in dram.items() if n.startswith(module + "_")}

    with ExitStack() as whole:
        def sb(n, shape, dt=F32, ctx=whole):
            return ctx.enter_context(nc.sbuf_tensor(n, shape, dt))

        x, ident, identb = sb("x_sb", [P, SEQ * NT, CH]), sb("ident_sb", [P, P]), sb("identb_sb", [P, P], BF16)
        psum = [whole.enter_context(nc.psum_tensor(f"bank{i}", [P, 512], F32)) for i in range(8)]
        loaded, rounded, stored = (whole.enter_context(nc.semaphore(n)) for n in ("loaded", "rounded", "stored"))

        with nc.Block() as block:
            @block.sync
            def _(sp):
                sp.dma_start(x[:], dram["x"].rearrange("b (t p) c -> p (b t) c", p=P)).then_inc(loaded, 16)
                sp.dma_start(ident[:], dram["ident"]).then_inc(loaded, 16)
                sp.wait_ge(loaded, 32)

            @block.vector
            def _(dve):
                dve.wait_ge(loaded, 32)
                dve.tensor_copy(identb[:], ident[:]).then_inc(rounded, 1)
                dve.wait_ge(rounded, 1)

        with ExitStack() as own:
            zT = sb("z0T", [P, SEQ * TOK], ctx=own)
            norm_stream(nc, "n0", x, None, zT, ident, psum)
            grouped_attention(nc, "ga", x, zT, wts("ga"), scratch, ident, psum)
        with ExitStack() as own:
            z = sb("z1", [P, SEQ * NT, CH], ctx=own)
            norm_stream(nc, "n1", x, z, None, ident, psum)
            local_stack(nc, "lo", z, 32, 16, 6, wts("lo"), {"ident": ident, "identb": identb}, psum)
            add_stream(nc, "lo_x", x, z)
        clear_semaphores(nc)
        with ExitStack() as own:
            zT = sb("z2T", [P, SEQ * TOK], ctx=own)
            norm_stream(nc, "n2", x, None, zT, ident, psum)
            chunk_attention(nc, "ca", x, zT, wts("ca"), ident, psum)
            norm_stream(nc, "n3", x, None, zT, ident, psum)
            gated_feed(nc, "gf", x, zT, wts("gf"), psum)
            with ExitStack() as inner:
                z = sb("z4", [P, SEQ * NT, CH], ctx=inner)
                norm_stream(nc, "n4", x, z, zT, ident, psum)
                memory_attention(nc, "ma", x, z, zT, wts("ma"), ident, psum)
        clear_semaphores(nc)
        with ExitStack() as own:
            z = sb("z5", [P, SEQ * NT, CH], ctx=own)
            norm_stream(nc, "n5", x, z, None, ident, psum)
            local_stack(nc, "lt", z, 64, 8, 2, wts("lt"), {"ident": ident, "identb": identb}, psum)
            add_stream(nc, "lt_x", x, z)
        clear_semaphores(nc)
        with ExitStack() as own:
            zT = sb("z6T", [P, SEQ * TOK], ctx=own)
            norm_stream(nc, "n6", x, None, zT, ident, psum)
            latent_attention(nc, "la", x, zT, wts("la"), ident, identb, psum)
            norm_stream(nc, "n7", x, None, zT, ident, psum)
            routed_feed(nc, "rf", x, zT, wts("rf"), ident, psum)

        with nc.Block() as block:
            @block.sync
            def _(sp):
                sp.dma_start(out.rearrange("b (t p) c -> p (b t) c", p=P), x[:]).then_inc(stored, 16)
                sp.wait_ge(stored, 16)
    return nc


def host_arrays(inp):
    arrays = {"x": np.asarray(inp["L0_attn_x"]), "ident": np.eye(P, dtype=np.float32)}
    modules = {"ga": grouped_weights(inp), "lo": local_weights(inp, "L0_ffn_", L0_FFN), "ca": chunk_weights(inp),
               "gf": swiglu_weights(inp), "ma": memory_weights(inp), "lt": local_weights(inp, "L2_ffn_", L2_FFN),
               "la": latent_weights(inp), "rf": routed_weights(inp)}
    for name, window in (("lo", 32), ("lt", 64)):
        modules[name]["rope"], modules[name]["mask"] = local_constants(window)
    for name, module in modules.items():
        arrays.update({f"{name}_{n}": a for n, a in module.items()})
    return {n: np.ascontiguousarray(a) for n, a in arrays.items()}


def kernel(**inputs):
    import concourse.bacc as _bacc
    from concourse.bass_utils import run_bass_kernel_spmd as _run

    nc = _bacc.Bacc("TRN2", target_bir_lowering=False, num_devices=1)
    arrays = {f"in_{n}_dram": a for n, a in host_arrays(inputs).items()}
    dram = {n[3:-5]: nc.dram_tensor(n, a.shape, mybir.dt.from_np(a.dtype), kind="ExternalInput").ap()
            for n, a in arrays.items()}
    out = nc.dram_tensor("out_0_dram", (SEQ, TOK, CH), F32, kind="ExternalOutput").ap()
    build_program(nc, dram, out)
    r = _run(nc, [arrays], core_ids=[0])
    return r.results[0]["out_0_dram"]
```

```python
from contextlib import ExitStack

import numpy as np

import concourse.bass as bass
from concourse import mybir

F32 = mybir.dt.float32
BF16 = mybir.dt.bfloat16
I32 = mybir.dt.int32
ALU = mybir.AluOpType
ACT = mybir.ActivationFunctionType
AX = mybir.AxisListType

P = 128
CH = 128
SEQ = 16
TOK = 256
NT = TOK // P
HD = 64
HID = 341
HCH = 3
HLAST = HID - 2 * P
MASKED = -1.0e37
EPS = 1e-5


class Count:

    def __init__(self, sem, per, credit=None):
        self.sem, self.per = sem, per
        self.credit = per if credit is None else credit

    def done(self, turn, m=0):
        return turn * self.per + (self.credit + m + 1)

    def prev(self, turn, m=0):
        return turn * self.per + (self.credit + m + 1 - self.per)


def hold(eng, sem, value, passed):
    eng.wait_ge(sem, value)
    eng.sem_inc(passed, 1)


def fresh(ap, n):
    return ap.rearrange("p (a b) -> p a b", b=n)


def norm_stream(nc, name, x, z, zT, ident, psum):
    GR = 4
    NG = SEQ * NT // GR
    with ExitStack() as ctx:
        def sem(n):
            return ctx.enter_context(nc.semaphore(f"{name}_{n}"))

        stats = ctx.enter_context(nc.sbuf_tensor(f"{name}_stats", [P, 2, GR, 6], F32))
        mv = ctx.enter_context(nc.sbuf_tensor(f"{name}_mv", [P, 2, GR, 2], F32))
        ve = ctx.enter_context(nc.sbuf_tensor(f"{name}_ve", [P, 2, GR], F32))
        rstd = ctx.enter_context(nc.sbuf_tensor(f"{name}_rstd", [P, 2, GR], F32))
        power = ctx.enter_context(nc.sbuf_tensor(f"{name}_pow", [P, GR], F32))
        zs = ctx.enter_context(nc.sbuf_tensor(f"{name}_zs", [P, 2, GR, CH], F32))
        stats_ready = Count(sem("stats"), 2)
        mv_ready = Count(sem("mv"), 2)
        ve_ready = Count(sem("ve"), 2)
        rstd_ready = Count(sem("rstd"), 2)
        z_ready = Count(sem("z"), 2)
        power_ready = sem("power")
        dve_passed, pool_passed = sem("dve_passed"), sem("pool_passed")
        turned = Count(sem("turned"), 2)
        zt_ready = Count(sem("zt"), 2)

        with nc.Block() as block:
            @block.vector
            def _(dve):
                for s in (stats_ready, mv_ready, z_ready):
                    dve.sem_inc(s.sem, s.credit)

                def statistics(g, h):
                    for k in range(GR):
                        last = dve.bn_stats(stats[:, h, k, :], x[:, bass.ds(g * 2 * GR + (h * GR + k), 1), :]
                                            .rearrange("p a c -> p (a c)"))
                    last.then_inc(stats_ready.sem, 1)
                    hold(dve, stats_ready.sem, stats_ready.done(g, h), dve_passed)
                    for k in range(GR):
                        last = dve.bn_aggr(mv[:, h, k, :], stats[:, h, k, :])
                    last.then_inc(mv_ready.sem, 1)

                def normalise(g, h):
                    dve.wait_ge(rstd_ready.sem, rstd_ready.done(g, h))
                    if zT is not None:
                        dve.wait_ge(turned.sem, turned.prev(g, h))
                    for k in range(GR):
                        tile = bass.ds(g * 2 * GR + (h * GR + k), 1)
                        for dst in ([] if z is None else [z[:, tile, :].rearrange("p a c -> p (a c)")]) + \
                                ([] if zT is None else [zs[:, h, k, :]]):
                            last = dve.tensor_scalar(dst, x[:, tile, :].rearrange("p a c -> p (a c)"),
                                                     mv[:, h, k, 0:1], rstd[:, h, k:k + 1],
                                                     ALU.subtract, ALU.mult)
                    last.then_inc(z_ready.sem, 1)

                statistics(0, 0)
                with dve.Fori(0, NG // 2 - 1) as g:
                    statistics(g, 1)
                    normalise(g, 0)
                    statistics(g + 1, 0)
                    normalise(g, 1)
                statistics(NG // 2 - 1, 1)
                normalise(NG // 2 - 1, 0)
                normalise(NG // 2 - 1, 1)

            @block.gpsimd
            def _(pool):
                for s in (ve_ready, rstd_ready):
                    pool.sem_inc(s.sem, s.credit)
                pool.memset(power[:], -0.5).then_inc(power_ready, 1)
                pool.wait_ge(power_ready, 1)
                with pool.Fori(0, NG // 2) as g:
                    for h in range(2):
                        hold(pool, mv_ready.sem, mv_ready.done(g, h), pool_passed)
                        pool.tensor_scalar(ve[:, h, :], mv[:, h, :, 1], EPS, None, ALU.add).then_inc(ve_ready.sem, 1)
                        pool.wait_ge(ve_ready.sem, ve_ready.done(g, h))
                        pool.tensor_tensor(out=rstd[:, h, :], in0=ve[:, h, :], in1=power[:], op=ALU.pow)\
                            .then_inc(rstd_ready.sem, 1)

            if zT is not None:
                @block.tensor
                def _(pe):
                    pe.sem_inc(turned.sem, turned.credit)
                    with pe.Fori(0, NG // 2) as g:
                        for h in range(2):
                            pe.wait_ge(z_ready.sem, z_ready.done(g, h))
                            pe.wait_ge(zt_ready.sem, zt_ready.prev(g, h))
                            for k in range(GR):
                                last = pe.transpose(psum[h][:, k * P:(k + 1) * P], zs[:, h, k, :], ident[:])
                            last.then_inc(turned.sem, 1)

                @block.scalar
                def _(act):
                    act.sem_inc(zt_ready.sem, zt_ready.credit)
                    with act.Fori(0, NG // 2) as g:
                        for h in range(2):
                            act.wait_ge(turned.sem, turned.done(g, h))
                            act.activation(zT[:, bass.ds(g * 2 * GR * P + h * GR * P, GR * P)], psum[h][:], ACT.Copy)\
                               .then_inc(zt_ready.sem, 1)


def local_stack(nc, name, z, W, H, depth, wts, consts, psum, turns=SEQ):
    ident, identb = consts["ident"], consts["identb"]
    INNER = H * HD
    NP = H // 2
    G = P // W
    NW = TOK // W // 2
    K2 = 2 * W
    CW = 512
    QC = INNER // CW
    PC = CW // P
    per_round = ["qkv", "qkv"] if QC == 2 else ["qk", "v"]
    chunks, of_unit = [], []
    for u in range(4):
        of_unit.append(list(range(len(chunks), len(chunks) + len(per_round[u % 2]))))
        chunks += [(u // 2, w, u % 2 if QC == 2 else 0) for w in per_round[u % 2]]
    NC = len(chunks)
    qk = [c for c in range(NC) if chunks[c][1] != "v"]
    vs = [c for c in range(NC) if chunks[c][1] == "v"]
    NQ, NV = len(qk), len(vs)
    qk_of_unit = [[qk.index(c) for c in of_unit[u] if c in qk] for u in range(4)]
    needed = [max(n for v in qk_of_unit[:u + 1] for n in v) for u in range(4)]
    v_done = [max(c for c in vs if chunks[c][0] == t) for t in range(NT)]
    BP = K2 * NW // P
    WB = NW // BP
    VC = HD + 1
    B_QKV, B_S, B_PT, B_O, B_T = (0, 1), (2, 3), 4, (5, 6), 7
    B_Y = B_PT if QC == 2 else B_T

    with ExitStack() as ctx:
        def sb(n, shape, dt=F32):
            return ctx.enter_context(nc.sbuf_tensor(f"{name}_{n}", shape, dt))

        def sem(n):
            return ctx.enter_context(nc.semaphore(f"{name}_{n}"))

        wqkv = sb("wqkv", [P, 3 * INNER])
        wo = sb("wo", [P, NP, CH])
        w1 = sb("w1", [P, 2 * HID])
        w2 = sb("w2", [P, HCH, CH])
        b1 = sb("b1", [P, 2 * HCH])
        gb = sb("gb", [P, 2])
        scales = sb("scales", [P, 2, HD])
        rope = sb("rope", [P, NT, 4, HD])
        table = sb("table", [P, NT, 4, HD])
        maskb = sb("maskb", [P, 2, 512], BF16)
        power = sb("power", [P, 8])
        hs = sb("hs", [P, NT, CH])
        hT = sb("hT", [P, TOK])
        sq = sb("sq", [P, 2, CW])
        ssq = sb("ssq", [P, 4, 8])
        rn = sb("rn", [P, 4, 8])
        qc = sb("qc", [P, 4, CW])
        t1 = sb("t1", [P, 2, CW])
        t2 = sb("t2", [P, 2, CW])
        qr = sb("qr", [P, 4, CW])
        qT = sb("qT", [P, NP, TOK])
        kbd = sb("kbd", [P, NP, 2, NT * (W + P)])
        vtok = sb("vtok", [P, NT, INNER])
        VH = 2 if WB == 2 else 1
        vw = sb("vw", [P, 2 * BP, VH, H, VC])
        mx = sb("mx", [P, 2, NW * 2])
        sd = sb("sd", [P, 2, 512])
        pr = sb("pr", [P, 2, 512])
        pT = sb("pT", [P, 2, 512])
        rd = sb("rd", [P, 2, NW])
        on = sb("on", [P, 2, NW, 2, HD])
        oT = sb("oT", [P, NP, TOK])
        fhs = sb("fhs", [P, 2, NT, CH])
        fst = sb("fst", [P, NT, 6])
        fmv = sb("fmv", [P, NT, 2])
        fve = sb("fve", [P, NT])
        frs = sb("frs", [P, NT])
        fhn = sb("fhn", [P, 2, NT, CH])
        fhT = sb("fhT", [P, TOK])
        gl = sb("gl", [P, 2, HCH, TOK])
        hu = sb("hu", [P, 2, HCH, TOK])

        init = sem("init")
        kbd_zero = sem("kbd_zero")
        mask_ready = sem("mask")
        dve_passed, pool_passed, sp_passed = sem("dve_passed"), sem("pool_passed"), sem("sp_passed")
        pe_passed = sem("pe_passed")
        const_ld = sem("const_ld")
        attn_w = Count(sem("attn_w"), 16 * 3, 0)
        ffn_w = Count(sem("ffn_w"), 16 * 4, 0)
        table_ready = Count(sem("table"), 1, 1)
        hs_ld = Count(sem("hs_ld"), 16 * 3, 0)
        hT_ps = Count(sem("hT_ps"), 1)
        hT_ready = Count(sem("hT"), 1)
        qkv_ready = Count(sem("qkv"), NC)
        copied = Count(sem("copied"), NC)
        sq_ready = Count(sem("sq"), NQ)
        ssq_ready = Count(sem("ssq"), NQ)
        rmax_ready = Count(sem("rmax"), NQ)
        rn_ready = Count(sem("rn"), NQ)
        sum_ready = Count(sem("sum"), NQ)
        t1_ready = Count(sem("t1"), NQ)
        t2_ready = Count(sem("t2"), NQ)
        qr_ready = Count(sem("qr"), NQ)
        qrT_ps = Count(sem("qrT_ps"), NQ)
        qkT_ready = Count(sem("qkT"), NQ)
        s_ready = Count(sem("s"), 4)
        mx_ready = Count(sem("mx"), 4)
        sd_ready = Count(sem("sd"), 4)
        p_ready = Count(sem("p"), 4)
        pT_ps = Count(sem("pT_ps"), 4)
        pT_ready = Count(sem("pT"), 4)
        o_ready = Count(sem("o"), 8)
        rd_ready = Count(sem("rd"), 8)
        on_ready = Count(sem("on"), 8)
        oT_ps = Count(sem("oT_ps"), 4)
        oT_ready = Count(sem("oT"), 4)
        y_ready = Count(sem("y"), NT)
        za_done = Count(sem("za"), NT)
        zf_done = Count(sem("zf"), 1, turns)
        fhs_ld = [Count(sem(f"fhs_ld{par}"), 16 * 3, 0) for par in range(2)]
        fst_ready = Count(sem("fst"), 1)
        fmv_ready = Count(sem("fmv"), 1)
        fve_ready = Count(sem("fve"), 1)
        frs_ready = Count(sem("frs"), 1)
        fhn_ready = Count(sem("fhn"), 1, 2)
        fhT_ps = Count(sem("fhT_ps"), 1, 2)
        fhT_ready = Count(sem("fhT"), 1)
        g_ready = Count(sem("g"), HCH)
        gl_ready = Count(sem("gl"), HCH)
        hu_ready = Count(sem("hu"), HCH, 2 * HCH)
        fy_ready = Count(sem("fy"), 1, 2)
        vdmas, tail = [[], []], None
        for w in range(TOK // W):
            k, blk, half = w // NW, w // WB, w % WB
            for part in range(2):
                tok = W * (w - 1 + part)
                if tok >= 0:
                    row = (half * K2 + part * W) if WB == 2 else part * W
                    piece = (row, blk, half, tok // P, tok % P)
                    if tok // P == k:
                        vdmas[k].append(piece)
                    else:
                        tail = piece
        vw_ld = [Count(sem(f"vw_ld{k}"), 16 * len(vdmas[k]), 1) for k in range(2)]
        tail_ld = Count(sem("tail_ld"), 16, 1)
        NINIT = 7

        def unit_pairs(u):
            return [(u % 2) * G + j for j in range(G)]

        def steps(i, u, new, old, ahead):
            now = (i, u) if new else None
            before1 = ((i, u - 1) if new else None) if u else ((i - 1, 3) if old else None)
            before2 = ((i, u - 2) if new else None) if u >= 2 else ((i - 1, u + 2) if old else None)
            turned = ((i, u + 1) if new else None) if u < 3 else ((i + 1, 0) if ahead else None)
            projected = ((i, u + 2) if new else None) if u < 2 else ((i + 1, u - 2) if ahead else None)
            return now, before1, before2, turned, projected

        def sweep(eng, l, slot, start=()):
            def turn(b, new, old, ahead):
                for u in range(4):
                    slot(l, b, u, new, old, ahead)

            turn(-1, False, False, True)
            turn(0, True, False, True)
            with eng.Fori(0, turns - 2) as b:
                turn(b + 1, True, True, True)
            turn(turns - 1, True, True, False)
            for u in range(4):
                if u < len(start):
                    start[u]()
                slot(l, turns, u, False, True, False)

        def feed_sweep(eng, step):
            with eng.Fori(0, turns // 2 - 1) as j:
                for par in range(2):
                    step(j, j * 2 + par, par, True, True)
            step(turns // 2 - 1, turns - 2, 0, True, False)
            step(turns // 2 - 1, turns - 1, 1, False, False)

        with nc.Block() as block:
            @block.sync
            def _(sp):
                sp.dma_start(rope[:], wts["rope"]).then_inc(const_ld, 16)
                sp.dma_start(sd[:], wts["mask"]).then_inc(const_ld, 16)

                def shifted(b, dst, ld):
                    sp.dma_start(dst[:, :, 0:64], z[:, bass.ds(b * NT, NT), 0:64]).then_inc(ld.sem, 16)
                    sp.dma_start(dst[1:P, :, 64:CH], z[0:P - 1, bass.ds(b * NT, NT), 64:CH]).then_inc(ld.sem, 16)
                    sp.dma_start(dst[0:1, 1, 64:CH], z[P - 1:P, bass.ds(b * NT, 1), 64:CH]
                                 .rearrange("p a c -> p (a c)")).then_inc(ld.sem, 16)

                def load_hs(l, b):
                    i = l * turns + b
                    hold(sp, zf_done.sem, i + 1, sp_passed)
                    hold(sp, hT_ps.sem, hT_ps.prev(i), sp_passed)
                    shifted(b, hs, hs_ld)

                def load_piece(piece, ld):
                    row, blk, half, t, src = piece
                    sp.dma_start(vw[row:row + W, blk, half, :, 0:HD],
                                 vtok[src:src + W, t, :].rearrange("p (h d) -> p h d", d=HD)).then_inc(ld.sem, 16)

                def load_tail(i):
                    hold(sp, copied.sem, copied.done(i, v_done[0]), sp_passed)
                    hold(sp, o_ready.sem, o_ready.prev(i, 7), sp_passed)
                    load_piece(tail, tail_ld)

                def load_vw(i, k):
                    hold(sp, copied.sem, copied.done(i, v_done[k]), sp_passed)
                    hold(sp, o_ready.sem, o_ready.prev(i, 4 * k + 3), sp_passed)
                    for piece in vdmas[k]:
                        load_piece(piece, vw_ld[k])

                def load_fhs(l, b, par):
                    i = l * turns + b
                    hold(sp, za_done.sem, za_done.done(i, 1), sp_passed)
                    hold(sp, fhn_ready.sem, fhn_ready.done(i - 2), sp_passed)
                    shifted(b, fhs[:, par], fhs_ld[par])

                for s in vw_ld + [tail_ld]:
                    sp.sem_inc(s.sem, s.credit)
                def load_attn(l):
                    at = bass.ds(l, 1)
                    sp.dma_start(wqkv[:], wts["Wqkv"][at].rearrange("l k n -> k (l n)")).then_inc(attn_w.sem, 16)
                    sp.dma_start(wo[:], wts["Wo"][at].rearrange("l (a k) n -> k (l a) n", k=P)).then_inc(attn_w.sem, 16)
                    sp.dma_start(scales[:], wts["qks"][at].rearrange("l a d -> (l a) d")
                                 .partition_broadcast(P)).then_inc(attn_w.sem, 16)

                def load_ffn(l):
                    at = bass.ds(l, 1)
                    sp.dma_start(w1[:], wts["W1"][at].rearrange("l k n -> k (l n)")).then_inc(ffn_w.sem, 16)
                    sp.dma_start(w2[:], wts["W2"][at].rearrange("l k a n -> k (l a) n")).then_inc(ffn_w.sem, 16)
                    sp.dma_start(b1[:], wts["b1"][at].rearrange("l k n -> k (l n)")).then_inc(ffn_w.sem, 16)
                    sp.dma_start(gb[:], wts["gb"][at].rearrange("l k n -> k (l n)")).then_inc(ffn_w.sem, 16)

                def turn(l, b, ahead, ahead2):
                    i = l * turns + b
                    load_tail(i)
                    load_vw(i, 1)
                    if ahead2:
                        load_hs(l, b + 2)
                    if ahead:
                        load_vw(i + 1, 0)

                def layer(l, ahead):
                    load_hs(l, 0)
                    hold(sp, zf_done.sem, l * turns + turns, sp_passed)
                    load_ffn(l)
                    load_hs(l, 1)
                    load_vw(l * turns, 0)
                    with sp.Fori(0, turns - 2) as b:
                        turn(l, b, True, True)
                    turn(l, turns - 2, True, False)
                    turn(l, turns - 1, False, False)
                    for par in range(2):
                        load_fhs(l, par, par)
                    with sp.Fori(1, turns // 4) as j:
                        for par in range(2):
                            load_fhs(l, j * 2 + par, par)
                    if ahead:
                        hold(sp, za_done.sem, za_done.done(l * turns + turns - 1, 1), sp_passed)
                        load_attn(l + 1)
                    with sp.Fori(turns // 4, turns // 2) as j:
                        for par in range(2):
                            load_fhs(l, j * 2 + par, par)

                load_attn(0)
                hold(sp, init, NINIT, sp_passed)
                with sp.Fori(0, depth - 1) as l:
                    layer(l, True)
                layer(depth - 1, False)

            @block.gpsimd
            def _(pool):
                pool.memset(power[:], -0.5).then_inc(init, 1)
                pool.memset(hs[:], 0.0).then_inc(init, 1)
                pool.memset(fhs[:], 0.0).then_inc(init, 1)
                pool.memset(vw[:], 0.0).then_inc(init, 1)
                pool.wait_ge(init, 4)
                for half in range(VH):
                    rows = slice(half * 64, half * 64 + 64) if VH == 2 else slice(0, P)
                    pool.memset(vw[rows, :, half, :, HD:VC], 1.0).then_inc(init, 2 // VH)
                pool.wait_ge(init, 6)
                pool.memset(hu[:], 1.0).then_inc(init, 1)
                for s in (rn_ready, t2_ready, fve_ready, frs_ready):
                    pool.sem_inc(s.sem, s.credit)

                def norms(i, n):
                    pool.wait_ge(rmax_ready.sem, rmax_ready.done(i, n))
                    pool.wait_ge(qr_ready.sem, qr_ready.done(i, n - 4))
                    pool.tensor_tensor(out=rn[:, n % 4, :], in0=ssq[:, n % 4, :], in1=power[:], op=ALU.pow)\
                        .then_inc(rn_ready.sem, 1)

                def turn_half(i, n):
                    t, what, _ = chunks[qk[n]]
                    pool.wait_ge(copied.sem, copied.done(i, qk[n]))
                    pool.wait_ge(sum_ready.sem, sum_ready.done(i, n - 2))
                    row = 1 if what == "q" else 3
                    src, dst = fresh(qc[:, n % 4, :], HD), fresh(t2[:, n % 2, :], HD)
                    for a in range(2):
                        o, s = a * 32, 32 - a * 32
                        last = pool.tensor_tensor(
                            out=dst[:, :, o:o + 32], in0=src[:, :, s:s + 32],
                            in1=table[:, t, row, o:o + 32].unsqueeze(1).to_broadcast([P, 8, 32]), op=ALU.mult)
                    last.then_inc(t2_ready.sem, 1)

                def slot(l, b, u, new, old, ahead):
                    _, _, _, _, projected = steps(l * turns + b, u, new, old, ahead)
                    if projected and qk_of_unit[projected[1]]:
                        i, (q, k) = projected[0], qk_of_unit[projected[1]]
                        turn_half(i, q)
                        norms(i, q)
                        turn_half(i, k)
                        norms(i, k)

                def deviation(l, b):
                    i = l * turns + b
                    hold(pool, fmv_ready.sem, fmv_ready.done(i), pool_passed)
                    pool.tensor_scalar(fve[:], fmv[:, :, 1], EPS, None, ALU.add).then_inc(fve_ready.sem, 1)
                    pool.wait_ge(fve_ready.sem, fve_ready.done(i))
                    pool.tensor_tensor(out=frs[:], in0=fve[:], in1=power[:, 0:NT], op=ALU.pow)\
                        .then_inc(frs_ready.sem, 1)

                with pool.Fori(0, depth) as l:
                    pool.wait_ge(table_ready.sem, table_ready.done(l))
                    sweep(pool, l, slot)
                    with pool.Fori(0, turns) as b:
                        deviation(l, b)

            @block.vector
            def _(dve):
                for s in (ssq_ready, rmax_ready, sum_ready, t1_ready, qr_ready, mx_ready, sd_ready, rd_ready, on_ready, za_done,
                          zf_done, fst_ready, fmv_ready, fhn_ready, hu_ready, table_ready):
                    dve.sem_inc(s.sem, s.credit)
                dve.memset(kbd[:], 0.0).then_inc(kbd_zero, 1)
                dve.wait_ge(const_ld, 32)
                dve.tensor_copy(maskb[:].rearrange("p a b -> p (a b)"), sd[:].rearrange("p a b -> p (a b)"))\
                   .then_inc(mask_ready, 1)
                dve.wait_ge(mask_ready, 1)
                dve.wait_ge(init, NINIT)

                def tables(l):
                    dve.wait_ge(attn_w.sem, attn_w.done(l, 47))
                    dve.wait_ge(t2_ready.sem, t2_ready.prev(l * turns, NQ - 1))
                    for w in range(2):
                        for t in range(NT):
                            last = dve.tensor_tensor(out=table[:, t, 2 * w, :], in0=rope[:, t, 2 * w, :],
                                                     in1=scales[:, w, :], op=ALU.mult)
                            for a in range(2):
                                o, s = a * 32, 32 - a * 32
                                last = dve.tensor_tensor(out=table[:, t, 2 * w + 1, o:o + 32],
                                                         in0=rope[:, t, 2 * w + 1, o:o + 32],
                                                         in1=scales[:, w, s:s + 32], op=ALU.mult)
                    last.then_inc(table_ready.sem, 1)
                    dve.wait_ge(table_ready.sem, table_ready.done(l))

                def squares(i, n):
                    dve.wait_ge(sq_ready.sem, sq_ready.done(i, n))
                    dve.wait_ge(rn_ready.sem, rn_ready.done(i, n - 4))
                    dve.tensor_reduce(ssq[:, n % 4, :], fresh(sq[:, n % 2, :], HD), AX.X, ALU.add)\
                       .then_inc(ssq_ready.sem, 1)

                def floor(i, n):
                    hold(dve, ssq_ready.sem, ssq_ready.done(i, n), dve_passed)
                    dve.tensor_scalar(ssq[:, n % 4, :], ssq[:, n % 4, :], 1e-24, None, ALU.max)\
                       .then_inc(rmax_ready.sem, 1)

                def straight(i, n):
                    t, what, _ = chunks[qk[n]]
                    dve.wait_ge(copied.sem, copied.done(i, qk[n]))
                    dve.wait_ge(qr_ready.sem, qr_ready.done(i, n - 2))
                    row = 0 if what == "q" else 2
                    dve.tensor_tensor(out=fresh(t1[:, n % 2, :], HD), in0=fresh(qc[:, n % 4, :], HD),
                                      in1=table[:, t, row, :].unsqueeze(1).to_broadcast([P, 8, HD]), op=ALU.mult)\
                       .then_inc(t1_ready.sem, 1)

                def rotated(i, n):
                    dve.wait_ge(t2_ready.sem, t2_ready.done(i, n))
                    dve.wait_ge(t1_ready.sem, t1_ready.done(i, n))
                    dve.tensor_tensor(out=t1[:, n % 2, :], in0=t1[:, n % 2, :], in1=t2[:, n % 2, :], op=ALU.add)\
                       .then_inc(sum_ready.sem, 1)

                def scaled(i, n):
                    dve.wait_ge(rn_ready.sem, rn_ready.done(i, n))
                    dve.wait_ge(qrT_ps.sem, qrT_ps.done(i, n - 4))
                    dve.wait_ge(sum_ready.sem, sum_ready.done(i, n))
                    dve.tensor_tensor(out=fresh(qr[:, n % 4, :], HD), in0=fresh(t1[:, n % 2, :], HD),
                                      in1=rn[:, n % 4, :].unsqueeze(2).to_broadcast([P, 8, HD]), op=ALU.mult)\
                       .then_inc(qr_ready.sem, 1)

                def row_max(i, u):
                    ps = psum[B_S[u % 2]][:].rearrange("p (a b) -> p a b", b=K2)
                    dve.wait_ge(s_ready.sem, s_ready.done(i, u))
                    dve.tensor_reduce(mx[:, u % 2, :], ps, AX.X, ALU.max).then_inc(mx_ready.sem, 1)

                def subtract(i, u):
                    ps = psum[B_S[u % 2]][:].rearrange("p (a b) -> p a b", b=K2)
                    dve.wait_ge(mx_ready.sem, mx_ready.done(i, u))
                    dve.wait_ge(p_ready.sem, p_ready.done(i, u - 2) if u >= 2 else p_ready.prev(i, u + 2))
                    dve.tensor_tensor(out=sd[:, u % 2, :].rearrange("p (a b) -> p a b", b=K2), in0=ps,
                                      in1=mx[:, u % 2, :].unsqueeze(2).to_broadcast([P, 2 * NW, K2]),
                                      op=ALU.subtract).then_inc(sd_ready.sem, 1)

                def divided(i, u, between=(None, None)):
                    dve.wait_ge(oT_ps.sem, oT_ps.done(i, u - 2) if u >= 2 else oT_ps.prev(i, u + 2))
                    for e in range(2):
                        ps = psum[B_O[e]][:, 0:NW * VC].rearrange("p (w v) -> p w v", v=VC)
                        dve.wait_ge(o_ready.sem, o_ready.done(i, 2 * u + e))
                        dve.reciprocal(rd[:, e, :], ps[:, :, HD]).then_inc(rd_ready.sem, 1)
                        if between[e]:
                            between[e]()
                        dve.wait_ge(rd_ready.sem, rd_ready.done(i, 2 * u + e))
                        dve.tensor_tensor(out=on[:, u % 2, :, e, :], in0=ps[:, :, 0:HD],
                                          in1=rd[:, e, :].unsqueeze(2).to_broadcast([P, NW, HD]), op=ALU.mult)\
                           .then_inc(on_ready.sem, 1)

                def to_stream(b, t, n, bank, ready, value, done):
                    dve.wait_ge(ready.sem, value)
                    zb = z[:, bass.ds(b * NT + t, n), :]
                    dve.tensor_tensor(out=zb, in0=psum[bank][:, 0:n * CH].rearrange("p (t c) -> p t c", c=CH),
                                      in1=zb, op=ALU.add).then_inc(done.sem, 1)

                def slot(l, b, u, new, old, ahead):
                    i = l * turns + b
                    now, before1, _, _, projected = steps(i, u, new, old, ahead)
                    late = ((i, u + 1) if new else None) if u < 3 else ((i + 1, 0) if ahead else None)
                    late = (late[0], qk_of_unit[late[1]]) if late else (0, [])
                    here = qk_of_unit[projected[1]] if projected else []
                    y = (b - 1, u // 2, 1, B_Y, y_ready, y_ready.done(i - 1, u // 2), za_done) \
                        if old and u % 2 == 0 else None
                    end = late[0] if late[1] else None
                    if end is not None:
                        k_end = late[1][1]
                    if here:
                        at, (q, k) = projected[0], here
                    if QC == 2:
                        if end is not None:
                            rotated(end, k_end)
                        if now:
                            row_max(*now)
                        if now:
                            subtract(*now)
                        if end is not None:
                            scaled(end, k_end)
                        if y:
                            to_stream(*y)
                        if here:
                            straight(at, q)
                            squares(at, q)
                            straight(at, k)
                            floor(at, q)
                        if before1:
                            divided(*before1, (lambda: squares(at, k), lambda: floor(at, k)) if here else (None, None))
                        elif here:
                            squares(at, k)
                            floor(at, k)
                        if here:
                            rotated(at, q)
                            scaled(at, q)
                    elif u % 2 == 0:
                        if here:
                            straight(at, q)
                            squares(at, q)
                        if now:
                            row_max(*now)
                        if here:
                            floor(at, q)
                        if now:
                            subtract(*now)
                        if here:
                            straight(at, k)
                        if before1:
                            divided(*before1, (lambda: squares(at, k), lambda: floor(at, k)) if here else (None, None))
                        elif here:
                            squares(at, k)
                            floor(at, k)
                        if here:
                            rotated(at, q)
                            scaled(at, q)
                        if y:
                            to_stream(*y)
                    else:
                        if end is not None:
                            rotated(end, k_end)
                            scaled(end, k_end)
                        if now:
                            row_max(*now)
                            subtract(*now)
                        if before1:
                            divided(*before1)

                def feed_norm(l, pair, b, par):
                    i = l * turns + b
                    dve.wait_ge(fhs_ld[par].sem, fhs_ld[par].done(l * (turns // 2) + pair, 47))
                    for t in range(NT):
                        last = dve.bn_stats(fst[:, t, :], fhs[:, par, t, :])
                    last.then_inc(fst_ready.sem, 1)
                    hold(dve, fst_ready.sem, fst_ready.done(i), dve_passed)
                    for t in range(NT):
                        last = dve.bn_aggr(fmv[:, t, :], fst[:, t, :])
                    last.then_inc(fmv_ready.sem, 1)

                def feed_scale(l, b, par):
                    i = l * turns + b
                    dve.wait_ge(frs_ready.sem, frs_ready.done(i))
                    dve.wait_ge(fhT_ps.sem, fhT_ps.done(i - 2))
                    for t in range(NT):
                        last = dve.tensor_scalar(fhn[:, par, t, :], fhs[:, par, t, :], fmv[:, t, 0:1], frs[:, t:t + 1],
                                                 ALU.subtract, ALU.mult)
                    last.then_inc(fhn_ready.sem, 1)

                def feed(l, b, par):
                    i = l * turns + b
                    dve.wait_ge(fy_ready.sem, fy_ready.done(i - 2))
                    for c in range(HCH):
                        n = P if c < 2 else HLAST
                        dve.wait_ge(gl_ready.sem, gl_ready.done(i, c))
                        dve.scalar_tensor_tensor(out=hu[0:n, par, c, :], in0=psum[3 * par + c][0:n, 0:TOK],
                                                 scalar=b1[0:n, c:c + 1], in1=gl[0:n, par, c, :],
                                                 op0=ALU.add, op1=ALU.mult).then_inc(hu_ready.sem, 1)

                def feed_stream(l, b):
                    to_stream(b, 0, NT, 6, fy_ready, fy_ready.done(l * turns + b), zf_done)

                def feed_start(l, par):
                    feed_norm(l, 0, par, par)
                    feed_scale(l, par, par)

                def feed_step(l, pair, b, par, ahead, ahead2):
                    if ahead2:
                        feed_norm(l, pair + 1, b + 2, par)
                    feed(l, b, par)
                    if ahead2:
                        feed_scale(l, b + 2, par)
                    feed_stream(l, b)

                with dve.Fori(0, depth) as l:
                    tables(l)
                    sweep(dve, l, slot, (lambda: hold(dve, ffn_w.sem, ffn_w.done(l, 63), dve_passed),
                                         lambda: feed_start(l, 0), lambda: feed_start(l, 1)))
                    feed_sweep(dve, lambda *step: feed_step(l, *step))

            @block.scalar
            def _(act):
                for s in (hT_ready, copied, sq_ready, qkT_ready, p_ready, pT_ready, oT_ready, fhT_ready, gl_ready):
                    act.sem_inc(s.sem, s.credit)
                act.wait_ge(kbd_zero, 1)
                act.wait_ge(init, NINIT)

                def copy_hT(i):
                    act.wait_ge(hT_ps.sem, hT_ps.done(i))
                    act.wait_ge(qkv_ready.sem, qkv_ready.prev(i, NC - 1))
                    act.activation(hT[:], psum[B_T][:, 0:TOK], ACT.Copy).then_inc(hT_ready.sem, 1)

                def copy_chunk(i, c):
                    t, what, j = chunks[c]
                    act.wait_ge(qkv_ready.sem, qkv_ready.done(i, c))
                    if what == "v":
                        act.wait_ge(vw_ld[t].sem, vw_ld[t].prev(i, vw_ld[t].per - 1))
                        if t == 0:
                            act.wait_ge(tail_ld.sem, tail_ld.prev(i, 15))
                        dst = vtok[:, t, j * CW:(j + 1) * CW]
                    else:
                        n = qk.index(c)
                        act.wait_ge(t1_ready.sem, t1_ready.done(i, n - 4))
                        act.wait_ge(t2_ready.sem, t2_ready.done(i, n - 4))
                        dst = qc[:, n % 4, :]
                    act.activation(dst, psum[B_QKV[c % 2]][:], ACT.Copy).then_inc(copied.sem, 1)
                    if what != "v":
                        act.wait_ge(ssq_ready.sem, ssq_ready.done(i, n - 2))
                        act.activation(sq[:, n % 2, :], psum[B_QKV[c % 2]][:], ACT.Square).then_inc(sq_ready.sem, 1)

                def copy_qk(i, n):
                    t, what, j = chunks[qk[n]]
                    act.wait_ge(qrT_ps.sem, qrT_ps.done(i, n))
                    act.wait_ge(s_ready.sem, s_ready.prev(i, 2 + j if QC == 2 else 3))
                    src = psum[B_T][:].rearrange("p (a b) -> p a b", b=P)
                    pairs = slice(j * PC, (j + 1) * PC)
                    if what == "q":
                        act.activation(qT[:, pairs, t * P:(t + 1) * P], src, ACT.Copy, scale=8.0)\
                           .then_inc(qkT_ready.sem, 1)
                        return
                    at = t * (W + P) + W
                    for e in range(2):
                        rows = slice(e * 64, e * 64 + 64)
                        last = act.activation(kbd[rows, pairs, e, at:at + P], src[rows], ACT.Copy)
                        if t == 0:
                            last = act.activation(kbd[rows, pairs, e, at + P:at + P + W], src[rows, :, P - W:P], ACT.Copy)
                    last.then_inc(qkT_ready.sem, 1)

                def exponentials(i, u):
                    act.wait_ge(sd_ready.sem, sd_ready.done(i, u))
                    act.wait_ge(pT_ps.sem, pT_ps.done(i, u - 2) if u >= 2 else pT_ps.prev(i, u + 2))
                    act.activation(pr[:, u % 2, :].rearrange("p (e w k) -> p w e k", e=2, w=NW),
                                   sd[:, u % 2, :].rearrange("p (w e k) -> p w e k", e=2, w=NW), ACT.Exp)\
                       .then_inc(p_ready.sem, 1)

                def copy_pT(i, u):
                    act.wait_ge(pT_ps.sem, pT_ps.done(i, u))
                    act.wait_ge(o_ready.sem, o_ready.done(i, 2 * u - 3) if u >= 2 else o_ready.prev(i, 2 * u + 5))
                    act.activation(pT[:, u % 2, :], psum[B_PT][:], ACT.Copy).then_inc(pT_ready.sem, 1)

                def copy_oT(i, u):
                    k, r = u // 2, u % 2
                    act.wait_ge(oT_ps.sem, oT_ps.done(i, u))
                    act.wait_ge(y_ready.sem, y_ready.prev(i, k))
                    act.activation(oT[:, r * G:(r + 1) * G, k * P:(k + 1) * P].rearrange("p j (w q) -> p w j q", q=W),
                                   psum[B_PT][:, 0:NW * P].rearrange("p (w j q) -> p w j q", w=NW, q=W),
                                   ACT.Copy).then_inc(oT_ready.sem, 1)

                def slot(l, b, u, new, old, ahead):
                    i = l * turns + b
                    now, before1, before2, turned, projected = steps(i, u, new, old, ahead)
                    t = qk_of_unit[turned[1]] if turned else []
                    c = of_unit[projected[1]] if projected else []
                    if QC == 2:
                        if u == 2 and ahead:
                            copy_hT(i + 1)
                        if t:
                            copy_qk(turned[0], t[0])
                        if c:
                            copy_chunk(projected[0], c[0])
                        if before1:
                            copy_pT(*before1)
                        if c:
                            copy_chunk(projected[0], c[1])
                        if now:
                            exponentials(*now)
                        if t:
                            copy_qk(turned[0], t[1])
                        if c:
                            copy_chunk(projected[0], c[2])
                    else:
                        for k in c:
                            copy_chunk(projected[0], k)
                        if u == 1 and ahead:
                            copy_hT(i + 1)
                        if before1:
                            copy_pT(*before1)
                        if t:
                            copy_qk(turned[0], t[0])
                        if now:
                            exponentials(*now)
                        if t:
                            copy_qk(turned[0], t[1])
                    if before2:
                        copy_oT(*before2)

                def copy_fhT(l, b):
                    i = l * turns + b
                    act.wait_ge(fhT_ps.sem, fhT_ps.done(i))
                    act.wait_ge(g_ready.sem, g_ready.prev(i, HCH - 1))
                    act.activation(fhT[:], psum[B_T][:, 0:TOK], ACT.Identity, bias=gb[:, 1:2], scale=gb[:, 0:1])\
                       .then_inc(fhT_ready.sem, 1)

                def gates(l, b, par):
                    i = l * turns + b
                    for c in range(HCH):
                        n = P if c < 2 else HLAST
                        act.wait_ge(g_ready.sem, g_ready.done(i, c))
                        act.wait_ge(hu_ready.sem, hu_ready.done(i - 2, c))
                        act.activation(gl[0:n, par, c, :], psum[3 * par + c][0:n, TOK:2 * TOK], ACT.Gelu,
                                       bias=b1[0:n, HCH + c:HCH + c + 1]).then_inc(gl_ready.sem, 1)

                def feed_step(l, pair, b, par, ahead, ahead2):
                    if ahead:
                        gates(l, b + 1, 1 - par)
                    if ahead2:
                        copy_fhT(l, b + 2)

                with act.Fori(0, depth) as l:
                    sweep(act, l, slot, (lambda: act.wait_ge(ffn_w.sem, ffn_w.done(l, 63)), lambda: copy_fhT(l, 0),
                                         lambda: gates(l, 0, 0), lambda: copy_fhT(l, 1)))
                    feed_sweep(act, lambda *step: feed_step(l, *step))

            @block.tensor
            def _(pe):
                for s in (hT_ps, qkv_ready, qrT_ps, s_ready, pT_ps, o_ready, oT_ps, y_ready, fhT_ps, g_ready, fy_ready):
                    pe.sem_inc(s.sem, s.credit)
                pe.wait_ge(mask_ready, 1)
                pe.wait_ge(kbd_zero, 1)
                pe.wait_ge(init, NINIT)

                def turn_h(i, free):
                    pe.wait_ge(hs_ld.sem, hs_ld.done(i, 47))
                    pe.wait_ge(*free)
                    for t in range(NT):
                        last = pe.transpose(psum[B_T][:, t * P:(t + 1) * P], hs[:, t, :], ident[:])
                    last.then_inc(hT_ps.sem, 1)

                def chunk(i, c):
                    t, what, j = chunks[c]
                    if c == 0:
                        pe.wait_ge(hT_ready.sem, hT_ready.done(i))
                    pe.wait_ge(copied.sem, copied.done(i, c - 2))
                    before = (c - 2) % NC
                    if before in qk:
                        n = qk.index(before)
                        pe.wait_ge(sq_ready.sem, sq_ready.done(i, n) if c >= 2 else sq_ready.prev(i, n))
                    col = {"q": 0, "k": INNER, "v": 2 * INNER}[what] + j * CW
                    pe.matmul(psum[B_QKV[c % 2]][:], hT[:, t * P:(t + 1) * P], wqkv[:, col:col + CW],
                              start=True, stop=True).then_inc(qkv_ready.sem, 1)

                def turn_qk(i, n, held):
                    pe.wait_ge(qr_ready.sem, qr_ready.done(i, n))
                    pe.wait_ge(qkT_ready.sem, qkT_ready.done(i, n - 1))
                    if held is not None:
                        pe.wait_ge(held[0].sem, held[0].done(*held[1]))
                    for p in range(PC):
                        last = pe.transpose(psum[B_T][:, p * P:(p + 1) * P], qr[:, n % 4, p * P:(p + 1) * P], ident[:])
                    last.then_inc(qrT_ps.sem, 1)

                def scores(i, u):
                    k = u // 2
                    ps = psum[B_S[u % 2]]
                    pe.wait_ge(qkT_ready.sem, qkT_ready.done(i, needed[u]))
                    pe.wait_ge(sd_ready.sem, sd_ready.done(i, u - 2) if u >= 2 else sd_ready.prev(i, u + 2))
                    pe.matmul(ps[:], identb[:], maskb[:, k, :], start=True, stop=True)
                    psv = ps[:].rearrange("p (w e k) -> p w e k", w=NW, e=2)
                    for w in range(NW):
                        col, key = (k * NW + w) * W, k * (W + P) + w * W
                        for j, pair in enumerate(unit_pairs(u)):
                            last = pe.matmul(psv[j * W:(j + 1) * W, w], qT[:, pair, col:col + W],
                                             kbd[:, pair, :, key:key + K2], start=False,
                                             stop=True, skip_group_check=True)
                    last.then_inc(s_ready.sem, 1)

                def turn_p(i, u, y):
                    pe.wait_ge(p_ready.sem, p_ready.done(i, u))
                    pe.wait_ge(oT_ready.sem, oT_ready.done(i, u - 2))
                    if y is not None:
                        pe.wait_ge(za_done.sem, za_done.done(*y))
                    for n in range(4):
                        last = pe.transpose(psum[B_PT][:, n * P:(n + 1) * P], pr[:, u % 2, n * P:(n + 1) * P], ident[:])
                    last.then_inc(pT_ps.sem, 1)

                def values(i, u):
                    k = u // 2
                    pe.wait_ge(pT_ready.sem, pT_ready.done(i, u))
                    pe.wait_ge(vw_ld[k].sem, vw_ld[k].done(i, vw_ld[k].per - 1))
                    if k == 1:
                        pe.wait_ge(tail_ld.sem, tail_ld.done(i, 15))
                    for e in range(2):
                        m = 2 * u + e
                        pe.wait_ge(on_ready.sem, on_ready.done(i, m - 2) if m >= 2 else on_ready.prev(i, m + 6))
                        for blk in range(BP):
                            for j, pair in enumerate(unit_pairs(u)):
                                c0 = blk * WB * VC
                                lhs = pT[:, u % 2, (e * BP + blk) * P + j * W:(e * BP + blk) * P + (j + 1) * W]
                                last = pe.matmul(
                                    psum[B_O[e]][j * W:(j + 1) * W, c0:c0 + WB * VC]
                                    .rearrange("p (a v) -> p a v", v=VC), lhs,
                                    vw[:, k * BP + blk, :, 2 * pair + e, :],
                                    start=True, stop=True, skip_group_check=True)
                        last.then_inc(o_ready.sem, 1)

                def turn_o(i, u, free):
                    pe.wait_ge(on_ready.sem, on_ready.done(i, 2 * u + 1))
                    pe.wait_ge(*free)
                    for w in range(NW):
                        last = pe.transpose(psum[B_PT][:, w * P:(w + 1) * P],
                                            on[:, u % 2, w].rearrange("p e d -> p (e d)"), ident[:])
                    last.then_inc(oT_ps.sem, 1)

                def out_project(i, t):
                    pe.wait_ge(oT_ready.sem, oT_ready.done(i, 2 * t + 1))
                    pe.wait_ge(za_done.sem, za_done.done(i, t - 1))
                    for pair in range(NP):
                        last = pe.matmul(psum[B_Y][:, 0:CH], oT[:, pair, t * P:(t + 1) * P],
                                         wo[:, pair, :], start=(pair == 0), stop=(pair == NP - 1))
                    last.then_inc(y_ready.sem, 1)

                def slot(l, b, u, new, old, ahead):
                    i = l * turns + b
                    now, before1, before2, turned, projected = steps(i, u, new, old, ahead)
                    t = qk_of_unit[turned[1]] if turned else []
                    c = of_unit[projected[1]] if projected else []
                    if before2:
                        free = (pT_ready.sem, pT_ready.done(*before1)) if before1 else \
                            (oT_ready.sem, oT_ready.done(before2[0], before2[1] - 1))
                    if QC == 2:
                        y = (i - 1, u // 2) if old and u % 2 == 0 else None
                        if now:
                            scores(*now)
                        if y:
                            out_project(*y)
                        if t:
                            turn_qk(turned[0], t[0], (hT_ready, (i + 1, 0)) if ahead and u >= 2 else None)
                        if c:
                            chunk(projected[0], c[0])
                        if before1:
                            turn_p(*before1, y)
                        if c:
                            chunk(projected[0], c[1])
                        if t:
                            turn_qk(turned[0], t[1], None)
                        if before1:
                            values(*before1)
                        if c:
                            chunk(projected[0], c[2])
                        if before2:
                            turn_o(*before2, free)
                        if u == 1 and ahead:
                            turn_h(i + 1, (qkT_ready.sem, qkT_ready.done(i, qk_of_unit[2][1])))
                    elif u % 2 == 0:
                        for k in c:
                            chunk(projected[0], k)
                        if now:
                            scores(*now)
                        if before1:
                            turn_p(*before1, None)
                            values(*before1)
                        if before2:
                            turn_o(*before2, free)
                        if old:
                            if u == 2 and not new:
                                pe.wait_ge(fhT_ready.sem, fhT_ready.done(l * turns))
                            out_project(i - 1, u // 2)
                    else:
                        if now:
                            scores(*now)
                        for k in c:
                            chunk(projected[0], k)
                        held = (za_done, (i - 1, u // 2)) if old else (hT_ready, (i, 0))
                        if u == 1 and ahead:
                            turn_h(i + 1, (held[0].sem, held[0].done(*held[1])))
                            held = (hT_ready, (i + 1, 0))
                        if before1:
                            turn_p(*before1, None)
                        if t:
                            turn_qk(turned[0], t[0], held)
                        if before1:
                            values(*before1)
                        if t:
                            turn_qk(turned[0], t[1], None)
                        if before2:
                            turn_o(*before2, free)

                def turn_f(l, b, par):
                    i = l * turns + b
                    pe.wait_ge(fhn_ready.sem, fhn_ready.done(i))
                    pe.wait_ge(fhT_ready.sem, fhT_ready.prev(i))
                    for t in range(NT):
                        last = pe.transpose(psum[B_T][:, t * P:(t + 1) * P], fhn[:, par, t, :], ident[:])
                    last.then_inc(fhT_ps.sem, 1)

                def hidden(l, b, par):
                    i = l * turns + b
                    pe.wait_ge(fhT_ready.sem, fhT_ready.done(i))
                    for c in range(HCH):
                        n = P if c < 2 else HLAST
                        pe.wait_ge(hu_ready.sem, hu_ready.done(i - 2, c))
                        for a in range(2):
                            last = pe.matmul(psum[3 * par + c][0:n, a * TOK:(a + 1) * TOK],
                                             w1[:, a * HID + c * P:a * HID + c * P + n], fhT[:],
                                             start=True, stop=True)
                        last.then_inc(g_ready.sem, 1)

                def down(l, b, par):
                    i = l * turns + b
                    pe.wait_ge(hu_ready.sem, hu_ready.done(i, HCH - 1))
                    pe.wait_ge(zf_done.sem, zf_done.done(i - 1))
                    for t in range(NT):
                        for c in range(HCH):
                            n = P if c < 2 else HLAST + 1
                            last = pe.matmul(psum[6][:, t * CH:(t + 1) * CH], hu[0:n, par, c, t * P:(t + 1) * P],
                                             w2[0:n, c, :], start=(c == 0), stop=(c == HCH - 1))
                    last.then_inc(fy_ready.sem, 1)

                def start_f(l, par):
                    i = l * turns + turns - 1
                    pe.wait_ge(qkT_ready.sem, qkT_ready.done(i, NQ - 1))
                    if QC == 1:
                        pe.wait_ge(za_done.sem, za_done.done(i, par))
                    turn_f(l, par, par)

                def start_hidden(l):
                    i = l * turns + turns - 1
                    pe.wait_ge(copied.sem, copied.done(i, NC - 1))
                    pe.wait_ge(sq_ready.sem, sq_ready.done(i, NQ - 1))
                    pe.wait_ge(sd_ready.sem, sd_ready.done(i, 2))
                    hidden(l, 0, 0)

                def feed_step(l, pair, b, par, ahead, ahead2):
                    if ahead:
                        hidden(l, b + 1, 1 - par)
                    if ahead2:
                        turn_f(l, b + 2, par)
                    down(l, b, par)

                with pe.Fori(0, depth) as l:
                    pe.wait_ge(zf_done.sem, l * turns + turns)
                    pe.wait_ge(attn_w.sem, attn_w.done(l, 47))
                    sweep(pe, l, slot, (lambda: hold(pe, ffn_w.sem, ffn_w.done(l, 63), pe_passed), lambda: start_f(l, 0),
                                        lambda: start_hidden(l), lambda: start_f(l, 1)))
                    hold(pe, za_done.sem, za_done.done(l * turns + turns - 1, NT - 1), pe_passed)
                    feed_sweep(pe, lambda *step: feed_step(l, *step))


def grouped_attention(nc, name, x, zT, wts, scratch, ident, psum):
    NI = 16
    ROWS = 256
    GR = 16
    GD = 8
    SCALE = float(np.float32(1.0) / np.float32(np.sqrt(CH)))
    B_S, B_PT, B_O, B_OT, B_Q, B_V = (0, 1), (2, 3), 4, 5, 6, 7

    with ExitStack() as ctx:
        def sb(n, shape, dt=F32):
            return ctx.enter_context(nc.sbuf_tensor(f"{name}_{n}", shape, dt))

        def sem(n):
            return ctx.enter_context(nc.semaphore(f"{name}_{n}"))

        wq = sb("wq", [P, GR, P])
        bq = sb("bq", [P, GR])
        wu = sb("wu", [P, CH])
        bu = sb("bu", [1, CH])
        ones = sb("ones", [1, P])
        qT = sb("qT", [P, 2, NI * ROWS])
        v = sb("v", [P, 2, NI * 2, 32])
        mxr = sb("mxr", [P, 2, 2])
        nmx = sb("nmx", [P, 2, 2])
        pr = sb("pr", [P, 2, 2, ROWS])
        pT = sb("pT", [P, 2, 2, ROWS])
        ob = sb("ob", [P, 2, ROWS])
        rd = sb("rd", [P, 2, 4])
        on = sb("on", [P, 2, NI, 2, GD])
        ot = sb("ot", [P, NT, CH])
        oT = sb("oT", [P, TOK])

        w_ld, init = sem("w_ld"), sem("init")
        q_ps = Count(sem("q_ps"), GR // 2)
        q_ready = Count(sem("q"), GR // 2)
        v_ps = Count(sem("v_ps"), 1)
        v_ready = Count(sem("v"), 1)
        s_ready = Count(sem("s"), NI)
        mxr_ready = Count(sem("mxr"), NI)
        nmx_ready = Count(sem("nmx"), NI)
        p_ready = Count(sem("p"), NI)
        pT_ps = Count(sem("pT_ps"), NI)
        pT_ready = Count(sem("pT"), NI)
        o_ready = Count(sem("o"), NI)
        ob_ready = Count(sem("ob"), 4)
        ot_ps = Count(sem("ot_ps"), 4)
        rd_ready = Count(sem("rd"), 4)
        on_ready = Count(sem("on"), 4)
        stored = Count(sem("stored"), 16)
        loaded = Count(sem("loaded"), 16)
        oT_ps = Count(sem("oT_ps"), 1)
        oT_ready = Count(sem("oT"), 1)
        y_ready = Count(sem("y"), 1)
        x_done = Count(sem("x"), 1)
        pe_passed, sp_passed = sem("pe_passed"), sem("sp_passed")

        def rounds(eng, project, turn, close):
            project(0, 0)
            turn(0, 0, True, False)
            with eng.Fori(0, (SEQ - 2) // 2) as j:
                turn(j * 2 + 1, 1, True, True)
                turn(j * 2 + 2, 0, True, True)
            turn(SEQ - 1, 1, False, True)
            close(SEQ - 1)

        with nc.Block() as block:
            @block.sync
            def _(sp):
                sp.sem_inc(stored.sem, stored.credit)
                sp.sem_inc(loaded.sem, loaded.credit)
                for dst, n in ((wq, "wq"), (bq, "bq"), (wu, "wu"), (bu, "bu")):
                    sp.dma_start(dst[:], wts[n]).then_inc(w_ld, 16)

                def turn(b, par, *_):
                    sp.wait_ge(on_ready.sem, on_ready.done(b, 3))
                    sp.dma_start(scratch[bass.ds(b, 1)].rearrange("a (n p d) -> p (a n) d", p=P, d=GD),
                                 on[:, par].rearrange("p n h d -> p (n h) d")).then_inc(stored.sem, 16)
                    hold(sp, stored.sem, stored.done(b, 15), sp_passed)
                    hold(sp, oT_ps.sem, oT_ps.prev(b), sp_passed)
                    sp.dma_start(ot[:], scratch[bass.ds(b, 1)].rearrange("a (t p c) -> p (a t) c", p=P, c=CH))\
                      .then_inc(loaded.sem, 16)

                with sp.Fori(0, SEQ // 2) as j:
                    turn(j * 2, 0)
                    turn(j * 2 + 1, 1)

            @block.gpsimd
            def _(pool):
                pool.memset(v[:], 0.0).then_inc(init, 1)
                pool.memset(ones[:], 1.0).then_inc(init, 1)
                pool.wait_ge(init, 2)
                pool.memset(v[:, :, :, GD:GD + 1], 1.0).then_inc(init, 1)

            @block.tensor
            def _(pe):
                for s in (q_ps, v_ps, s_ready, pT_ps, o_ready, ot_ps, oT_ps, y_ready):
                    pe.sem_inc(s.sem, s.credit)
                pe.wait_ge(w_ld, 64)
                pe.wait_ge(init, 3)

                def groups(b, m):
                    pe.wait_ge(q_ready.sem, q_ready.done(b, m - 1) if m else q_ready.prev(b, GR // 2 - 1))
                    for a in range(2):
                        last = pe.matmul(psum[B_Q][:, a * TOK:(a + 1) * TOK], wq[:, 2 * m + a, :],
                                         zT[:, bass.ds(b * TOK, TOK)], start=True, stop=True)
                    last.then_inc(q_ps.sem, 1)

                def turn_v(b, par, free):
                    pe.wait_ge(q_ready.sem, q_ready.done(b, GR // 2 - 1))
                    hold(pe, *free, pe_passed)
                    for n in range(2 * NI):
                        last = pe.transpose(psum[B_V][:, n * GD:(n + 1) * GD], qT[0:GD, par, n * P:(n + 1) * P],
                                            ident[0:GD, 0:GD])
                    last.then_inc(v_ps.sem, 1)

                def scores(b, par, n):
                    if n == 0:
                        pe.wait_ge(q_ready.sem, q_ready.done(b, GR // 2 - 1))
                    pe.wait_ge(p_ready.sem, p_ready.done(b, n - 2) if n >= 2 else p_ready.prev(b, NI - 2 + n))
                    for h in range(2):
                        last = pe.matmul(psum[B_S[n % 2]][:, h * ROWS:(h + 1) * ROWS],
                                         qT[:, par, n * ROWS + h * P:n * ROWS + (h + 1) * P],
                                         qT[:, par, n * ROWS:(n + 1) * ROWS], start=True, stop=True)
                    last.then_inc(s_ready.sem, 1)

                def turn_p(b, n):
                    pe.wait_ge(p_ready.sem, p_ready.done(b, n))
                    pe.wait_ge(pT_ready.sem, pT_ready.done(b, n - 2) if n >= 2 else pT_ready.prev(b, NI - 2 + n))
                    for kh in range(2):
                        for qh in range(2):
                            last = pe.transpose(psum[B_PT[n % 2]][:, kh * ROWS + qh * P:kh * ROWS + (qh + 1) * P],
                                                pr[:, n % 2, qh, kh * P:(kh + 1) * P], ident[:])
                    last.then_inc(pT_ps.sem, 1)

                def values(b, par, n):
                    c = n % 4
                    pe.wait_ge(pT_ready.sem, pT_ready.done(b, n))
                    if n == 0:
                        pe.wait_ge(v_ready.sem, v_ready.done(b))
                    if c == 0:
                        pe.wait_ge(ob_ready.sem, ob_ready.done(b, n // 4 - 1) if n else ob_ready.prev(b, 3))
                    for kh in range(2):
                        last = pe.matmul(psum[B_O][32 * c:32 * c + 32, 0:ROWS],
                                         v[:, par, 2 * n + kh, :], pT[:, n % 2, kh, :],
                                         start=(kh == 0), stop=(kh == 1))
                    last.then_inc(o_ready.sem, 1)

                def turn_o(b, q):
                    pe.wait_ge(ob_ready.sem, ob_ready.done(b, q))
                    pe.wait_ge(on_ready.sem, on_ready.done(b, q - 1) if q else on_ready.prev(b, 3))
                    for h in range(2):
                        last = pe.transpose(psum[B_OT][:, h * P:(h + 1) * P], ob[:, q % 2, h * P:(h + 1) * P], ident[:])
                    last.then_inc(ot_ps.sem, 1)

                def close_turn(b, v_value):
                    pe.wait_ge(loaded.sem, loaded.done(b, 15))
                    pe.wait_ge(v_ready.sem, v_value)
                    for t in range(NT):
                        last = pe.transpose(psum[B_V][:, t * P:(t + 1) * P], ot[:, t, :], ident[:])
                    last.then_inc(oT_ps.sem, 1)

                def close_project(b):
                    pe.wait_ge(oT_ready.sem, oT_ready.done(b))
                    for t in range(NT):
                        pe.matmul(psum[B_V][:, TOK + t * CH:TOK + (t + 1) * CH], ones[:], bu[:], start=True, stop=False)
                        last = pe.matmul(psum[B_V][:, TOK + t * CH:TOK + (t + 1) * CH], oT[:, t * P:(t + 1) * P], wu[:],
                                         start=False, stop=True)
                    last.then_inc(y_ready.sem, 1)

                def project(b, par):
                    for m in range(GR // 2):
                        groups(b, m)
                    turn_v(b, par, (v_ready.sem, v_ready.prev(b)))

                def turn(b, par, ahead, behind):
                    scores(b, par, 0)
                    for n in range(NI):
                        if n + 1 < NI:
                            scores(b, par, n + 1)
                        if ahead and n % 2:
                            groups(b + 1, n // 2)
                        turn_p(b, n)
                        if n >= 1:
                            values(b, par, n - 1)
                        if n >= 5 and n % 4 == 1:
                            turn_o(b, (n - 5) // 4)
                        if behind and n == 8:
                            close_turn(b - 1, v_ready.done(b))
                        if behind and n == 10:
                            close_project(b - 1)
                    values(b, par, NI - 1)
                    if ahead:
                        turn_v(b + 1, 1 - par, (x_done.sem, x_done.prev(b)))
                    turn_o(b, 3)

                def close(b):
                    close_turn(b, v_ready.done(b))
                    close_project(b)

                rounds(pe, project, turn, close)

            @block.vector
            def _(dve):
                for s in (q_ready, v_ready, mxr_ready, nmx_ready, pT_ready, rd_ready, on_ready, x_done):
                    dve.sem_inc(s.sem, s.credit)
                dve.wait_ge(w_ld, 64)
                dve.wait_ge(init, 3)

                def groups(b, par, m):
                    dve.wait_ge(q_ps.sem, q_ps.done(b, m))
                    for g in (2 * m, 2 * m + 1):
                        last = dve.tensor_scalar(qT[:, par, :].rearrange("p (t g) -> p g t", g=GR)[:, g],
                                                 psum[B_Q][:, (g % 2) * TOK:(g % 2 + 1) * TOK], bq[:, g:g + 1], None,
                                                 ALU.add)
                    last.then_inc(q_ready.sem, 1)

                def copy_v(b, par):
                    dve.wait_ge(v_ps.sem, v_ps.done(b))
                    dve.tensor_copy(v[:, par, :, 0:GD], psum[B_V][:, 0:2 * NI * GD].rearrange("p (n d) -> p n d", d=GD))\
                       .then_inc(v_ready.sem, 1)

                def row_max(b, n):
                    dve.wait_ge(s_ready.sem, s_ready.done(b, n))
                    dve.tensor_reduce(mxr[:, n % 2, :], psum[B_S[n % 2]][:].rearrange("p (h k) -> p h k", h=2),
                                      AX.X, ALU.max).then_inc(mxr_ready.sem, 1)
                    dve.wait_ge(mxr_ready.sem, mxr_ready.done(b, n))
                    dve.wait_ge(p_ready.sem, p_ready.done(b, n - 2) if n >= 2 else p_ready.prev(b, NI - 2 + n))
                    dve.tensor_scalar(nmx[:, n % 2, :], mxr[:, n % 2, :], -SCALE, None, ALU.mult)\
                       .then_inc(nmx_ready.sem, 1)

                def copy_pT(b, n):
                    dve.wait_ge(pT_ps.sem, pT_ps.done(b, n))
                    dve.wait_ge(o_ready.sem, o_ready.done(b, n - 2) if n >= 2 else o_ready.prev(b, NI - 2 + n))
                    dve.tensor_copy(pT[:, n % 2].rearrange("p h k -> p (h k)"), psum[B_PT[n % 2]][:])\
                       .then_inc(pT_ready.sem, 1)

                def divide(b, par, q):
                    ps = psum[B_OT][:, 0:2 * P].rearrange("p (h c r) -> p h c r", h=2, c=4)
                    dve.wait_ge(ot_ps.sem, ot_ps.done(b, q))
                    dve.reciprocal(rd[:], ps[:, :, :, GD]).then_inc(rd_ready.sem, 1)
                    dve.wait_ge(rd_ready.sem, rd_ready.done(b, q))
                    dve.wait_ge(loaded.sem, loaded.prev(b, 15))
                    for h in range(2):
                        last = dve.tensor_tensor(out=on[:, par, 4 * q:4 * q + 4, h, :], in0=ps[:, h, :, 0:GD],
                                                 in1=rd[:, h, :].unsqueeze(2).to_broadcast([P, 4, GD]), op=ALU.mult)
                    last.then_inc(on_ready.sem, 1)

                def close(b):
                    dve.wait_ge(y_ready.sem, y_ready.done(b))
                    xb = x[:, bass.ds(b * NT, NT), :]
                    dve.tensor_tensor(out=xb, in0=psum[B_V][:, TOK:2 * TOK].rearrange("p (t c) -> p t c", c=CH), in1=xb,
                                      op=ALU.add).then_inc(x_done.sem, 1)

                def project(b, par):
                    for m in range(GR // 2):
                        groups(b, par, m)
                    copy_v(b, par)

                def turn(b, par, ahead, behind):
                    row_max(b, 0)
                    for n in range(NI):
                        if n + 1 < NI:
                            row_max(b, n + 1)
                        if ahead and n % 2:
                            groups(b + 1, 1 - par, n // 2)
                        copy_pT(b, n)
                        if n >= 5 and n % 4 == 1:
                            divide(b, par, (n - 5) // 4)
                        if behind and n == 11:
                            close(b - 1)
                    if ahead:
                        copy_v(b + 1, 1 - par)
                    divide(b, par, 3)

                rounds(dve, project, turn, close)

            @block.scalar
            def _(act):
                for s in (p_ready, ob_ready, oT_ready):
                    act.sem_inc(s.sem, s.credit)

                def exponentials(b, n):
                    act.wait_ge(nmx_ready.sem, nmx_ready.done(b, n))
                    act.wait_ge(pT_ps.sem, pT_ps.done(b, n - 2) if n >= 2 else pT_ps.prev(b, NI - 2 + n))
                    for h in range(2):
                        last = act.activation(pr[:, n % 2, h, :], psum[B_S[n % 2]][:, h * ROWS:(h + 1) * ROWS], ACT.Exp,
                                              bias=nmx[:, n % 2, h:h + 1], scale=SCALE)
                    last.then_inc(p_ready.sem, 1)

                def copy_o(b, q):
                    act.wait_ge(o_ready.sem, o_ready.done(b, 4 * q + 3))
                    act.wait_ge(ot_ps.sem, ot_ps.done(b, q - 2) if q >= 2 else ot_ps.prev(b, q + 2))
                    act.activation(ob[:, q % 2, :], psum[B_O][:, 0:ROWS], ACT.Copy)\
                       .then_inc(ob_ready.sem, 1)

                def close(b):
                    act.wait_ge(oT_ps.sem, oT_ps.done(b))
                    act.wait_ge(y_ready.sem, y_ready.prev(b))
                    act.activation(oT[:], psum[B_V][:, 0:TOK], ACT.Copy).then_inc(oT_ready.sem, 1)

                def turn(b, par, ahead, behind):
                    exponentials(b, 0)
                    for n in range(NI):
                        if n + 1 < NI:
                            exponentials(b, n + 1)
                        if n >= 4 and n % 4 == 0:
                            copy_o(b, n // 4 - 1)
                        if behind and n == 9:
                            close(b - 1)
                    copy_o(b, 3)

                rounds(act, lambda b, par: None, turn, close)


def gated_feed(nc, name, x, zT, wts, psum):
    CK, HC = 512, 3
    TURNS = SEQ * TOK // CK
    NTILE = CK // P
    B_G, B_U, B_Y = (0, 1, 2), (3, 4, 5), 6
    with ExitStack() as ctx:
        def sb(n, shape, dt=F32):
            return ctx.enter_context(nc.sbuf_tensor(f"{name}_{n}", shape, dt))

        def sem(n):
            return ctx.enter_context(nc.semaphore(f"{name}_{n}"))

        wi = sb("wi", [P, 3, HC * P], I32)
        wf = sb("wf", [P, 3, HC * P])
        sg = sb("sg", [P, HC, CK])
        h = sb("h", [P, HC, CK])
        w_ld, wf_ready = sem("w_ld"), sem("wf")
        g_ready = Count(sem("g"), HC)
        sg_ready = Count(sem("sg"), HC)
        h_ready = Count(sem("h"), HC)
        y_ready = Count(sem("y"), 1)
        x_done = Count(sem("x"), 1)

        def rounds(eng, up, down):
            for c in range(HC):
                up(0, c)
            with eng.Fori(0, TURNS - 1) as j:
                up(j + 1, 0)
                down(j)
                for c in range(1, HC):
                    up(j + 1, c)
            down(TURNS - 1)

        with nc.Block() as block:
            @block.sync
            def _(sp):
                for n in range(3):
                    sp.dma_start(wi[:, n, :], wts[("w_gate", "w_up", "w_down")[n]]).then_inc(w_ld, 16)

            @block.tensor
            def _(pe):
                for s in (g_ready, y_ready):
                    pe.sem_inc(s.sem, s.credit)
                pe.wait_ge(wf_ready, 1)

                def up(j, c):
                    pe.wait_ge(h_ready.sem, h_ready.prev(j, c))
                    for n, bank in ((0, B_G[c]), (1, B_U[c])):
                        last = pe.matmul(psum[bank][:], wf[:, n, c * P:(c + 1) * P], zT[:, bass.ds(j * CK, CK)],
                                         start=True, stop=True)
                    last.then_inc(g_ready.sem, 1)

                def down(j):
                    pe.wait_ge(h_ready.sem, h_ready.done(j, HC - 1))
                    pe.wait_ge(x_done.sem, x_done.prev(j))
                    for t in range(NTILE):
                        for c in range(HC):
                            last = pe.matmul(psum[B_Y][:, t * CH:(t + 1) * CH], h[:, c, t * P:(t + 1) * P],
                                             wf[:, 2, c * P:(c + 1) * P], start=(c == 0), stop=(c == HC - 1))
                    last.then_inc(y_ready.sem, 1)

                rounds(pe, up, down)

            @block.scalar
            def _(act):
                act.sem_inc(sg_ready.sem, sg_ready.credit)

                def up(j, c):
                    act.wait_ge(g_ready.sem, g_ready.done(j, c))
                    act.wait_ge(h_ready.sem, h_ready.prev(j, c))
                    act.activation(sg[:, c, :], psum[B_G[c]][:], ACT.Silu).then_inc(sg_ready.sem, 1)

                rounds(act, up, lambda j: None)

            @block.vector
            def _(dve):
                for s in (h_ready, x_done):
                    dve.sem_inc(s.sem, s.credit)
                dve.wait_ge(w_ld, 48)
                dve.tensor_scalar(wf[:].rearrange("p a b -> p (a b)"), wi[:].rearrange("p a b -> p (a b)"),
                                  float(np.float32(1.0 / 127.0)), None, ALU.mult).then_inc(wf_ready, 1)

                def up(j, c):
                    dve.wait_ge(sg_ready.sem, sg_ready.done(j, c))
                    dve.wait_ge(y_ready.sem, y_ready.prev(j))
                    dve.tensor_tensor(out=h[:, c, :], in0=psum[B_U[c]][:], in1=sg[:, c, :], op=ALU.mult)\
                       .then_inc(h_ready.sem, 1)

                def down(j):
                    dve.wait_ge(y_ready.sem, y_ready.done(j))
                    xb = x[:, bass.ds(j * NTILE, NTILE), :]
                    dve.tensor_tensor(out=xb, in0=psum[B_Y][:].rearrange("p (t c) -> p t c", c=CH), in1=xb, op=ALU.add)\
                       .then_inc(x_done.sem, 1)

                rounds(dve, up, down)


def chunk_attention(nc, name, x, zT, wts, ident, psum):
    H, D, CK = 16, 8, 64
    NCK = TOK // CK
    NG8 = 2 * H
    VD = D + 1
    SCALE = float(np.float32(1.0 / np.sqrt(D)))
    B_QK, B_T, B_V, B_S, B_PT, B_O, B_Y = 0, 1, 2, (3, 4), 5, 6, 7
    with ExitStack() as ctx:
        def sb(n, shape, dt=F32):
            return ctx.enter_context(nc.sbuf_tensor(f"{name}_{n}", shape, dt))

        def sem(n):
            return ctx.enter_context(nc.semaphore(f"{name}_{n}"))

        wa = sb("wa", [P, 3 * CH])
        wp = sb("wp", [P, CH])
        rope = sb("rope", [P, 2, D])
        headmask = sb("headmask", [P, H])
        zs = sb("zs", [P, TOK])
        zd = sb("zd", [P, NCK, 2, CK])
        qk = sb("qk", [P, 2, NG8, D])
        qkr = sb("qkr", [P, NT, 2, CH])
        qT = sb("qT", [P, NT, 2, P])
        kbd = sb("kbd", [P, NCK, H, CK])
        vbd = sb("vbd", [P, NCK, H // 2, 2, VD])
        mx = sb("mx", [P, 2, 8])
        sd = sb("sd", [P, 2, 512])
        pr = sb("pr", [P, 2, 512])
        pT = sb("pT", [P, 2, 4, P])
        rd = sb("rd", [P, 8])
        on = sb("on", [P, NT, H, D])
        oT = sb("oT", [P, TOK])

        w_ld, init = sem("w_ld"), sem("init")
        zs_ready = Count(sem("zs"), 1)
        qk_ps = Count(sem("qk_ps"), NT)
        rot_ready = Count(sem("rot"), NT)
        qkr_ready = Count(sem("qkr"), NT)
        qkT_ps = Count(sem("qkT_ps"), NT)
        qT_ready = Count(sem("qT"), NT)
        kbd0_ready = Count(sem("kbd0"), NT)
        kbd1_ready = Count(sem("kbd1"), NT)
        v_ps = Count(sem("v_ps"), NT)
        vbd_ready = Count(sem("vbd"), NT)
        s_ready = Count(sem("s"), 4)
        mx_ready = Count(sem("mx"), 4)
        sd_ready = Count(sem("sd"), 4)
        p_ready = Count(sem("p"), 4)
        pT_ps = Count(sem("pT_ps"), 4)
        pT_ready = Count(sem("pT"), 4)
        o_ready = Count(sem("o"), 4)
        rd_ready = Count(sem("rd"), 4)
        on_ready = Count(sem("on"), 4)
        oT_ps = Count(sem("oT_ps"), NT)
        oT_ready = Count(sem("oT"), NT)
        y_ready = Count(sem("y"), NT)
        x_done = Count(sem("x"), NT)
        dve_passed, act_passed, pe_passed = sem("dve_passed"), sem("act_passed"), sem("pe_passed")

        def spread(eng, t, c):
            return eng.tensor_tensor(
                out=kbd[:, 2 * t + c], in0=qT[:, t, 1, c * CK:(c + 1) * CK].unsqueeze(1).to_broadcast([P, H, CK]),
                in1=headmask[:].unsqueeze(2).to_broadcast([P, H, CK]), op=ALU.mult)

        def sweep(eng, slot):
            def turn(b, new, old, ahead):
                for u in range(4):
                    now = (b, u) if new else None
                    before = ((b, u - 1) if new else None) if u else ((b - 1, 3) if old else None)
                    ahead_tile = ((b, 1) if new else None) if u < 2 else ((b + 1, 0) if ahead else None)
                    closing = None
                    if u % 2:
                        closing = ((b, 0) if new else None) if u == 3 else ((b - 1, 1) if old else None)
                    slot(b, u, now, before, ahead_tile, closing, ahead)

            turn(-1, False, False, True)
            turn(0, True, False, True)
            with eng.Fori(0, SEQ - 2) as b:
                turn(b + 1, True, True, True)
            turn(SEQ - 1, True, True, False)
            turn(SEQ, False, True, False)

        with nc.Block() as block:
            @block.sync
            def _(sp):
                for dst, n in ((wa, "w_attn"), (wp, "w_proj"), (rope, "rope"), (headmask, "headmask")):
                    sp.dma_start(dst[:], wts[n]).then_inc(w_ld, 16)

            @block.gpsimd
            def _(pool):
                pool.memset(vbd[:], 0.0).then_inc(init, 1)
                pool.wait_ge(init, 1)
                for e in range(2):
                    pool.memset(vbd[e * CK:(e + 1) * CK, :, :, e, D:VD], 1.0).then_inc(init, 1)
                pool.sem_inc(kbd0_ready.sem, kbd0_ready.credit)
                pool.wait_ge(w_ld, 64)

                def slot(b, u, now, before, tile, closing, ahead):
                    if tile and u % 2:
                        at, t = tile
                        pool.wait_ge(qT_ready.sem, qT_ready.done(at, t))
                        pool.wait_ge(s_ready.sem, s_ready.prev(at, 2 * t + 1))
                        spread(pool, t, 0).then_inc(kbd0_ready.sem, 1)

                sweep(pool, slot)

            @block.tensor
            def _(pe):
                for s in (qk_ps, qkT_ps, v_ps, s_ready, pT_ps, o_ready, oT_ps, y_ready):
                    pe.sem_inc(s.sem, s.credit)
                pe.wait_ge(w_ld, 64)

                def project(b, t):
                    if t == 0:
                        pe.wait_ge(zs_ready.sem, zs_ready.done(b))
                    pe.wait_ge(rot_ready.sem, rot_ready.done(b, t - 1))
                    pe.matmul(psum[B_QK][:, 0:TOK], zs[:, t * P:(t + 1) * P], wa[:, 0:2 * CH],
                              start=True, stop=True).then_inc(qk_ps.sem, 1)
                    pe.wait_ge(vbd_ready.sem, vbd_ready.done(b, t - 1))
                    for c in range(2):
                        last = pe.matmul(psum[B_V][:, c * CH:(c + 1) * CH], zd[:, 2 * t + c].rearrange("p a k -> p (a k)"),
                                         wa[:, 2 * CH:3 * CH], start=True, stop=True)
                    last.then_inc(v_ps.sem, 1)

                def turn_qk(b, t):
                    pe.wait_ge(qkr_ready.sem, qkr_ready.done(b, t))
                    pe.wait_ge(qT_ready.sem, qT_ready.done(b, t - 1))
                    for w in range(2):
                        last = pe.transpose(psum[B_T][:, w * P:(w + 1) * P], qkr[:, t, w, :], ident[:])
                    last.then_inc(qkT_ps.sem, 1)

                def scores(b, u):
                    t, hh = u // 2, u % 2
                    if hh == 0:
                        hold(pe, qT_ready.sem, qT_ready.done(b, t), pe_passed)
                        hold(pe, kbd0_ready.sem, kbd0_ready.done(b, t), pe_passed)
                        hold(pe, kbd1_ready.sem, kbd1_ready.done(b, t), pe_passed)
                    hold(pe, sd_ready.sem, sd_ready.done(b, u - 2), pe_passed)
                    for c in range(2):
                        last = pe.matmul(psum[B_S[u % 2]][c * CK:(c + 1) * CK, :], qT[:, t, 0, c * CK:(c + 1) * CK],
                                         kbd[:, 2 * t + c, hh * 8:hh * 8 + 8, :], start=True, stop=True)
                    last.then_inc(s_ready.sem, 1)

                def turn_p(b, u):
                    pe.wait_ge(p_ready.sem, p_ready.done(b, u))
                    pe.wait_ge(pT_ready.sem, pT_ready.done(b, u - 1))
                    for pair in range(4):
                        last = pe.transpose(psum[B_PT][:, pair * P:(pair + 1) * P], pr[:, u % 2, pair * P:(pair + 1) * P],
                                            ident[:])
                    last.then_inc(pT_ps.sem, 1)

                def values(b, u):
                    t, hh = u // 2, u % 2
                    if hh == 0:
                        hold(pe, vbd_ready.sem, vbd_ready.done(b, t), pe_passed)
                    hold(pe, pT_ready.sem, pT_ready.done(b, u), pe_passed)
                    hold(pe, on_ready.sem, on_ready.done(b, u - 1), pe_passed)
                    for c in range(2):
                        for pair in range(4):
                            last = pe.matmul(psum[B_O][c * CK:(c + 1) * CK, pair * 2 * VD:(pair + 1) * 2 * VD],
                                             pT[:, u % 2, pair, c * CK:(c + 1) * CK],
                                             vbd[:, 2 * t + c, hh * 4 + pair].rearrange("p e d -> p (e d)"),
                                             start=True, stop=True, skip_group_check=True)
                    last.then_inc(o_ready.sem, 1)

                def turn_o(b, t):
                    pe.wait_ge(on_ready.sem, on_ready.done(b, 2 * t + 1))
                    pe.wait_ge(x_done.sem, x_done.done(b, t - 1))
                    pe.transpose(psum[B_Y][:, 0:P], on[:, t].rearrange("p h d -> p (h d)"), ident[:])\
                      .then_inc(oT_ps.sem, 1)

                def out_project(b, t):
                    pe.wait_ge(oT_ready.sem, oT_ready.done(b, t))
                    pe.matmul(psum[B_Y][:, 0:CH], oT[:, t * P:(t + 1) * P], wp[:], start=True, stop=True)\
                      .then_inc(y_ready.sem, 1)

                def slot(b, u, now, before, tile, closing, ahead):
                    if before:
                        turn_p(*before)
                    if closing:
                        turn_o(*closing)
                    if tile and u % 2 == 0:
                        project(*tile)
                    if now:
                        scores(*now)
                    if before:
                        values(*before)
                    if closing:
                        out_project(*closing)
                    if tile and u % 2 == 0:
                        turn_qk(*tile)

                sweep(pe, slot)

            @block.scalar
            def _(act):
                for s in (zs_ready, qT_ready, vbd_ready, p_ready, pT_ready, oT_ready):
                    act.sem_inc(s.sem, s.credit)
                act.wait_ge(init, 3)

                def copy_z(b):
                    act.wait_ge(v_ps.sem, v_ps.prev(b, 1))
                    src = zT[:, bass.ds(b * TOK, TOK)]
                    act.activation(zs[:], src, ACT.Copy)
                    for a in range(2):
                        last = act.activation(zd[:, :, a, :], src.rearrange("p (c k) -> p c k", k=CK), ACT.Copy)
                    last.then_inc(zs_ready.sem, 1)

                def copy_q(b, t):
                    act.wait_ge(qkT_ps.sem, qkT_ps.done(b, t))
                    act.wait_ge(s_ready.sem, s_ready.prev(b, 2 * t + 1))
                    act.activation(qT[:, t].rearrange("p w c -> p (w c)"), psum[B_T][:, 0:2 * P], ACT.Copy)\
                       .then_inc(qT_ready.sem, 1)

                def copy_v(b, t):
                    act.wait_ge(v_ps.sem, v_ps.done(b, t))
                    act.wait_ge(o_ready.sem, o_ready.prev(b, 2 * t + 1))
                    for e in range(2):
                        rows = slice(e * CK, (e + 1) * CK)
                        last = act.activation(
                            vbd[rows, 2 * t:2 * t + 2, :, e, 0:D],
                            psum[B_V][rows, 0:2 * CH].rearrange("p (c h e d) -> p c h e d", c=2, e=2, d=D)[:, :, :, e, :],
                            ACT.Copy)
                    last.then_inc(vbd_ready.sem, 1)

                def exponentials(b, u):
                    act.wait_ge(sd_ready.sem, sd_ready.done(b, u))
                    act.wait_ge(pT_ps.sem, pT_ps.done(b, u - 2))
                    act.activation(pr[:, u % 2, :], sd[:, u % 2, :], ACT.Exp, scale=SCALE).then_inc(p_ready.sem, 1)

                def copy_p(b, u):
                    act.wait_ge(pT_ps.sem, pT_ps.done(b, u))
                    act.wait_ge(o_ready.sem, o_ready.done(b, u - 2))
                    act.activation(pT[:, u % 2].rearrange("p a b -> p (a b)"), psum[B_PT][:], ACT.Copy)\
                       .then_inc(pT_ready.sem, 1)

                def copy_o(b, t):
                    act.wait_ge(oT_ps.sem, oT_ps.done(b, t))
                    act.wait_ge(y_ready.sem, y_ready.prev(b, t))
                    act.activation(oT[:, t * P:(t + 1) * P], psum[B_Y][:, 0:P], ACT.Copy).then_inc(oT_ready.sem, 1)

                def slot(b, u, now, before, tile, closing, ahead):
                    if before:
                        copy_p(*before)
                    if closing:
                        copy_o(*closing)
                    if tile and u % 2 == 0:
                        copy_v(*tile)
                    if now:
                        exponentials(*now)
                    if tile and u % 2 == 0:
                        copy_q(*tile)
                    if u == 1 and ahead:
                        copy_z(b + 1)

                sweep(act, slot)

            @block.vector
            def _(dve):
                for s in (rot_ready, qkr_ready, kbd1_ready, mx_ready, sd_ready, rd_ready, on_ready, x_done):
                    dve.sem_inc(s.sem, s.credit)
                dve.wait_ge(w_ld, 64)

                def rotate(b, t):
                    src = psum[B_QK][:, 0:TOK].rearrange("p (n d) -> p n d", d=D)
                    dve.wait_ge(qk_ps.sem, qk_ps.done(b, t))
                    dve.wait_ge(qkr_ready.sem, qkr_ready.done(b, t - 1))
                    dve.tensor_tensor(out=qk[:, 0], in0=src, in1=rope[:, 0, :].unsqueeze(1).to_broadcast([P, NG8, D]),
                                      op=ALU.mult)
                    for a in range(2):
                        o, s = a * 4, 4 - a * 4
                        last = dve.tensor_tensor(
                            out=qk[:, 1, :, o:o + 4], in0=src[:, :, s:s + 4],
                            in1=rope[:, 1, o:o + 4].unsqueeze(1).to_broadcast([P, NG8, 4]), op=ALU.mult)
                    last.then_inc(rot_ready.sem, 1)
                    dve.wait_ge(rot_ready.sem, rot_ready.done(b, t))
                    dve.wait_ge(qkT_ps.sem, qkT_ps.prev(b, t))
                    dve.tensor_tensor(out=qkr[:, t].rearrange("p w c -> p (w c)"),
                                      in0=qk[:, 0].rearrange("p n d -> p (n d)"),
                                      in1=qk[:, 1].rearrange("p n d -> p (n d)"), op=ALU.add).then_inc(qkr_ready.sem, 1)

                def spread_k(b, t):
                    dve.wait_ge(qT_ready.sem, qT_ready.done(b, t))
                    dve.wait_ge(s_ready.sem, s_ready.prev(b, 2 * t + 1))
                    spread(dve, t, 1).then_inc(kbd1_ready.sem, 1)

                def softmax(b, u):
                    ps = psum[B_S[u % 2]][:].rearrange("p (a b) -> p a b", b=CK)
                    dve.wait_ge(s_ready.sem, s_ready.done(b, u))
                    dve.tensor_reduce(mx[:, u % 2, :], ps, AX.X, ALU.max).then_inc(mx_ready.sem, 1)
                    dve.wait_ge(mx_ready.sem, mx_ready.done(b, u))
                    dve.wait_ge(p_ready.sem, p_ready.done(b, u - 2))
                    dve.tensor_tensor(out=sd[:, u % 2, :].rearrange("p (a b) -> p a b", b=CK), in0=ps,
                                      in1=mx[:, u % 2, :].unsqueeze(2).to_broadcast([P, 8, CK]), op=ALU.subtract)\
                       .then_inc(sd_ready.sem, 1)

                def divided(b, u):
                    t, hh = u // 2, u % 2
                    pso = psum[B_O][:, 0:8 * VD].rearrange("p (h v) -> p h v", v=VD)
                    dve.wait_ge(o_ready.sem, o_ready.done(b, u))
                    dve.reciprocal(rd[:], pso[:, :, D]).then_inc(rd_ready.sem, 1)
                    dve.wait_ge(rd_ready.sem, rd_ready.done(b, u))
                    dve.wait_ge(oT_ps.sem, oT_ps.prev(b, t))
                    dve.tensor_tensor(out=on[:, t, hh * 8:hh * 8 + 8, :], in0=pso[:, :, 0:D],
                                      in1=rd[:].unsqueeze(2).to_broadcast([P, 8, D]), op=ALU.mult)\
                       .then_inc(on_ready.sem, 1)

                def to_stream(b, t):
                    dve.wait_ge(y_ready.sem, y_ready.done(b, t))
                    xb = x[:, bass.ds(b * NT + t, 1), :].rearrange("p a c -> p (a c)")
                    dve.tensor_tensor(out=xb, in0=psum[B_Y][:, 0:CH], in1=xb, op=ALU.add).then_inc(x_done.sem, 1)

                def slot(b, u, now, before, tile, closing, ahead):
                    if tile and u % 2:
                        spread_k(*tile)
                    if tile and u % 2 == 0:
                        rotate(*tile)
                    if now:
                        softmax(*now)
                    if before:
                        divided(*before)
                    if closing:
                        to_stream(*closing)

                sweep(dve, slot)


def latent_attention(nc, name, x, zT, wts, ident, identb, psum):
    R, VD = 64, CH + 1
    SCALE = 0.125
    BLOCKS = ((0, 0), (1, 0), (1, 1))
    B_L, B_V, B_S, B_PT, B_O, B_OT, B_Y = 0, 1, 2, 3, 4, 5, 6
    with ExitStack() as ctx:
        def sb(n, shape, dt=F32):
            return ctx.enter_context(nc.sbuf_tensor(f"{name}_{n}", shape, dt))

        def sem(n):
            return ctx.enter_context(nc.semaphore(f"{name}_{n}"))

        wb = sb("wb", [P, R])
        wv = sb("wv", [P, CH])
        wo = sb("wo", [P, CH])
        bv = sb("bv", [1, CH])
        bo = sb("bo", [1, CH])
        ones = sb("ones", [1, P])
        mask = sb("mask", [P, P])
        maskb = sb("maskb", [P, P], BF16)
        zs = sb("zs", [P, TOK])
        lat = sb("lat", [R, TOK])
        v = sb("v", [P, 2, NT, VD])
        mxr = sb("mxr", [P, NT])
        nmx = sb("nmx", [P, NT])
        pr = sb("pr", [P, 3, P])
        pT = sb("pT", [P, 3, P])
        rd = sb("rd", [P, NT])
        on = sb("on", [P, NT, CH])
        oT = sb("oT", [P, TOK])

        w_ld, init = sem("w_ld"), sem("init")
        names = ("zs", "l_ps", "lat", "v_ps", "v", "s", "mxr", "nmx", "p", "pT_ps", "pT", "o", "rd", "on", "oT_ps",
                 "oT", "y", "x")
        (zs_ready, l_ps, lat_ready, v_ps, v_ready, s_ready, mxr_ready, nmx_ready, p_ready, pT_ps, pT_ready, o_ready,
         rd_ready, on_ready, oT_ps, oT_ready, y_ready, x_done) = (Count(sem(n), 1) for n in names)
        pe_passed = sem("pe_passed")

        def rounds(eng, project, scores, middle, close):
            project(0, 0)
            scores(0)
            with eng.Fori(0, (SEQ - 2) // 2) as j:
                for a in range(2):
                    project(j * 2 + (a + 1), 1 - a)
                    middle(j * 2 + a, a)
                    scores(j * 2 + (a + 1))
                    close(j * 2 + a)
            project(SEQ - 1, 1)
            middle(SEQ - 2, 0)
            scores(SEQ - 1)
            close(SEQ - 2)
            middle(SEQ - 1, 1)
            close(SEQ - 1)

        with nc.Block() as block:
            @block.sync
            def _(sp):
                for dst, n in ((wb, "W_basis"), (wv, "W_v"), (wo, "W_o"), (bv, "b_v"), (bo, "b_o"), (mask, "causal")):
                    sp.dma_start(dst[:], wts[n]).then_inc(w_ld, 16)

            @block.gpsimd
            def _(pool):
                pool.memset(v[:], 1.0).then_inc(init, 1)
                pool.memset(ones[:], 1.0).then_inc(init, 1)

            @block.tensor
            def _(pe):
                for s in (l_ps, v_ps, s_ready, pT_ps, o_ready, oT_ps, y_ready):
                    pe.sem_inc(s.sem, s.credit)
                pe.wait_ge(w_ld, 96)
                pe.wait_ge(init, 3)

                def project(b, par):
                    hold(pe, lat_ready.sem, lat_ready.prev(b), pe_passed)
                    pe.wait_ge(zs_ready.sem, zs_ready.done(b))
                    pe.matmul(psum[B_L][0:R, 0:TOK], wb[:], zs[:], start=True, stop=True).then_inc(l_ps.sem, 1)
                    hold(pe, v_ready.sem, v_ready.prev(b), pe_passed)
                    for t in range(NT):
                        pe.matmul(psum[B_V][:, t * CH:(t + 1) * CH], ones[:], bv[:], start=True, stop=False)
                        last = pe.matmul(psum[B_V][:, t * CH:(t + 1) * CH], zs[:, t * P:(t + 1) * P], wv[:],
                                         start=False, stop=True)
                    last.then_inc(v_ps.sem, 1)

                def scores(b):
                    pe.wait_ge(lat_ready.sem, lat_ready.done(b))
                    pe.wait_ge(p_ready.sem, p_ready.prev(b))
                    for n, (qt, kt) in enumerate(BLOCKS):
                        out = psum[B_S][:, n * P:(n + 1) * P]
                        if qt == kt:
                            pe.matmul(out, identb[:], maskb[:], start=True, stop=False)
                        last = pe.matmul(out, lat[:, qt * P:(qt + 1) * P], lat[:, kt * P:(kt + 1) * P],
                                         start=(qt != kt), stop=True)
                    last.then_inc(s_ready.sem, 1)

                def middle(b, par):
                    pe.wait_ge(p_ready.sem, p_ready.done(b))
                    pe.wait_ge(pT_ready.sem, pT_ready.prev(b))
                    for n in range(3):
                        last = pe.transpose(psum[B_PT][:, n * P:(n + 1) * P], pr[:, n, :], ident[:])
                    last.then_inc(pT_ps.sem, 1)
                    hold(pe, v_ready.sem, v_ready.done(b), pe_passed)
                    pe.wait_ge(pT_ready.sem, pT_ready.done(b))
                    pe.wait_ge(on_ready.sem, on_ready.prev(b))
                    for n, (qt, kt) in enumerate(BLOCKS):
                        last = pe.matmul(psum[B_O][:, qt * VD:(qt + 1) * VD], pT[:, n, :], v[:, par, kt, :],
                                         start=(kt == 0), stop=(kt == qt))
                    last.then_inc(o_ready.sem, 1)

                def close(b):
                    pe.wait_ge(on_ready.sem, on_ready.done(b))
                    pe.wait_ge(oT_ready.sem, oT_ready.prev(b))
                    for t in range(NT):
                        last = pe.transpose(psum[B_OT][:, t * P:(t + 1) * P], on[:, t, :], ident[:])
                    last.then_inc(oT_ps.sem, 1)
                    pe.wait_ge(oT_ready.sem, oT_ready.done(b))
                    pe.wait_ge(x_done.sem, x_done.prev(b))
                    for t in range(NT):
                        pe.matmul(psum[B_Y][:, t * CH:(t + 1) * CH], ones[:], bo[:], start=True, stop=False)
                        last = pe.matmul(psum[B_Y][:, t * CH:(t + 1) * CH], oT[:, t * P:(t + 1) * P], wo[:],
                                         start=False, stop=True)
                    last.then_inc(y_ready.sem, 1)

                rounds(pe, project, scores, middle, close)

            @block.scalar
            def _(act):
                for s in (zs_ready, lat_ready, p_ready, pT_ready, oT_ready):
                    act.sem_inc(s.sem, s.credit)
                act.wait_ge(init, 3)

                def project(b, par):
                    act.wait_ge(v_ps.sem, v_ps.prev(b))
                    act.activation(zs[:], zT[:, bass.ds(b * TOK, TOK)], ACT.Copy).then_inc(zs_ready.sem, 1)
                    act.wait_ge(l_ps.sem, l_ps.done(b))
                    act.wait_ge(s_ready.sem, s_ready.prev(b))
                    act.activation(lat[:], psum[B_L][0:R, 0:TOK], ACT.Copy).then_inc(lat_ready.sem, 1)

                def scores(b):
                    act.wait_ge(nmx_ready.sem, nmx_ready.done(b))
                    act.wait_ge(pT_ps.sem, pT_ps.prev(b))
                    act.activation(pr[:, 0, :], psum[B_S][:, 0:P], ACT.Exp, bias=nmx[:, 0:1], scale=SCALE)
                    act.activation(pr[:, 1:3, :].rearrange("p a b -> p (a b)"), psum[B_S][:, P:3 * P], ACT.Exp,
                                   bias=nmx[:, 1:2], scale=SCALE).then_inc(p_ready.sem, 1)

                def middle(b, par):
                    act.wait_ge(pT_ps.sem, pT_ps.done(b))
                    act.wait_ge(o_ready.sem, o_ready.prev(b))
                    act.activation(pT[:].rearrange("p a b -> p (a b)"), psum[B_PT][:, 0:3 * P], ACT.Copy)\
                       .then_inc(pT_ready.sem, 1)

                def close(b):
                    act.wait_ge(oT_ps.sem, oT_ps.done(b))
                    act.wait_ge(y_ready.sem, y_ready.prev(b))
                    act.activation(oT[:], psum[B_OT][:, 0:TOK], ACT.Copy).then_inc(oT_ready.sem, 1)

                rounds(act, project, scores, middle, close)

            @block.vector
            def _(dve):
                for s in (v_ready, mxr_ready, nmx_ready, rd_ready, on_ready, x_done):
                    dve.sem_inc(s.sem, s.credit)
                dve.wait_ge(w_ld, 96)
                dve.tensor_copy(maskb[:], mask[:]).then_inc(init, 1)
                dve.wait_ge(init, 3)

                def project(b, par):
                    dve.wait_ge(v_ps.sem, v_ps.done(b))
                    dve.tensor_copy(v[:, par, :, 0:CH], psum[B_V][:, 0:TOK].rearrange("p (t c) -> p t c", c=CH))\
                       .then_inc(v_ready.sem, 1)

                def scores(b):
                    dve.wait_ge(s_ready.sem, s_ready.done(b))
                    dve.tensor_reduce(mxr[:, 0:1], psum[B_S][:, 0:P], AX.X, ALU.max)
                    dve.tensor_reduce(mxr[:, 1:2], psum[B_S][:, P:3 * P], AX.X, ALU.max).then_inc(mxr_ready.sem, 1)
                    dve.wait_ge(mxr_ready.sem, mxr_ready.done(b))
                    dve.wait_ge(p_ready.sem, p_ready.prev(b))
                    dve.tensor_scalar(nmx[:], mxr[:], -SCALE, None, ALU.mult).then_inc(nmx_ready.sem, 1)

                def middle(b, par):
                    ps = psum[B_O][:, 0:2 * VD].rearrange("p (t v) -> p t v", v=VD)
                    dve.wait_ge(o_ready.sem, o_ready.done(b))
                    dve.reciprocal(rd[:], ps[:, :, CH]).then_inc(rd_ready.sem, 1)
                    dve.wait_ge(rd_ready.sem, rd_ready.done(b))
                    dve.wait_ge(oT_ps.sem, oT_ps.prev(b))
                    dve.tensor_tensor(out=on[:], in0=ps[:, :, 0:CH], in1=rd[:].unsqueeze(2).to_broadcast([P, NT, CH]),
                                      op=ALU.mult).then_inc(on_ready.sem, 1)

                def close(b):
                    dve.wait_ge(y_ready.sem, y_ready.done(b))
                    xb = x[:, bass.ds(b * NT, NT), :]
                    dve.tensor_tensor(out=xb, in0=psum[B_Y][:, 0:TOK].rearrange("p (t c) -> p t c", c=CH), in1=xb,
                                      op=ALU.add).then_inc(x_done.sem, 1)

                rounds(dve, project, scores, middle, close)


def memory_attention(nc, name, x, z, zT, wts, ident, psum):
    A48, TW = 48, 48 + 2 * CH
    SL = (slice(0, 8), slice(32, 48))
    NS = (8, 16)
    BW = TOK + P
    SCALE = float(np.float32(CH) ** np.float32(-0.5))
    B_TOK, B_CH, B_M, B_SR, B_T = (0, 1), (2, 3), (4, 5), 6, 7
    with ExitStack() as ctx:
        def sb(n, shape, dt=F32):
            return ctx.enter_context(nc.sbuf_tensor(f"{name}_{n}", shape, dt))

        def sem(n):
            return ctx.enter_context(nc.semaphore(f"{name}_{n}"))

        wt = sb("wt", [P, TW])
        wc = sb("wc", [P, 4, CH])
        wm = sb("wm", [P, 3, CH])
        tokb = sb("tokb", [P, TW])
        chb = sb("chb", [P, 4])
        combb = sb("combb", [1, CH])
        gbr = sb("gbr", [P, 2, CH])
        decay = sb("decay", [P, 2, BW])
        ones = sb("ones", [1, P])
        power = sb("power", [P, NT])
        zs = sb("zs", [P, 2, TOK])
        tok = sb("tok", [P, 2, NT, TW])
        mxa = sb("mxa", [P, NT, 2])
        sa = sb("sa", [P, NT, A48])
        ea = sb("ea", [P, NT, A48])
        gp = sb("gp", [P, NT, 4])
        eg = sb("eg", [P, NT, 4])
        rg = sb("rg", [P, NT, 2])
        eg1 = sb("eg1", [P, NT, 2])
        den = sb("den", [P, NT, 2])
        dg = sb("dg", [P, NT, 2])
        ra = sb("ra", [P, NT, 2])
        adr = sb("adr", [P, 2, NT, A48])
        aT = sb("aT", [A48, 2, TOK])
        ch = sb("ch", [P, 4, TOK])
        mt = sb("mt", [P, 2, BW])
        mxs = sb("mxs", [P, NT, 2])
        ss = sb("ss", [P, NT, A48])
        es = sb("es", [P, NT, A48])
        dens = sb("dens", [P, NT, 2])
        rs = sb("rs", [P, NT, 2])
        w = sb("w", [P, NT, A48])
        wT = sb("wT", [A48, TOK])
        gt = sb("gt", [P, 2, BW])
        rT = sb("rT", [P, 2, TOK])
        cc = sb("cc", [P, NT, CH])
        st = sb("st", [P, NT, 6])
        mv = sb("mv", [P, NT, 2])
        ve = sb("ve", [P, NT])
        rstd = sb("rstd", [P, NT])
        cn = sb("cn", [P, NT, CH])

        w_ld, init = sem("w_ld"), sem("init")
        names = ("zs", "tok_ps", "tok", "mxa", "sa", "ea", "den", "dg", "rg", "ra", "adr", "aT_ps", "aT", "ch_ps", "ch",
                 "m", "mt", "s", "mxs", "ss", "es", "dens", "rs", "w", "wT_ps", "wT", "g", "gt", "r", "rT", "c", "cc",
                 "st", "mv", "ve", "rstd", "cn", "cg", "cb", "x")
        (zs_ready, tok_ps, tok_ready, mxa_ready, sa_ready, ea_ready, den_ready, dg_ready, rg_ready, ra_ready, adr_ready, aT_ps,
         aT_ready, ch_ps, ch_ready, m_ready, mt_ready, s_ready, mxs_ready, ss_ready, es_ready, dens_ready, rs_ready,
         w_ready, wT_ps, wT_ready, g_ready, gt_ready, r_ready, rT_ready, c_ready, cc_ready, st_ready, mv_ready,
         ve_ready, rstd_ready, cn_ready, cg_ready, cb_ready, x_done) = (Count(sem(n), 1) for n in names)
        for s in (gt_ready, g_ready, r_ready, aT_ps, c_ready):
            s.credit = 2
        pe_passed, dve_passed, pool_passed = sem("pe_passed"), sem("dve_passed"), sem("pool_passed")

        def rounds(eng, turn):
            turn(-2, 0, False, False, True)
            turn(-1, 1, False, True, True)
            with eng.Fori(0, (SEQ - 2) // 2) as j:
                turn(j * 2, 0, True, True, True)
                turn(j * 2 + 1, 1, True, True, True)
            turn(SEQ - 2, 0, True, True, False)
            turn(SEQ - 1, 1, True, False, False)

        with nc.Block() as block:
            @block.sync
            def _(sp):
                for dst, n in ((wt, "wt"), (wc, "wc"), (wm, "wm"), (chb, "chb"), (combb, "combb"), (decay, "decay")):
                    sp.dma_start(dst[:], wts[n]).then_inc(w_ld, 16)
                sp.dma_start(tokb[:], wts["tokb"].partition_broadcast(P)).then_inc(w_ld, 16)
                sp.dma_start(gbr[:], wts["gbr"].partition_broadcast(P)).then_inc(w_ld, 16)

            @block.gpsimd
            def _(pool):
                for s in (ve_ready, rstd_ready):
                    pool.sem_inc(s.sem, s.credit)
                pool.memset(ones[:], 1.0).then_inc(init, 1)
                pool.memset(power[:], -0.5).then_inc(init, 1)
                for a in (sa, ss, w, adr):
                    pool.memset(a[:], 0.0).then_inc(init, 1)
                pool.wait_ge(init, 6)
                with pool.Fori(0, SEQ) as b:
                    hold(pool, mv_ready.sem, mv_ready.done(b), pool_passed)
                    pool.tensor_scalar(ve[:], mv[:, :, 1], EPS, None, ALU.add).then_inc(ve_ready.sem, 1)
                    pool.wait_ge(ve_ready.sem, ve_ready.done(b))
                    pool.tensor_tensor(out=rstd[:], in0=ve[:], in1=power[:], op=ALU.pow).then_inc(rstd_ready.sem, 1)

            @block.tensor
            def _(pe):
                for s in (tok_ps, aT_ps, ch_ps, m_ready, s_ready, wT_ps, g_ready, r_ready, c_ready):
                    pe.sem_inc(s.sem, s.credit)
                pe.wait_ge(w_ld, 128)
                pe.wait_ge(init, 6)

                def project(b, par):
                    pe.wait_ge(zs_ready.sem, zs_ready.done(b))
                    hold(pe, tok_ready.sem, tok_ready.prev(b), pe_passed)
                    hold(pe, ss_ready.sem, ss_ready.prev(b), pe_passed)
                    for t in range(NT):
                        last = pe.matmul(psum[B_TOK[t]][:, 0:TW], zs[:, par, t * P:(t + 1) * P], wt[:],
                                         start=True, stop=True)
                    last.then_inc(tok_ps.sem, 1)
                    hold(pe, gt_ready.sem, gt_ready.done(b - 2), pe_passed)
                    pe.wait_ge(ch_ready.sem, ch_ready.prev(b))
                    for k in range(4):
                        last = pe.matmul(psum[B_CH[k // 2]][:, (k % 2) * TOK:(k % 2 + 1) * TOK], wc[:, k, :],
                                         zs[:, par, :], start=True, stop=True)
                    last.then_inc(ch_ps.sem, 1)

                def turn_adr(b, par, before):
                    hold(pe, adr_ready.sem, adr_ready.done(b), pe_passed)
                    if before is not None:
                        hold(pe, wT_ready.sem, wT_ready.done(before), pe_passed)
                    for t in range(NT):
                        last = pe.transpose(psum[B_T][0:A48, t * P:(t + 1) * P], adr[:, par, t, :], ident[:])
                    last.then_inc(aT_ps.sem, 1)

                def blocks(out, lhs, rhs):
                    pe.matmul(out[:, 0:TOK], lhs[:, 0:P], rhs[:, 0:TOK], start=True, stop=True)
                    return pe.matmul(out[:, TOK:BW], lhs[:, P:TOK], rhs[:, P:TOK], start=True, stop=True)

                def match(b):
                    pe.wait_ge(ch_ready.sem, ch_ready.done(b))
                    hold(pe, mt_ready.sem, mt_ready.prev(b), pe_passed)
                    for r in range(2):
                        last = blocks(psum[B_M[r]], ch[:, 2 * r, :], ch[:, 2 * r + 1, :])
                    last.then_inc(m_ready.sem, 1)

                def score(b, par):
                    hold(pe, adr_ready.sem, adr_ready.done(b), pe_passed)
                    hold(pe, tok_ready.sem, tok_ready.done(b), pe_passed)
                    pe.wait_ge(mt_ready.sem, mt_ready.done(b))
                    for r in range(2):
                        for t in range(NT):
                            at = TW + t * A48
                            out = psum[B_TOK[0]][:, at + SL[r].start:at + SL[r].stop]
                            last = pe.matmul(out, mt[:, r, t * P:(t + 1) * P], adr[:, par, 0, SL[r]],
                                             start=True, stop=(t == 0))
                        last = pe.matmul(out, mt[:, r, TOK:BW], adr[:, par, 1, SL[r]], start=False, stop=True)
                    last.then_inc(s_ready.sem, 1)

                def turn_w(b):
                    hold(pe, cc_ready.sem, cc_ready.prev(b), pe_passed)
                    hold(pe, w_ready.sem, w_ready.done(b), pe_passed)
                    for t in range(NT):
                        last = pe.transpose(psum[B_T][0:A48, t * P:(t + 1) * P], w[:, t, :], ident[:])
                    last.then_inc(wT_ps.sem, 1)

                def weights(b, par, last_ch):
                    hold(pe, wT_ready.sem, wT_ready.done(b), pe_passed)
                    hold(pe, aT_ready.sem, aT_ready.done(b), pe_passed)
                    hold(pe, ch_ready.sem, ch_ready.done(last_ch), pe_passed)
                    for r in range(2):
                        last = blocks(psum[B_CH[r]], aT[SL[r], par, :], wT[SL[r], :])
                    last.then_inc(g_ready.sem, 1)

                def read(b, par):
                    hold(pe, rT_ready.sem, rT_ready.prev(b), pe_passed)
                    pe.wait_ge(gt_ready.sem, gt_ready.done(b))
                    for r in range(2):
                        val = slice(A48 + r * CH, A48 + (r + 1) * CH)
                        pe.matmul(psum[B_SR][:, r * TOK:(r + 1) * TOK], tok[:, par, 0, val], gt[:, r, 0:TOK],
                                  start=True, stop=True)
                        last = pe.matmul(psum[B_SR][:, r * TOK + P:(r + 1) * TOK], tok[:, par, 1, val],
                                         gt[:, r, TOK:BW], start=False, stop=True, skip_group_check=True)
                    last.then_inc(r_ready.sem, 1)

                def close(b, par, ahead):
                    if ahead:
                        hold(pe, aT_ready.sem, aT_ready.done(b + 1), pe_passed)
                    pe.wait_ge(rT_ready.sem, rT_ready.done(b))
                    for t in range(NT):
                        out = psum[B_T][:, t * CH:(t + 1) * CH]
                        tt = slice(t * P, (t + 1) * P)
                        pe.matmul(out, ones[:], combb[:], start=True, stop=False)
                        pe.matmul(out, zs[:, par, tt], wm[:, 0, :], start=False, stop=False)
                        pe.matmul(out, rT[:, 0, tt], wm[:, 1, :], start=False, stop=False)
                        last = pe.matmul(out, rT[:, 1, tt], wm[:, 2, :], start=False, stop=True)
                    last.then_inc(c_ready.sem, 1)

                def turn(b, par, cur, mid, far):
                    if cur:
                        turn_w(b)
                    if mid:
                        match(b + 1)
                    if cur:
                        weights(b, par, b + 1 if mid else b)
                    if mid:
                        score(b + 1, 1 - par)
                        turn_adr(b + 1, 1 - par, b if cur else None)
                    if cur:
                        read(b, par)
                        close(b, par, mid)
                    if far:
                        project(b + 2, par)

                rounds(pe, turn)

            @block.scalar
            def _(act):
                for s in (zs_ready, ch_ready, ea_ready, aT_ready, es_ready, wT_ready, rT_ready):
                    act.sem_inc(s.sem, s.credit)
                act.wait_ge(w_ld, 128)

                def copy_z(b, par):
                    act.wait_ge(c_ready.sem, c_ready.done(b - 2))
                    act.activation(zs[:, par, :], zT[:, bass.ds(b * TOK, TOK)], ACT.Copy).then_inc(zs_ready.sem, 1)

                def copy_ch(b):
                    act.wait_ge(ch_ps.sem, ch_ps.done(b))
                    act.wait_ge(m_ready.sem, m_ready.prev(b))
                    for k in range(4):
                        last = act.activation(ch[:, k, :], psum[B_CH[k // 2]][:, (k % 2) * TOK:(k % 2 + 1) * TOK],
                                              ACT.Identity, bias=chb[:, k:k + 1])
                    last.then_inc(ch_ready.sem, 1)

                def address(b):
                    act.wait_ge(sa_ready.sem, sa_ready.done(b))
                    act.activation(ea[:], sa[:], ACT.Exp)
                    act.activation(eg[:], gp[:], ACT.Exp, scale=5.0).then_inc(ea_ready.sem, 1)

                def copy_a(b, par):
                    act.wait_ge(aT_ps.sem, aT_ps.done(b))
                    act.wait_ge(g_ready.sem, g_ready.done(b - 2))
                    act.activation(aT[:, par, :], psum[B_T][0:A48, 0:TOK], ACT.Copy).then_inc(aT_ready.sem, 1)

                def score(b):
                    act.wait_ge(ss_ready.sem, ss_ready.done(b))
                    act.activation(es[:], ss[:], ACT.Exp, scale=SCALE).then_inc(es_ready.sem, 1)

                def copy_w(b):
                    act.wait_ge(wT_ps.sem, wT_ps.done(b))
                    act.wait_ge(g_ready.sem, g_ready.prev(b))
                    act.activation(wT[:], psum[B_T][0:A48, 0:TOK], ACT.Copy).then_inc(wT_ready.sem, 1)

                def copy_r(b):
                    act.wait_ge(r_ready.sem, r_ready.done(b))
                    act.wait_ge(c_ready.sem, c_ready.prev(b))
                    act.activation(rT[:].rearrange("p r t -> p (r t)"), psum[B_SR][:], ACT.Copy)\
                       .then_inc(rT_ready.sem, 1)

                def turn(b, par, cur, mid, far):
                    if cur:
                        copy_w(b)
                    if mid:
                        copy_a(b + 1, 1 - par)
                        score(b + 1)
                    if cur:
                        copy_r(b)
                    if far:
                        copy_z(b + 2, par)
                        copy_ch(b + 2)
                        address(b + 2)

                rounds(act, turn)

            @block.vector
            def _(dve):
                for s in (tok_ready, mxa_ready, sa_ready, den_ready, dg_ready, rg_ready, ra_ready, adr_ready, mt_ready, mxs_ready,
                          ss_ready, dens_ready, rs_ready, w_ready, gt_ready, cc_ready, st_ready, mv_ready, cn_ready,
                          cg_ready, cb_ready, x_done):
                    dve.sem_inc(s.sem, s.credit)
                dve.wait_ge(w_ld, 128)
                dve.wait_ge(init, 6)

                def each(op):
                    for r in range(2):
                        last = op(r)
                    return last

                def bc(ap, r):
                    return ap[:, :, r:r + 1].to_broadcast([P, NT, NS[r]])

                def project(b, par):
                    tk = tok[:, par]
                    dve.wait_ge(tok_ps.sem, tok_ps.done(b))
                    dve.wait_ge(r_ready.sem, r_ready.done(b - 2))
                    dve.wait_ge(aT_ps.sem, aT_ps.done(b - 2))
                    for t in range(NT):
                        last = dve.tensor_tensor(out=tok[:, par, t, :], in0=psum[B_TOK[t]][:, 0:TW], in1=tokb[:],
                                                 op=ALU.add)
                    last.then_inc(tok_ready.sem, 1)
                    dve.wait_ge(tok_ready.sem, tok_ready.done(b))
                    each(lambda r: dve.tensor_reduce(mxa[:, :, r], tk[:, :, SL[r]], AX.X, ALU.max))\
                        .then_inc(mxa_ready.sem, 1)
                    dve.wait_ge(mxa_ready.sem, mxa_ready.done(b))
                    dve.tensor_scalar(gp[:, :, 0:2], tk[:, :, 8:10], 0.0, None, ALU.min)
                    dve.tensor_scalar(gp[:, :, 2:4], tk[:, :, 8:10], 0.0, -1.0, ALU.max, ALU.mult)
                    each(lambda r: dve.tensor_tensor(out=sa[:, :, SL[r]], in0=tk[:, :, SL[r]], in1=bc(mxa, r),
                                                     op=ALU.subtract)).then_inc(sa_ready.sem, 1)
                    dve.wait_ge(ea_ready.sem, ea_ready.done(b))
                    dve.tensor_tensor(out=eg1[:], in0=eg[:, :, 0:2], in1=eg[:, :, 2:4], op=ALU.add)
                    each(lambda r: dve.tensor_reduce(den[:, :, r], ea[:, :, SL[r]], AX.X, ALU.add))\
                        .then_inc(den_ready.sem, 1)
                    dve.wait_ge(den_ready.sem, den_ready.done(b))
                    dve.tensor_tensor(out=dg[:], in0=den[:], in1=eg1[:], op=ALU.mult).then_inc(dg_ready.sem, 1)
                    dve.wait_ge(dg_ready.sem, dg_ready.done(b))
                    dve.reciprocal(rg[:], dg[:]).then_inc(rg_ready.sem, 1)
                    dve.wait_ge(rg_ready.sem, rg_ready.done(b))
                    dve.tensor_tensor(out=ra[:], in0=rg[:], in1=eg[:, :, 0:2], op=ALU.mult).then_inc(ra_ready.sem, 1)
                    dve.wait_ge(ra_ready.sem, ra_ready.done(b))
                    each(lambda r: dve.tensor_tensor(out=adr[:, par, :, SL[r]], in0=ea[:, :, SL[r]], in1=bc(ra, r),
                                                     op=ALU.mult)).then_inc(adr_ready.sem, 1)

                def match(b):
                    dve.wait_ge(m_ready.sem, m_ready.done(b))
                    dve.wait_ge(s_ready.sem, s_ready.prev(b))
                    each(lambda r: dve.tensor_tensor(out=mt[:, r, :], in0=psum[B_M[r]][:, 0:BW], in1=decay[:, r, :],
                                                     op=ALU.mult)).then_inc(mt_ready.sem, 1)

                def score(b):
                    ps = psum[B_TOK[0]][:, TW:TW + NT * A48].rearrange("p (t a) -> p t a", t=NT)
                    dve.wait_ge(s_ready.sem, s_ready.done(b))
                    each(lambda r: dve.tensor_reduce(mxs[:, :, r], ps[:, :, SL[r]], AX.X, ALU.max))\
                        .then_inc(mxs_ready.sem, 1)
                    dve.wait_ge(mxs_ready.sem, mxs_ready.done(b))
                    each(lambda r: dve.tensor_tensor(out=ss[:, :, SL[r]], in0=ps[:, :, SL[r]], in1=bc(mxs, r),
                                                     op=ALU.subtract)).then_inc(ss_ready.sem, 1)
                    dve.wait_ge(es_ready.sem, es_ready.done(b))
                    each(lambda r: dve.tensor_reduce(dens[:, :, r], es[:, :, SL[r]], AX.X, ALU.add))\
                        .then_inc(dens_ready.sem, 1)
                    dve.wait_ge(dens_ready.sem, dens_ready.done(b))
                    dve.reciprocal(rs[:], dens[:]).then_inc(rs_ready.sem, 1)
                    dve.wait_ge(rs_ready.sem, rs_ready.done(b))
                    dve.wait_ge(wT_ps.sem, wT_ps.prev(b))
                    each(lambda r: dve.tensor_tensor(out=w[:, :, SL[r]], in0=es[:, :, SL[r]], in1=bc(rs, r),
                                                     op=ALU.mult)).then_inc(w_ready.sem, 1)

                def read(b):
                    dve.wait_ge(g_ready.sem, g_ready.done(b))
                    dve.wait_ge(r_ready.sem, r_ready.prev(b))
                    each(lambda r: dve.tensor_tensor(out=gt[:, r, :], in0=psum[B_CH[r]][:, 0:BW], in1=decay[:, r, :],
                                                     op=ALU.mult)).then_inc(gt_ready.sem, 1)

                def close(b):
                    tiles = bass.ds(b * NT, NT)
                    dve.wait_ge(c_ready.sem, c_ready.done(b))
                    dve.tensor_tensor(out=cc[:], in0=psum[B_T][:, 0:TOK].rearrange("p (t c) -> p t c", c=CH),
                                      in1=z[:, tiles, :], op=ALU.add).then_inc(cc_ready.sem, 1)
                    hold(dve, cc_ready.sem, cc_ready.done(b), dve_passed)
                    for t in range(NT):
                        last = dve.bn_stats(st[:, t, :], cc[:, t, :])
                    last.then_inc(st_ready.sem, 1)
                    hold(dve, st_ready.sem, st_ready.done(b), dve_passed)
                    for t in range(NT):
                        last = dve.bn_aggr(mv[:, t, :], st[:, t, :])
                    last.then_inc(mv_ready.sem, 1)
                    dve.wait_ge(rstd_ready.sem, rstd_ready.done(b))
                    for t in range(NT):
                        last = dve.tensor_scalar(cn[:, t, :], cc[:, t, :], mv[:, t, 0:1], rstd[:, t:t + 1],
                                                 ALU.subtract, ALU.mult)
                    last.then_inc(cn_ready.sem, 1)
                    dve.wait_ge(cn_ready.sem, cn_ready.done(b))
                    dve.tensor_tensor(out=cc[:], in0=cn[:], in1=gbr[:, 0:1, :].to_broadcast([P, NT, CH]), op=ALU.mult)\
                       .then_inc(cg_ready.sem, 1)
                    dve.wait_ge(cg_ready.sem, cg_ready.done(b))
                    dve.tensor_tensor(out=cn[:], in0=cc[:], in1=gbr[:, 1:2, :].to_broadcast([P, NT, CH]), op=ALU.add)\
                       .then_inc(cb_ready.sem, 1)
                    dve.wait_ge(cb_ready.sem, cb_ready.done(b))
                    dve.tensor_tensor(out=x[:, tiles, :], in0=cn[:], in1=x[:, tiles, :], op=ALU.add)\
                       .then_inc(x_done.sem, 1)

                def turn(b, par, cur, mid, far):
                    if mid:
                        match(b + 1)
                    if cur:
                        read(b)
                    if mid:
                        score(b + 1)
                    if cur:
                        close(b)
                    if far:
                        project(b + 2, par)

                rounds(dve, turn)


def routed_feed(nc, name, x, zT, wts, ident, psum):
    E, FC, CK = 8, 4, 512
    NTILE = SEQ * NT
    TURNS = SEQ * TOK // CK
    CT = CK // P
    with ExitStack() as ctx:
        def sb(n, shape, dt=F32):
            return ctx.enter_context(nc.sbuf_tensor(f"{name}_{n}", shape, dt))

        def sem(n):
            return ctx.enter_context(nc.semaphore(f"{name}_{n}"))

        w1 = sb("w1", [P, E, FC * P])
        w2 = sb("w2", [P, E, FC, CH])
        b1 = sb("b1", [P, E * FC])
        b2 = sb("b2", [P, 16 * CH])
        wr = sb("wr", [P, E])
        br = sb("br", [P, E])
        rank = sb("rank", [P, E])
        zs = sb("zs", [P, 2, TOK])
        lg = sb("lg", [P, NTILE, E])
        work = sb("work", [P, NTILE, E])
        gate = sb("gate", [P, NTILE, E])
        best = sb("best", [P, NTILE])
        den = sb("den", [P, NTILE])
        prob = sb("prob", [P, NTILE])
        gT = sb("gT", [P, 2, P])
        h = sb("h", [P, 2, FC, CK])
        w_ld, w2_ld, step, lg_all = sem("w_ld"), sem("w2_ld"), sem("step"), sem("lg_all")
        exps, gT_ps, gT_ready, bias_ps, bias_done = (sem(n) for n in ("exps", "gT_ps", "gT", "bias_ps", "bias_done"))
        zs_ready = Count(sem("zs"), 2)
        l_ps = Count(sem("l_ps"), 2)
        lg_ready = Count(sem("lg"), 2)
        h_ps = Count(sem("h_ps"), E * FC)
        ha_ready = Count(sem("ha"), E * FC // 2)
        hv_ready = Count(sem("hv"), E * FC // 2)
        y_ready = Count(sem("y"), E)
        x_done = Count(sem("x"), E)

        with nc.Block() as block:
            @block.sync
            def _(sp):
                for dst, n in ((wr, "Wr"), (b1, "b1"), (b2, "b2"), (rank, "rank")):
                    sp.dma_start(dst[:], wts[n]).then_inc(w_ld, 16)
                sp.dma_start(br[:], wts["br"].partition_broadcast(P)).then_inc(w_ld, 16)
                sp.dma_start(w1[:], wts["W1"].rearrange("e k f -> k e f")).then_inc(w2_ld, 16)
                sp.dma_start(w2[:], wts["W2"].rearrange("e (f k) n -> k e f n", k=P)).then_inc(w2_ld, 16)

            @block.tensor
            def _(pe):
                for s in (l_ps, h_ps, y_ready):
                    pe.sem_inc(s.sem, s.credit)
                pe.wait_ge(w_ld, 80)
                with pe.Fori(0, SEQ // 2) as j:
                    for a in range(2):
                        pe.wait_ge(lg_ready.sem, lg_ready.prev(j, a))
                        pe.wait_ge(zs_ready.sem, zs_ready.done(j, a))
                        for t in range(NT):
                            last = pe.matmul(psum[a][:, t * E:(t + 1) * E], zs[:, a, t * P:(t + 1) * P], wr[:],
                                             start=True, stop=True)
                        last.then_inc(l_ps.sem, 1)
                pe.wait_ge(step, 9)
                for a in range(2):
                    last = pe.transpose(psum[a][:, 0:P], gate[:, a * 16:(a + 1) * 16, :].rearrange("p t e -> p (t e)"),
                                        ident[:])
                last.then_inc(gT_ps, 1)
                pe.wait_ge(gT_ready, 1)
                for n in range(8):
                    pe.matmul(psum[n][:], gT[:, n // 4, :], b2[:, (n % 4) * 512:(n % 4 + 1) * 512], start=True, stop=True)\
                      .then_inc(bias_ps, 1)
                pe.wait_ge(bias_done, 8)
                pe.wait_ge(w2_ld, 32)

                def hidden(j, e, f):
                    m = e * (FC // 2) + f // 2
                    done = (ha_ready, hv_ready)[f % 2]
                    pe.wait_ge(done.sem, done.done(j, m - FC // 2) if e else done.prev(j, m + (E - 1) * FC // 2))
                    pe.matmul(psum[f][:], w1[:, e, f * P:(f + 1) * P], zT[:, bass.ds(j * CK, CK)], start=True, stop=True)\
                      .then_inc(h_ps.sem, 1)

                def down(j, e):
                    pe.wait_ge(ha_ready.sem, ha_ready.done(j, (e + 1) * FC // 2 - 1))
                    pe.wait_ge(hv_ready.sem, hv_ready.done(j, (e + 1) * FC // 2 - 1))
                    pe.wait_ge(x_done.sem, x_done.done(j, e - 2) if e >= 2 else x_done.prev(j, E - 2 + e))
                    for t in range(CT):
                        for f in range(FC):
                            last = pe.matmul(psum[4 + e % 2][:, t * CH:(t + 1) * CH], h[:, e % 2, f, t * P:(t + 1) * P],
                                             w2[:, e, f, :], start=(f == 0), stop=(f == FC - 1))
                    last.then_inc(y_ready.sem, 1)

                with pe.Fori(0, TURNS) as j:
                    for e in range(E):
                        for f in range(FC):
                            hidden(j, e, f)
                        if e:
                            down(j, e - 1)
                    down(j, E - 1)

            @block.scalar
            def _(act):
                for s in (zs_ready, ha_ready):
                    act.sem_inc(s.sem, s.credit)
                with act.Fori(0, SEQ // 2) as j:
                    for a in range(2):
                        act.wait_ge(l_ps.sem, l_ps.prev(j, a))
                        act.activation(zs[:, a, :], zT[:, bass.ds(j * 2 * TOK + a * TOK, TOK)], ACT.Copy)\
                           .then_inc(zs_ready.sem, 1)
                act.wait_ge(step, 2)
                act.activation(work[:].rearrange("p t e -> p (t e)"), work[:].rearrange("p t e -> p (t e)"), ACT.Exp)\
                   .then_inc(exps, 1)
                act.wait_ge(gT_ps, 1)
                for a in range(2):
                    last = act.activation(gT[:, a, :], psum[a][:, 0:P], ACT.Copy)
                last.then_inc(gT_ready, 1)
                act.wait_ge(w_ld, 80)
                with act.Fori(0, TURNS) as j:
                    for e in range(E):
                        for f in range(0, FC, 2):
                            act.wait_ge(h_ps.sem, h_ps.done(j, e * FC + f))
                            act.wait_ge(y_ready.sem, y_ready.done(j, e - 2) if e >= 2 else y_ready.prev(j, E - 2 + e))
                            act.activation(h[:, e % 2, f, :], psum[f][:], ACT.Relu, bias=b1[:, e * FC + f:e * FC + f + 1])\
                               .then_inc(ha_ready.sem, 1)

            @block.vector
            def _(dve):
                for s in (lg_ready, hv_ready, x_done):
                    dve.sem_inc(s.sem, s.credit)
                dve.wait_ge(w_ld, 80)
                with dve.Fori(0, SEQ // 2) as j:
                    for a in range(2):
                        dve.wait_ge(l_ps.sem, l_ps.done(j, a))
                        dve.tensor_tensor(out=lg[:, bass.ds(j * 2 * NT + a * NT, NT), :],
                                          in0=psum[a][:, 0:NT * E].rearrange("p (t e) -> p t e", e=E),
                                          in1=br[:].unsqueeze(1).to_broadcast([P, NT, E]), op=ALU.add)\
                           .then_inc(lg_ready.sem, 1)

                def over(ap):
                    return ap[:].unsqueeze(2).to_broadcast([P, NTILE, E])

                ranks = rank[:].unsqueeze(1).to_broadcast([P, NTILE, E])
                dve.wait_ge(lg_ready.sem, SEQ + lg_ready.credit)
                dve.tensor_reduce(best[:], lg[:], AX.X, ALU.max).then_inc(step, 1)
                dve.wait_ge(step, 1)
                dve.tensor_tensor(out=work[:], in0=lg[:], in1=over(best), op=ALU.subtract).then_inc(step, 1)
                dve.wait_ge(exps, 1)
                dve.tensor_reduce(den[:], work[:], AX.X, ALU.add).then_inc(step, 1)
                dve.wait_ge(step, 3)
                dve.reciprocal(prob[:], den[:])
                dve.tensor_tensor(out=work[:], in0=lg[:], in1=over(best), op=ALU.is_equal).then_inc(step, 1)
                dve.wait_ge(step, 4)
                dve.tensor_tensor(out=lg[:], in0=work[:], in1=ranks, op=ALU.mult).then_inc(step, 1)
                dve.wait_ge(step, 5)
                dve.tensor_reduce(best[:], lg[:], AX.X, ALU.max).then_inc(step, 1)
                dve.wait_ge(step, 6)
                dve.tensor_tensor(out=work[:], in0=lg[:], in1=over(best), op=ALU.is_equal).then_inc(step, 2)
                dve.wait_ge(step, 8)
                dve.tensor_tensor(out=gate[:], in0=work[:], in1=over(prob), op=ALU.mult).then_inc(step, 1)
                for n in range(8):
                    dve.wait_ge(bias_ps, n + 1)
                    dve.tensor_tensor(out=x[:, 4 * n:4 * n + 4, :], in0=psum[n][:].rearrange("p (t c) -> p t c", c=CH),
                                      in1=x[:, 4 * n:4 * n + 4, :], op=ALU.add).then_inc(bias_done, 1)
                dve.wait_ge(bias_done, 8)

                def relus(j, e):
                    for f in range(1, FC, 2):
                        dve.wait_ge(h_ps.sem, h_ps.done(j, e * FC + f))
                        dve.wait_ge(y_ready.sem, y_ready.done(j, e - 2) if e >= 2 else y_ready.prev(j, E - 2 + e))
                        dve.tensor_scalar(h[:, e % 2, f, :], psum[f][:], b1[:, e * FC + f:e * FC + f + 1], 0.0,
                                          ALU.add, ALU.max).then_inc(hv_ready.sem, 1)

                def add(j, e):
                    dve.wait_ge(y_ready.sem, y_ready.done(j, e))
                    dve.wait_ge(x_done.sem, x_done.done(j, e - 1) if e else x_done.prev(j, E - 1))
                    for t in range(CT):
                        tile = bass.ds(j * CT + t, 1)
                        xt = x[:, tile, :].rearrange("p a c -> p (a c)")
                        last = dve.scalar_tensor_tensor(out=xt, in0=psum[4 + e % 2][:, t * CH:(t + 1) * CH],
                                                        scalar=gate[:, tile, e:e + 1].rearrange("p a c -> p (a c)"),
                                                        in1=xt, op0=ALU.mult, op1=ALU.add)
                    last.then_inc(x_done.sem, 1)

                with dve.Fori(0, TURNS) as j:
                    for e in range(E):
                        relus(j, e)
                        if e:
                            add(j, e - 1)
                    add(j, E - 1)


def local_constants(W):
    f = np.float32
    half = np.arange(0, HD, 2, dtype=f)
    inv_freq = (f(1.0) / np.power(f(10000.0), half / f(HD))).astype(f)
    t = np.arange(TOK, dtype=f)
    freqs = t[:, None] * inv_freq[None, :]
    freqs = np.concatenate([freqs, freqs], -1)
    base = ((half + f(0.4 * HD)) / f(1.4 * HD)).astype(f)
    power = ((t - f(TOK // 2)) / f(W // 2)).astype(f)
    scale = np.power(base[None, :], power[:, None]).astype(f)
    scale = np.concatenate([scale, scale], -1)
    sign = np.where(np.arange(HD) < HD // 2, -1.0, 1.0).astype(f)[None, :]
    cos, sin = np.cos(freqs).astype(f), np.sin(freqs).astype(f) * sign
    inv = (f(1.0) / scale).astype(f)
    tabs = np.stack([cos * scale, sin * scale, cos * inv, sin * inv], 1).astype(f)
    rope = np.ascontiguousarray(tabs.reshape(NT, P, 4, HD).transpose(1, 0, 2, 3))
    q = np.arange(P)[:, None] % W
    k = np.arange(2 * W)[None, :]
    seen = (k >= q) & (k <= q + W)
    NW = TOK // W // 2
    mask = np.zeros((P, 2, NW, 2, 2 * W), f)
    for h in range(2):
        for w in range(NW):
            ok = seen & (k >= W) if (h == 0 and w == 0) else seen
            mask[:, h, w] = np.where(ok, 0.0, MASKED)[:, None, :]
    return rope, mask.reshape(P, 2, 512)


def local_weights(inp, pre, names):
    wqkv, qs, ks, wo, g, b, w1, b1, w2, b2 = (np.asarray(inp[pre + n]) for n in names)
    depth = wqkv.shape[0]
    b1t = np.zeros((depth, P, 2 * HCH), b1.dtype)
    w2t = np.zeros((depth, P, HCH, CH), w2.dtype)
    for c in range(HCH):
        n = min(P, HID - c * P)
        for a in range(2):
            b1t[:, :n, a * HCH + c] = b1[:, a * HID + c * P:a * HID + c * P + n]
        w2t[:, :n, c] = w2[:, c * P:c * P + n]
    w2t[:, HLAST, HCH - 1] = b2
    return {"Wqkv": wqkv, "Wo": wo, "qks": np.stack([qs, ks], 1), "W1": w1, "W2": w2t, "b1": b1t,
            "gb": np.stack([g, b], 2)}


def grouped_weights(inp):
    wq, bq, wu, bu = (np.asarray(inp["L0_attn_" + n]) for n in ("wq", "bq", "wu", "bu"))
    wt = np.zeros((CH, 16, P), wq.dtype)
    wt[:, :, :8] = wq.T.reshape(CH, 16, 8)
    bt = np.zeros((P, 16), bq.dtype)
    bt[:8] = bq.reshape(16, 8).T
    return {"wq": wt, "bq": bt, "wu": np.ascontiguousarray(wu.T), "bu": bu[None, :]}


def swiglu_weights(inp):
    wg, wu, wd = (np.asarray(inp["L1_ffn_" + n]) for n in ("w_gate", "w_up", "w_down"))
    return {"w_gate": np.ascontiguousarray(wg.T), "w_up": np.ascontiguousarray(wu.T),
            "w_down": np.ascontiguousarray(wd.T.reshape(3, P, CH).transpose(1, 0, 2).reshape(P, 3 * CH))}


def chunk_weights(inp):
    f = np.float32
    inv_freq = (f(1.0) / np.power(f(10000.0), np.arange(0, 8, 2, dtype=f) / f(8))).astype(f)
    freqs = np.outer(np.arange(64, dtype=f), inv_freq).astype(f)
    cos, sin = np.tile(np.cos(freqs).astype(f), (2, 1)), np.tile(np.sin(freqs).astype(f), (2, 1))
    rope = np.stack([np.concatenate([cos, cos], 1), np.concatenate([sin, -sin], 1)], 1)
    head = (np.arange(P)[:, None] // 8 == np.arange(16)[None, :]).astype(f)
    return {"w_attn": np.ascontiguousarray(np.asarray(inp["L1_attn_w_attn"]).T),
            "w_proj": np.ascontiguousarray(np.asarray(inp["L1_attn_w_proj"]).T), "rope": rope, "headmask": head}


def latent_weights(inp):
    w = {n: np.asarray(inp["L3_attn_" + n]) for n in ("W_basis", "W_v", "W_o", "b_v", "b_o")}
    causal = np.where(np.arange(P)[None, :] <= np.arange(P)[:, None], 0.0, MASKED).astype(np.float32)
    return {"W_basis": np.ascontiguousarray(w["W_basis"].T), "W_v": np.ascontiguousarray(w["W_v"].T),
            "W_o": np.ascontiguousarray(w["W_o"].T), "b_v": w["b_v"][None, :], "b_o": w["b_o"][None, :],
            "causal": causal}


def memory_weights(inp):
    g = {n[8:]: np.asarray(v) for n, v in inp.items() if n.startswith("L2_attn_")}
    dt = g["reg_val_w"].dtype
    wt, tb = np.zeros((CH, 48 + 2 * CH), dt), np.zeros((48 + 2 * CH,), dt)
    for at, n in ((0, "reg_addr"), (8, "reg_gate"), (9, "mem_gate"), (32, "mem_addr"), (48, "reg_val"),
                  (48 + CH, "mem_val")):
        w, b = g[n + "_w"], g[n + "_b"]
        wt[:, at:at + w.shape[0]] = w.T
        tb[at:at + w.shape[0]] = b
    four = ("reg_val", "reg_q", "mem_val", "mem_q")
    s, t = np.arange(P)[:, None], np.arange(TOK)[None, :]
    blocks = []
    for d in (1.0, 0.995):
        first = np.where(s <= t, np.power(d, np.maximum(t - s, 0)), 0.0)
        second = np.where(s + P <= t[:, P:], np.power(d, np.maximum(t[:, P:] - s - P, 0)), 0.0)
        blocks.append(np.concatenate([first, second], 1))
    return {"wt": wt, "tokb": tb, "wc": np.stack([g[n + "_w"].T for n in four], 1),
            "chb": np.stack([g[n + "_b"] for n in four], 1),
            "wm": g["comb_w"].T.reshape(3, CH, CH).transpose(1, 0, 2), "combb": g["comb_b"][None, :],
            "gbr": np.stack([g["ln_g"], g["ln_b"]]), "decay": np.stack(blocks, 1).astype(np.float32)}


def routed_weights(inp):
    w = {n: np.asarray(inp["L3_ffn_" + n]) for n in ("Wr", "br", "W1", "b1", "W2", "b2")}
    b2 = np.zeros((16, 8, 16, CH), w["b2"].dtype)
    for t in range(16):
        b2[t, :, t] = w["b2"]
    rank = np.broadcast_to(np.arange(8, 0, -1, dtype=np.float32), (P, 8))
    return {"Wr": w["Wr"], "br": w["br"], "W1": w["W1"], "W2": w["W2"], "rank": rank,
            "b1": w["b1"].reshape(8, 4, P).transpose(2, 0, 1).reshape(P, 32), "b2": b2.reshape(P, 16 * CH)}


L0_FFN = ("Wqkv", "q_scale", "k_scale", "Wo", "ln_g", "ln_b", "W1", "b1", "W2", "b2")
L2_FFN = ("wqkv", "q_scale", "k_scale", "wo", "ln_g", "ln_b", "w1", "b1", "w2", "b2")


def add_stream(nc, name, x, z):
    with nc.semaphore(f"{name}_added") as added, nc.Block() as block:
        @block.vector
        def _(dve):
            for part in range(2):
                tiles = slice(part * SEQ, (part + 1) * SEQ)
                dve.tensor_tensor(out=x[:, tiles, :], in0=x[:, tiles, :], in1=z[:, tiles, :], op=ALU.add)\
                   .then_inc(added, 1)
            dve.wait_ge(added, 2)


def clear_semaphores(nc):
    given_back = sorted(int(s) for s in nc.released_uncleared_semaphores)
    first = [s for s in given_back if s - 1 not in given_back]
    last = [s for s in given_back if s + 1 not in given_back]
    with nc.Block() as block:
        @block.gpsimd
        def _(pool):
            for a, b in zip(first, last):
                pool.sem_clear(range(a, b + 1))


def build_program(nc, dram, out):
    scratch = nc.dram_tensor("group_scratch_dram", (SEQ, TOK * CH), F32, kind="Internal").ap()

    def wts(module):
        return {n[len(module) + 1:]: ap for n, ap in dram.items() if n.startswith(module + "_")}

    with ExitStack() as whole:
        def sb(n, shape, dt=F32, ctx=whole):
            return ctx.enter_context(nc.sbuf_tensor(n, shape, dt))

        x, ident, identb = sb("x_sb", [P, SEQ * NT, CH]), sb("ident_sb", [P, P]), sb("identb_sb", [P, P], BF16)
        psum = [whole.enter_context(nc.psum_tensor(f"bank{i}", [P, 512], F32)) for i in range(8)]
        loaded, rounded, stored = (whole.enter_context(nc.semaphore(n)) for n in ("loaded", "rounded", "stored"))

        with nc.Block() as block:
            @block.sync
            def _(sp):
                sp.dma_start(x[:], dram["x"].rearrange("b (t p) c -> p (b t) c", p=P)).then_inc(loaded, 16)
                sp.dma_start(ident[:], dram["ident"]).then_inc(loaded, 16)
                sp.wait_ge(loaded, 32)

            @block.vector
            def _(dve):
                dve.wait_ge(loaded, 32)
                dve.tensor_copy(identb[:], ident[:]).then_inc(rounded, 1)
                dve.wait_ge(rounded, 1)

        with ExitStack() as own:
            zT = sb("z0T", [P, SEQ * TOK], ctx=own)
            norm_stream(nc, "n0", x, None, zT, ident, psum)
            grouped_attention(nc, "ga", x, zT, wts("ga"), scratch, ident, psum)
        with ExitStack() as own:
            z = sb("z1", [P, SEQ * NT, CH], ctx=own)
            norm_stream(nc, "n1", x, z, None, ident, psum)
            local_stack(nc, "lo", z, 32, 16, 6, wts("lo"), {"ident": ident, "identb": identb}, psum)
            add_stream(nc, "lo_x", x, z)
        clear_semaphores(nc)
        with ExitStack() as own:
            zT = sb("z2T", [P, SEQ * TOK], ctx=own)
            norm_stream(nc, "n2", x, None, zT, ident, psum)
            chunk_attention(nc, "ca", x, zT, wts("ca"), ident, psum)
            norm_stream(nc, "n3", x, None, zT, ident, psum)
            gated_feed(nc, "gf", x, zT, wts("gf"), psum)
            with ExitStack() as inner:
                z = sb("z4", [P, SEQ * NT, CH], ctx=inner)
                norm_stream(nc, "n4", x, z, zT, ident, psum)
                memory_attention(nc, "ma", x, z, zT, wts("ma"), ident, psum)
        clear_semaphores(nc)
        with ExitStack() as own:
            z = sb("z5", [P, SEQ * NT, CH], ctx=own)
            norm_stream(nc, "n5", x, z, None, ident, psum)
            local_stack(nc, "lt", z, 64, 8, 2, wts("lt"), {"ident": ident, "identb": identb}, psum)
            add_stream(nc, "lt_x", x, z)
        clear_semaphores(nc)
        with ExitStack() as own:
            zT = sb("z6T", [P, SEQ * TOK], ctx=own)
            norm_stream(nc, "n6", x, None, zT, ident, psum)
            latent_attention(nc, "la", x, zT, wts("la"), ident, identb, psum)
            norm_stream(nc, "n7", x, None, zT, ident, psum)
            routed_feed(nc, "rf", x, zT, wts("rf"), ident, psum)

        with nc.Block() as block:
            @block.sync
            def _(sp):
                sp.dma_start(out.rearrange("b (t p) c -> p (b t) c", p=P), x[:]).then_inc(stored, 16)
                sp.wait_ge(stored, 16)
    return nc


def host_arrays(inp):
    arrays = {"x": np.asarray(inp["L0_attn_x"]), "ident": np.eye(P, dtype=np.float32)}
    modules = {"ga": grouped_weights(inp), "lo": local_weights(inp, "L0_ffn_", L0_FFN), "ca": chunk_weights(inp),
               "gf": swiglu_weights(inp), "ma": memory_weights(inp), "lt": local_weights(inp, "L2_ffn_", L2_FFN),
               "la": latent_weights(inp), "rf": routed_weights(inp)}
    for name, window in (("lo", 32), ("lt", 64)):
        modules[name]["rope"], modules[name]["mask"] = local_constants(window)
    for name, module in modules.items():
        arrays.update({f"{name}_{n}": a for n, a in module.items()})
    return {n: np.ascontiguousarray(a) for n, a in arrays.items()}


def kernel(**inputs):
    import concourse.bacc as _bacc
    from concourse.bass_utils import run_bass_kernel_spmd as _run

    nc = _bacc.Bacc("TRN2", target_bir_lowering=False, num_devices=1)
    arrays = {f"in_{n}_dram": a for n, a in host_arrays(inputs).items()}
    dram = {n[3:-5]: nc.dram_tensor(n, a.shape, mybir.dt.from_np(a.dtype), kind="ExternalInput").ap()
            for n, a in arrays.items()}
    out = nc.dram_tensor("out_0_dram", (SEQ, TOK, CH), F32, kind="ExternalOutput").ap()
    build_program(nc, dram, out)
    r = _run(nc, [arrays], core_ids=[0])
    return r.results[0]["out_0_dram"]
```
